# Optimizing a Trainium2 kernel written in Bass

```python
import numpy as np
import jax
import jax.numpy as jnp

def _softmax(x, axis=-1):
    return jax.nn.softmax(x, axis=axis)

def _gelu(x):
    return jax.nn.gelu(x, approximate=True)

def _silu(x):
    return jax.nn.silu(x)

def _sigmoid(x):
    return jax.nn.sigmoid(x)

def _layernorm(x, axis=-1, eps=1e-05):
    m = jnp.mean(x, axis=axis, keepdims=True)
    v = jnp.var(x, axis=axis, keepdims=True)
    return (x - m) / jnp.sqrt(v + eps)

def _scatter_add(tgt, idx, src, axis=0):
    return tgt.at[idx].add(src)

def _segment_sum(src, seg, n):
    return jax.ops.segment_sum(src, seg, n)
kernel_name = 'mk_adj_preln_d2_adj_r2_2aef1b'

def setup_inputs(seed: int=0):
    np.random.seed(seed)
    _w = jnp.asarray

    def _rec_inputs():
        import jax
        import jax.numpy as jnp
        _gk = jax.random.key(seed)
        x = 7.22e-05 + 1 * jax.random.normal(jax.random.fold_in(_gk, 1), (4096, 512), jnp.float32)
        _a = jax.random.bernoulli(jax.random.fold_in(_gk, 2), 0.00195312, (4096, 4096))
        _af = _a.astype(jnp.float32)
        adj = _af
        return (x, adj)
    x, adj = _rec_inputs()

    def _L0_gnn_setup():
        import jax, jax.numpy as jnp
        import numpy as np
        N = 4096
        D = 512
        key = jax.random.key(seed)
        ks = jax.random.split(key, 13)
        w_scale = 1.0 / np.sqrt(D)
        inp = {'query': jax.random.normal(ks[0], (N, D), dtype=jnp.float32), 'key': jax.random.normal(ks[1], (N, D), dtype=jnp.float32), 'value': jax.random.normal(ks[2], (N, D), dtype=jnp.float32), 'adj_matrix': jax.random.randint(ks[3], (N, N), 0, 2).astype(jnp.float32), 'Wq': jax.random.normal(ks[4], (D, D), dtype=jnp.float32) * w_scale, 'bq': jax.random.normal(ks[5], (D,), dtype=jnp.float32) * 0.01, 'Wk': jax.random.normal(ks[6], (D, D), dtype=jnp.float32) * w_scale, 'bk': jax.random.normal(ks[7], (D,), dtype=jnp.float32) * 0.01, 'Wv': jax.random.normal(ks[8], (D, D), dtype=jnp.float32) * w_scale, 'bv': jax.random.normal(ks[9], (D,), dtype=jnp.float32) * 0.01, 'Wm': jax.random.normal(ks[10], (D, D), dtype=jnp.float32) * w_scale, 'bm': jax.random.normal(ks[11], (D,), dtype=jnp.float32) * 0.01}
        return inp
    _L0_gnn_all = _L0_gnn_setup()
    _L0_gnn_in = {k: v for k, v in _L0_gnn_all.items() if k in ('key', 'value', 'Wq', 'bq', 'Wk', 'bk', 'Wv', 'bv', 'Wm', 'bm')}
    del _L0_gnn_all

    def _L1_gnn_setup():
        import jax, jax.numpy as jnp
        import numpy as np
        ALPHA = 0.2
        NEG = -9000000000000000.0
        N, NFEAT, NHID, NHEADS = (2048, 512, 64, 8)
        EMB = NHID * NHEADS
        key = jax.random.key(seed)
        ks = jax.random.split(key, 16)
        x = jax.random.normal(ks[0], (N, NFEAT), dtype=jnp.float32)
        adj = (jax.random.uniform(ks[1], (N, N)) < 0.01).astype(jnp.float32)
        adj = jnp.maximum(adj, jnp.eye(N, dtype=jnp.float32))
        s = 0.05
        W = jax.random.normal(ks[2], (NHEADS, NFEAT, NHID), dtype=jnp.float32) * s
        a1 = jax.random.normal(ks[3], (NHEADS, NHID), dtype=jnp.float32) * s
        a2 = jax.random.normal(ks[4], (NHEADS, NHID), dtype=jnp.float32) * s
        W1 = jax.random.normal(ks[5], (EMB // 2, EMB), dtype=jnp.float32) * s
        b1 = jnp.zeros((EMB // 2,), dtype=jnp.float32)
        W2 = jax.random.normal(ks[6], (NFEAT // 4, EMB // 2), dtype=jnp.float32) * s
        b2 = jnp.zeros((NFEAT // 4,), dtype=jnp.float32)
        W3 = jax.random.normal(ks[7], (NFEAT // 2, NFEAT // 4), dtype=jnp.float32) * s
        b3 = jnp.zeros((NFEAT // 2,), dtype=jnp.float32)
        W4 = jax.random.normal(ks[8], (NFEAT, NFEAT // 2), dtype=jnp.float32) * s
        b4 = jnp.zeros((NFEAT,), dtype=jnp.float32)
        return {'x': x, 'adj': adj, 'W': W, 'a1': a1, 'a2': a2, 'W1': W1, 'b1': b1, 'W2': W2, 'b2': b2, 'W3': W3, 'b3': b3, 'W4': W4, 'b4': b4}
    _L1_gnn_all = _L1_gnn_setup()
    _L1_gnn_in = {k: v for k, v in _L1_gnn_all.items() if k in ('W', 'a1', 'a2', 'W1', 'b1', 'W2', 'b2', 'W3', 'b3', 'W4', 'b4')}
    del _L1_gnn_all
    return {'x': x, 'adj': adj, 'L0_gnn_key': _L0_gnn_in['key'], 'L0_gnn_value': _L0_gnn_in['value'], 'L0_gnn_Wq': _L0_gnn_in['Wq'], 'L0_gnn_bq': _L0_gnn_in['bq'], 'L0_gnn_Wk': _L0_gnn_in['Wk'], 'L0_gnn_bk': _L0_gnn_in['bk'], 'L0_gnn_Wv': _L0_gnn_in['Wv'], 'L0_gnn_bv': _L0_gnn_in['bv'], 'L0_gnn_Wm': _L0_gnn_in['Wm'], 'L0_gnn_bm': _L0_gnn_in['bm'], 'L1_gnn_W': _L1_gnn_in['W'], 'L1_gnn_a1': _L1_gnn_in['a1'], 'L1_gnn_a2': _L1_gnn_in['a2'], 'L1_gnn_W1': _L1_gnn_in['W1'], 'L1_gnn_b1': _L1_gnn_in['b1'], 'L1_gnn_W2': _L1_gnn_in['W2'], 'L1_gnn_b2': _L1_gnn_in['b2'], 'L1_gnn_W3': _L1_gnn_in['W3'], 'L1_gnn_b3': _L1_gnn_in['b3'], 'L1_gnn_W4': _L1_gnn_in['W4'], 'L1_gnn_b4': _L1_gnn_in['b4']}

def reference(x, adj, L0_gnn_key, L0_gnn_value, L0_gnn_Wq, L0_gnn_bq, L0_gnn_Wk, L0_gnn_bk, L0_gnn_Wv, L0_gnn_bv, L0_gnn_Wm, L0_gnn_bm, L1_gnn_W, L1_gnn_a1, L1_gnn_a2, L1_gnn_W1, L1_gnn_b1, L1_gnn_W2, L1_gnn_b2, L1_gnn_W3, L1_gnn_b3, L1_gnn_W4, L1_gnn_b4):
    import jax
    import jax.numpy as jnp

    def _L0_gnn_ref(query, key, value, adj_matrix, Wq, bq, Wk, bk, Wv, bv, Wm, bm):
        import jax, jax.numpy as jnp
        import numpy as np
        N = 4096
        D = 512
        q = query @ Wq.T + bq
        k = key @ Wk.T + bk
        v = value @ Wv.T + bv
        scale = q.shape[0] ** 0.5
        scores = jnp.einsum('nd,md->nm', q, k) / scale
        adj_scores = scores * adj_matrix
        adj_scores = jnp.where(jnp.abs(adj_scores) < 1e-05, -1000000000.0, adj_scores)
        prob = jax.nn.softmax(adj_scores, axis=-1)
        x = jnp.einsum('nm,md->nd', prob, v)
        return x @ Wm.T + bm

    def _L1_gnn_ref(x, adj, W, a1, a2, W1, b1, W2, b2, W3, b3, W4, b4):
        import jax, jax.numpy as jnp
        import numpy as np
        ALPHA = 0.2
        NEG = -9000000000000000.0
        N, NFEAT, NHID, NHEADS = (2048, 512, 64, 8)
        EMB = NHID * NHEADS
        Wh = jnp.einsum('nf,hfd->hnd', x, W)
        e_src = jnp.einsum('hnd,hd->hn', Wh, a1)
        e_dst = jnp.einsum('hnd,hd->hn', Wh, a2)
        e = jax.nn.leaky_relu(e_src[:, :, None] + e_dst[:, None, :], ALPHA)
        e = jnp.where(adj[None] > 0, e, NEG)
        att = jax.nn.softmax(e, axis=-1)
        h = jnp.einsum('hnm,hmd->hnd', att, Wh)
        h = jax.nn.elu(h)
        enc = jnp.transpose(h, (1, 0, 2)).reshape(x.shape[0], -1)
        out = jax.nn.relu(enc @ W1.T + b1)
        out = jax.nn.relu(out @ W2.T + b2)
        out = jax.nn.relu(out @ W3.T + b3)
        out = out @ W4.T + b4
        return out
    h = jnp.maximum(_layernorm(x, axis=-1), 0.0)
    x = x + _L0_gnn_ref(h, L0_gnn_key, L0_gnn_value, adj, L0_gnn_Wq, L0_gnn_bq, L0_gnn_Wk, L0_gnn_bk, L0_gnn_Wv, L0_gnn_bv, L0_gnn_Wm, L0_gnn_bm)
    h = jnp.maximum(_layernorm(x, axis=-1), 0.0)
    x = x + _L1_gnn_ref(h, adj, L1_gnn_W, L1_gnn_a1, L1_gnn_a2, L1_gnn_W1, L1_gnn_b1, L1_gnn_W2, L1_gnn_b2, L1_gnn_W3, L1_gnn_b3, L1_gnn_W4, L1_gnn_b4)
    return x

_drawn_inputs = setup_inputs


def setup_inputs(seed=0):
    import zlib

    import numpy as np

    out = dict(_drawn_inputs(seed))
    spreads = {'L1_gnn_b1': (0.0, 0.667),
     'L1_gnn_b2': (0.0, 0.352),
     'L1_gnn_b3': (0.0, 0.1),
     'L1_gnn_b4': (0.0, 0.1)}
    factors = {'L0_gnn_bq': 51.449,
     'L0_gnn_bk': 64.0,
     'L0_gnn_bv': 6.372,
     'L0_gnn_bm': 5.959,
     'L1_gnn_a1': 56.748,
     'L1_gnn_a2': 8.0}
    for name, (base, spread) in spreads.items():
        noise = np.random.default_rng([zlib.crc32(name.encode()), seed]).standard_normal(out[name].shape)
        drawn = base * np.exp(spread * noise) if base else spread * noise
        out[name] = jnp.asarray(drawn.astype(out[name].dtype))
    for name, factor in factors.items():
        out[name] = (out[name] * factor).astype(out[name].dtype)
    return out
```

```python
from contextlib import ExitStack

import concourse.bass as bass
from concourse import mybir

F32 = mybir.dt.float32
F16 = mybir.dt.float16
BF16 = mybir.dt.bfloat16
ALU = mybir.AluOpType
ACT = mybir.ActivationFunctionType
AX = mybir.AxisListType.X
RMAX = bass.bass_isa.ReduceOp.max

P = 128
EPS = 1e-5


class Semaphores:

    def __init__(self, nc, ctx):
        self.nc, self.ctx = nc, ctx
        self.act, self.pool, self.pe, self.dve, self.sp = (self.new(f"{n}_carrier") for n in ("act", "pool", "pe", "dve", "sp"))

    def new(self, name):
        return self.ctx.enter_context(self.nc.semaphore(name))


def wait_alone(eng, sem, value, carrier):
    eng.wait_ge(sem, value)
    eng.sem_inc(carrier, 1)


def row_norm(nc, dve, x, stats, sums, scale, tile, carrier, stats_done, sums_done, rstd_done, norm_done):
    nc.vector.bn_stats(stats[:], x).then_inc(stats_done, 1)
    wait_alone(dve, stats_done, tile + 1, carrier)
    nc.vector.bn_aggr(sums[:, 0:2], stats[:]).then_inc(sums_done, 1)
    dve.wait_ge(sums_done, tile * 2 + 1)
    nc.vector.tensor_scalar(sums[:, 2:3], sums[:, 1:2], EPS, None, ALU.add).then_inc(sums_done, 1)
    dve.wait_ge(rstd_done, tile + 1)
    nc.vector.scalar_tensor_tensor(out=scale[:, 1:2], in0=sums[:, 0:1], scalar=-1.0, in1=scale[:, 0:1],
                                   op0=ALU.mult, op1=ALU.mult).then_inc(norm_done, 1)


def row_rstd(nc, pool, sums, scale, tile, sums_done, h_done, rstd_done):
    pool.wait_ge(h_done, 1 + tile)
    pool.wait_ge(sums_done, tile * 2 + 2)
    nc.gpsimd.tensor_tensor(scale[:, 0:1], sums[:, 2:3], sums[:, 3:4], ALU.pow).then_inc(rstd_done, 1)


def row_relu_norm(nc, act, x, scale, tile, norm_done, h_done):
    act.wait_ge(norm_done, tile + 1)
    nc.scalar.activation(x, x, ACT.Relu, scale=scale[:, 0:1], bias=scale[:, 1:2]).then_inc(h_done, 1)


def weight_products(nc, sems, d, keep, psum):
    T = 4
    with ExitStack() as ctx:
        def sb(name, shape, dt=F32):
            return ctx.enter_context(nc.sbuf_tensor(name, shape, dt))

        def sem(name):
            return sems.new((name))

        wk, wq, wv, wm = (sb(f"{n}_raw", [P, T, 512]) for n in ("wk", "wq", "wv", "wm"))
        bq, bk, bv = (sb(f"{n}_col", [P, T]) for n in ("bq", "bk", "bv"))
        bm = sb("bm_row", [P, 512])
        loaded_qk, loaded_vm = sem("loaded_qk"), sem("loaded_vm")
        product_done, product_copied = sem("product_done"), sem("product_copied")
        block = ctx.enter_context(nc.Block())

        @block.sync
        def _(sp):
            for dst, src in ((wk, d["L0_gnn_Wk"]), (wq, d["L0_gnn_Wq"])):
                sp.dma_start(dst[:], src.rearrange("(t p) n -> p t n", p=P)).then_inc(loaded_qk, 16)
            for dst, src in ((wv, d["L0_gnn_Wv"]), (wm, d["WmT"])):
                sp.dma_start(dst[:], src.rearrange("(t p) n -> p t n", p=P)).then_inc(loaded_vm, 16)
            for dst, src in ((bq, d["bq_cols"]), (bk, d["bk_cols"]), (bv, d["bv_cols"])):
                sp.dma_start(dst[:], src).then_inc(loaded_vm, 16)
            sp.dma_start(bm[:], d["bm_rows"]).then_inc(loaded_vm, 16)

        @block.tensor
        def _(pe):
            pe.wait_ge(loaded_qk, 32)
            for a, b, bank in ((wk, wq, 0), (wv, wm, 4)):
                if bank:
                    pe.wait_ge(loaded_vm, 96)
                for e in range(T):
                    for o in range(T):
                        last = nc.tensor.matmul(psum[:, bank + e, :], a[:, o, e * P:(e + 1) * P], b[:, o, :],
                                                start=(o == 0), stop=(o == T - 1))
                    last.then_inc(product_done, 1)
            pe.wait_ge(product_copied, 2)
            for w, bias, col in ((wq, bk, 0), (wk, bq, T)):
                for e in range(T):
                    for o in range(T):
                        last = nc.tensor.matmul(psum[:, 0, col + e:col + e + 1], w[:, o, e * P:(e + 1) * P],
                                                bias[:, o:o + 1], start=(o == 0), stop=(o == T - 1))
            for o in range(T):
                last = nc.tensor.matmul(psum[:, 0, 2 * T:2 * T + 1], bk[:, o:o + 1].broadcast_to([P, P]),
                                        bq[:, o:o + 1], start=(o == 0), stop=(o == T - 1))
            last.then_inc(product_done, 1)
            for o in range(T):
                last = nc.tensor.matmul(psum[:, 1, :], bv[:, o:o + 1].broadcast_to([P, P]), wm[:, o, :],
                                        start=(o == 0), stop=(o == T - 1))
            last.then_inc(product_done, 1)

        @block.vector
        def _(dve):
            for n, dst in enumerate([keep["wqk"][:, e, :] for e in range(T)] + [keep["wvm"][:, e, :] for e in range(T)]):
                dve.wait_ge(product_done, n + 1)
                nc.vector.tensor_copy(dst, psum[:, n, :]).then_inc(product_copied, 1)
            dve.wait_ge(product_done, 2 * T + 1)
            nc.vector.tensor_copy(keep["bias_cols"][:], psum[:, 0, 0:2 * T + 1]).then_inc(product_copied, 1)
            dve.wait_ge(product_done, 2 * T + 2)
            nc.vector.tensor_tensor(keep["bvm"][:], psum[:, 1, :], bm[:], ALU.add).then_inc(product_copied, 1)


def keys_and_values(nc, sems, d, keep, psum, g, v, c_all, ht_dram):
    T, B = 4, 8
    wqk, wvm, gk = keep["wqk"], keep["wvm"], keep["bias_cols"]
    with ExitStack() as ctx:
        def sb(name, shape, dt=F32):
            return ctx.enter_context(nc.sbuf_tensor(name, shape, dt))

        def sem(name):
            return sems.new((name))

        key_t = sb("key_t", [P, 2, T, 512])
        value_t = sb("value_t", [P, 2, T, 512])
        v_sum = sb("v_sum", [P, 2, 512])
        x_tile = sb("x_tile0", [P, 2, 512])
        h_stage = sb("h_stage", [P, 2, 2, T, 256], F16)
        stats, sums, scale = sb("stats0", [P, 6]), sb("sums0", [P, 4]), sb("scale0", [P, 2])
        ident = sb("ident0", [P, P])
        key_in, value_in, x_in, stage_stored = ([sem(f"{n}{i}") for i in range(2)] for n in ("key_in", "value_in", "x_in", "stage_stored"))
        ident_in, exponent_in = sem("ident_in0"), sem("exponent_in0")
        tile_done, bank_free = sem("tile_done"), sem("bank_free")
        c_done, c_free = sem("c_done"), sem("c_free")
        g_high_done, v_high_done, v_sum_free = (sem(n) for n in ("g_high", "v_high", "v_sum_free"))
        stats_done, sums_done, rstd_done, norm_done, h_done = (sem(n) for n in ( "stats_s0", "sums_s0", "rstd0", "norm0", "h0"))
        turned, high_done, low_done = (sem(n) for n in ("turned0", "high0", "low0"))
        block = ctx.enter_context(nc.Block())

        kv = d["keyT"].rearrange("(t p) m -> p t m", p=P)
        vv = d["valueT"].rearrange("(t p) m -> p t m", p=P)
        xv = d["x"].rearrange("(n p) k -> n p k", p=P)

        @block.sync
        def _(sp):
            def load_block(m, half):
                sp.dma_start(key_t[:, half], kv[:, :, bass.ds(m * 512, 512)]).then_inc(key_in[half], 16)
                sp.dma_start(value_t[:, half], vv[:, :, bass.ds(m * 512, 512)]).then_inc(value_in[half], 16)

            def next_x(m, n):
                sp.wait_ge(turned, m * 4 + n + 1)
                sp.dma_start(x_tile[:, n % 2], xv[m * 4 + n + 2]).then_inc(x_in[n % 2], 16)

            def store_h(m, pair):
                wait_alone(sp, low_done, 2 + m * 4 + pair * 2 + 2, sems.sp)
                sp.dma_start(ht_dram[m * 2 + pair], h_stage[:, pair].rearrange("p a t i -> p (a t i)")).then_inc(stage_stored[pair], 16)

            for pair in range(2):
                sp.sem_inc(stage_stored[pair], 16)
            sp.dma_start(ident[:], d["ident"]).then_inc(ident_in, 16)
            for half in range(2):
                sp.dma_start(x_tile[:, half], xv[half]).then_inc(x_in[half], 16)
                load_block(half, half)
            with sp.Fori(0, B // 2 - 1) as it:
                for half in range(2):
                    for n in range(4):
                        next_x(it * 2 + half, n)
                        if n % 2:
                            store_h(it * 2 + half, n // 2)
                    load_block(it * 2 + half + 2, half)
            for n in range(4):
                next_x(B - 2, n)
                if n % 2:
                    store_h(B - 2, n // 2)
            for n in range(2):
                next_x(B - 1, n)
            for pair in range(2):
                store_h(B - 1, pair)
                sp.wait_ge(stage_stored[pair], 16 + 16 * B)

        @block.tensor
        def _(pe):
            pe.wait_ge(ident_in, 16)
            with pe.Fori(0, B // 2) as it:
                for half in range(2):
                    m = it * 2 + half
                    pe.wait_ge(key_in[half], it * 16 + 16)
                    pe.wait_ge(value_in[half], it * 16 + 16)
                    for q in range(2 * T):
                        n = q % T
                        pe.wait_ge(bank_free, m * 8 + q + 1)
                        for e in range(T):
                            if q < T:
                                a, b = wqk[:, e, n * P:(n + 1) * P], key_t[:, half, e, :]
                            else:
                                a, b = value_t[:, half, e, n * P:(n + 1) * P], wvm[:, e, :]
                            last = nc.tensor.matmul(psum[:, n, :], a, b, start=(e == 0), stop=(e == T - 1))
                        last.then_inc(tile_done, 1)
                        if q == T - 1:
                            pe.wait_ge(c_free, m + 1)
                            for s in range(T):
                                for e in range(T):
                                    last = nc.tensor.matmul(psum[:, 4 + half, s:s + 1], key_t[:, half, e, s * P:(s + 1) * P],
                                                            gk[:, T + e:T + e + 1], start=(e == 0), stop=(e == T - 1))
                            last.then_inc(c_done, 1)
                        if q % 2:
                            n = q // 2
                            pe.wait_ge(h_done, 1 + m * 4 + n + 1)
                            pe.wait_ge(low_done, m * 4 + n + 1)
                            for t in range(T):
                                last = nc.tensor.transpose(psum[:, 6 + n % 2, t * P:(t + 1) * P],
                                                           x_tile[:, n % 2, t * P:(t + 1) * P], ident[:])
                            last.then_inc(turned, 1)

        @block.scalar
        def _(act):
            act.sem_inc(h_done, 1)
            with act.Fori(0, B // 2) as it:
                for half in range(2):
                    m = it * 2 + half
                    for n in range(4):
                        row_relu_norm(nc, act, x_tile[:, n % 2], scale, m * 4 + n, norm_done, h_done)
                        for q in (2 * n, 2 * n + 1):
                            if q < T:
                                wait_alone(act, tile_done, m * 8 + q + 1, sems.act)
                                nc.scalar.activation(g[:, 0, q, bass.ds(m * 512, 512)], psum[:, q, :], ACT.Identity,
                                                     bias=gk[:, q:q + 1]).then_inc(g_high_done, 1)
                            else:
                                wait_alone(act, bank_free, T + m * 8 + q + 1, sems.act)
                                nc.scalar.copy(v[:, 0, m * 4 + q - T, :], v_sum[:, q % 2]).then_inc(v_high_done, 1)
                        act.wait_ge(turned, m * 4 + n + 1)
                        if n % 2 == 0:
                            act.wait_ge(stage_stored[n // 2], m * 16 + 16)
                        nc.scalar.copy(h_stage[:, n // 2, 0, :, (n % 2) * P:(n % 2 + 1) * P],
                                       psum[:, 6 + n % 2, :].rearrange("p (t i) -> p t i", t=T)).then_inc(high_done, 1)

        @block.vector
        def _(dve):
            dve.sem_inc(bank_free, T)
            dve.sem_inc(c_free, 2)
            dve.sem_inc(low_done, 2)
            with dve.Fori(0, B // 2) as it:
                for half in range(2):
                    m = it * 2 + half
                    for n in range(4):
                        dve.wait_ge(x_in[n % 2], (m * 2 + n // 2) * 16 + 16)
                        row_norm(nc, dve, x_tile[:, n % 2], stats, sums, scale, m * 4 + n, sems.dve, stats_done, sums_done, rstd_done, norm_done)
                        for q in (2 * n, 2 * n + 1):
                            if q < T:
                                dve.wait_ge(g_high_done, m * 4 + q + 1)
                                cols = bass.ds(m * 512, 512)
                                nc.vector.scalar_tensor_tensor(out=g[:, 1, q, cols], in0=psum[:, q, :], scalar=gk[:, q:q + 1],
                                                               in1=g[:, 0, q, cols], op0=ALU.add, op1=ALU.subtract
                                                               ).then_inc(bank_free, 1)
                            else:
                                dve.wait_ge(tile_done, m * 8 + q + 1)
                                dve.wait_ge(v_sum_free, m * 4 + q - T + 1)
                                nc.vector.tensor_tensor(v_sum[:, q % 2], psum[:, q - T, :], keep["bvm"][:],
                                                        ALU.add).then_inc(bank_free, 1)
                            if q == T:
                                dve.wait_ge(c_done, m + 1)
                                nc.vector.tensor_scalar(c_all[:, bass.ds(m * 4, 4)], psum[:, 4 + half, 0:T],
                                                        gk[:, 2 * T:2 * T + 1], None, ALU.add).then_inc(c_free, 1)
                        dve.wait_ge(high_done, m * 4 + n + 1)
                        nc.vector.tensor_tensor(h_stage[:, n // 2, 1, :, (n % 2) * P:(n % 2 + 1) * P],
                                                psum[:, 6 + n % 2, :].rearrange("p (t i) -> p t i", t=T),
                                                h_stage[:, n // 2, 0, :, (n % 2) * P:(n % 2 + 1) * P],
                                                ALU.subtract).then_inc(low_done, 1)

        @block.gpsimd
        def _(pool):
            nc.gpsimd.memset(sums[:, 3:4], -0.5).then_inc(exponent_in, 1)
            pool.wait_ge(exponent_in, 1)
            pool.sem_inc(v_sum_free, 2)
            with pool.Fori(0, B // 2) as it:
                for half in range(2):
                    m = it * 2 + half
                    for n in range(4):
                        row_rstd(nc, pool, sums, scale, m * 4 + n, sums_done, h_done, rstd_done)
                        if n >= 2:
                            for q in (2 * n - T, 2 * n - T + 1):
                                pool.wait_ge(v_high_done, m * 4 + q + 1)
                                nc.gpsimd.tensor_tensor(v[:, 1, m * 4 + q, :], v_sum[:, q % 2], v[:, 0, m * 4 + q, :],
                                                        ALU.subtract).then_inc(v_sum_free, 1)


NODES = 4096
QB = 256
MASKED = -1e9


def attention(nc, sems, d, psum, g, v, c_all, ht_dram, x1_dram):
    T, JP, BLOCKS = 4, 16, NODES // QB
    SCALE, MARK = 64.0, 2.0 ** 80
    with ExitStack() as ctx:
        def sb(name, shape, dt=F32):
            return ctx.enter_context(nc.sbuf_tensor(name, shape, dt))

        def sem(name):
            return sems.new((name))

        strip = sb("strip", [P, 2 * JP, QB])
        prob = sb("prob", [P, 2, 2 * JP, QB], F16)
        h_t = sb("h_t", [P, 2, T, QB], F16)
        adj = sb("adj", [P, 2, 2, QB])
        least = sb("least", [P, 2, QB])
        weight = sb("weight", [P, 2, QB])
        mark = sb("mark", [P, 2, QB], BF16)
        bound = sb("bound", [P, 1])
        res = sb("res", [P, 512])
        ones = sb("ones", [P, 1], F16)
        total, inv = sb("total", [P, 2]), sb("inv", [P, 2])
        h_in, res_in, ones_in, stored = (sem(n) for n in ("h_in", "res_in", "ones_in", "stored1"))
        adj_in = [sem(f"adj_in{i}") for i in range(2)]
        scored, score_free = sem("scored"), sem("score_free")
        abs_done, mark_done, pair_done, least_done, least_clear, bound_in = (sem(n) for n in ("abs_s", "mark_s", "pair_s", "least_s", "least_clear", "bound_in"))
        halves_done, top_row, shifted, high_done, weight_done, low_done = (sem(n) for n in ("halves", "top_row", "shifted", "high1", "weight_s", "low1"))
        prob_used, total_done, inv_done, res_done = (sem(n) for n in ("prob_used", "total_done", "inv_done", "res_done"))
        block = ctx.enter_context(nc.Block())
        adj_v = d["adjT"].rearrange("(k a p) i -> k p a i", p=P, a=2)
        xv = d["x"].rearrange("(n p) k -> n p k", p=P)
        x1v = x1_dram.rearrange("(n p) k -> n p k", p=P)


        @block.sync
        def _(sp):
            def load_adj(b, k, par):
                sp.wait_ge(score_free, (b * JP + k) + 1)
                sp.dma_start(adj[:, par], adj_v[k, :, :, bass.ds(b * QB, QB)]).then_inc(adj_in[par], 16)

            def load_block(b):
                with sp.Fori(0, JP // 2) as kk:
                    for par in range(2):
                        load_adj(b, kk * 2 + par, par)

            sp.dma_start(h_t[:].rearrange("p a t i -> p (a t i)"), ht_dram[0]).then_inc(h_in, 16)
            load_block(0)
            with sp.Fori(1, BLOCKS) as b:
                sp.wait_ge(scored, b * JP)
                sp.dma_start(h_t[:].rearrange("p a t i -> p (a t i)"), ht_dram[b]).then_inc(h_in, 16)
                load_block(b)

        @block.tensor
        def _(pe):
            def scores(b):
                wait_alone(pe, h_in, b * 16 + 16, sems.pe)
                with pe.Fori(0, JP // 2) as kk:
                    for par in range(2):
                        pe.wait_ge(score_free, (b * JP + kk * 2 + par) + 1)
                        for a in range(2):
                            jt = kk * 4 + par * 2 + a
                            first = True
                            for t in range(T):
                                key = [g[:, hl, t, bass.ds(jt * P, P)] for hl in range(2)]
                                for kh, hh in ((0, 0), (0, 1), (1, 0)):
                                    last = nc.tensor.matmul(psum[:, par, a * QB:(a + 1) * QB], key[kh], h_t[:, hh, t, :],
                                                            start=first, stop=(t == T - 1 and kh == 1))
                                    first = False
                        last.then_inc(scored, 1)

            def outputs(b):
                pe.wait_ge(res_done, 1 + b * 2)

                def key_tile(jt, start, stop):
                    for s in range(2):
                        high = prob[:, 0, jt, s * P:(s + 1) * P]
                        low = prob[:, 1, jt, s * P:(s + 1) * P]
                        nc.tensor.matmul(psum[:, 2 + s, :], high, v[:, 0, jt, :], start=start, stop=False)
                        nc.tensor.matmul(psum[:, 2 + s, :], high, v[:, 1, jt, :], start=False, stop=False)
                        nc.tensor.matmul(psum[:, 4 + s, 0:1], high, ones[:], start=start, stop=False)
                        nc.tensor.matmul(psum[:, 2 + s, :], low, v[:, 0, jt, :], start=False, stop=stop)
                        last = nc.tensor.matmul(psum[:, 4 + s, 0:1], low, ones[:], start=False, stop=stop)
                    return last

                pe.wait_ge(low_done, 1 + b * JP + 1)
                key_tile(0, True, False)
                key_tile(1, False, False).then_inc(prob_used, 1)
                with pe.Fori(1, JP - 1) as k:
                    pe.wait_ge(low_done, 1 + b * JP + k + 1)
                    key_tile(k * 2, False, False)
                    key_tile(k * 2 + 1, False, False).then_inc(prob_used, 1)
                pe.wait_ge(low_done, 1 + b * JP + JP)
                key_tile(2 * JP - 2, False, False)
                key_tile(2 * JP - 1, False, True).then_inc(prob_used, 1)

            pe.wait_ge(ones_in, 1)
            scores(0)
            with pe.Fori(1, BLOCKS) as b:
                scores(b)
                outputs(b - 1)
            outputs(BLOCKS - 1)

        @block.vector
        def _(dve):
            dve.sem_inc(score_free, 2)
            for done in (pair_done, low_done, res_done):
                dve.sem_inc(done, 1)
            nc.vector.memset(bound[:], MARK * SCALE * 1e-5).then_inc(bound_in, 1)
            nc.vector.memset(ones[:], 1.0).then_inc(ones_in, 1)

            def product(b, k, par, kk=0):
                n = b * JP + k
                dve.wait_ge(scored, n + 1)
                dve.wait_ge(adj_in[par], (b * (JP // 2) + kk) * 16 + 16)
                for a in range(2):
                    ins = nc.vector.scalar_tensor_tensor(
                        out=strip[:, k * 2 + a, :], in0=psum[:, par, a * QB:(a + 1) * QB],
                        scalar=c_all[:, bass.ds(k * 2 + a, 1)], in1=adj[:, par, a, :], op0=ALU.add, op1=ALU.mult)
                ins.then_inc(score_free, 1)

            def negate(b, k):
                n = b * JP + k
                t = strip[:, bass.ds(k * 2, 2), :]
                dve.wait_ge(mark_done, 1 + n + 1)
                nc.vector.scalar_tensor_tensor(out=t, in0=mark[:], scalar=-MASKED * SCALE, in1=t,
                                               op0=ALU.min, op1=ALU.subtract).then_inc(pair_done, 1)
                dve.wait_ge(pair_done, 1 + n + 1)
                nc.vector.tensor_tensor(least[:], least[:], t, ALU.min).then_inc(least_done, 1)

            def mask_scores(b):
                nc.vector.memset(least[:], 3.0e38).then_inc(least_clear, 1)
                wait_alone(dve, least_clear, b + 1, sems.dve)
                product(b, 0, 0)
                with dve.Fori(0, JP // 2 - 1) as kk:
                    product(b, kk * 2 + 1, 1, kk)
                    negate(b, kk * 2)
                    product(b, kk * 2 + 2, 0, kk + 1)
                    negate(b, kk * 2 + 1)
                product(b, JP - 1, 1, JP // 2 - 1)
                negate(b, JP - 2)
                negate(b, JP - 1)
                dve.wait_ge(least_done, b * JP + JP)
                nc.vector.scalar_tensor_tensor(out=least[:, 0, :], in0=least[:, 0, :], scalar=1.0, in1=least[:, 1, :],
                                               op0=ALU.mult, op1=ALU.min).then_inc(halves_done, 1)
                dve.wait_ge(halves_done, b * 2 + 1)
                nc.vector.tensor_scalar(least[:, 0, :], least[:, 0, :], -1.0, None, ALU.mult).then_inc(halves_done, 1)

            def probabilities(b):
                wait_alone(dve, top_row, b + 1, sems.dve)
                with dve.Fori(0, JP) as k:
                    n = b * JP + k
                    t = strip[:, bass.ds(k * 2, 2), :]
                    nc.vector.tensor_tensor(t, t, least[:, 1:2, :].broadcast_to([P, 2, QB]), ALU.add).then_inc(shifted, 1)
                    dve.wait_ge(weight_done, n + 1)
                    nc.vector.tensor_tensor(prob[:, 1, bass.ds(k * 2, 2), :], weight[:], prob[:, 0, bass.ds(k * 2, 2), :],
                                            ALU.subtract).then_inc(low_done, 1)

            def finish(b):
                for s in range(2):
                    n = b * 2 + s
                    if s == 0:
                        dve.wait_ge(prob_used, b * JP + JP)
                        for i in range(2):
                            ins = nc.vector.tensor_copy(total[:, i:i + 1], psum[:, 4 + i, 0:1])
                        ins.then_inc(total_done, 1)
                        dve.wait_ge(total_done, b + 1)
                        nc.vector.reciprocal(inv[:], total[:]).then_inc(inv_done, 1)
                        dve.wait_ge(inv_done, b + 1)
                    dve.wait_ge(res_in, n * 16 + 16)
                    nc.vector.scalar_tensor_tensor(out=res[:], in0=psum[:, 2 + s, :], scalar=inv[:, s:s + 1], in1=res[:],
                                                         op0=ALU.mult, op1=ALU.add).then_inc(res_done, 1)

            mask_scores(0)
            probabilities(0)
            with dve.Fori(1, BLOCKS) as b:
                mask_scores(b)
                probabilities(b)
                finish(b - 1)
            finish(BLOCKS - 1)

        @block.scalar
        def _(act):
            def marks(b):
                with act.Fori(0, JP) as k:
                    n = b * JP + k
                    act.wait_ge(mark_done, 1 + n)
                    wait_alone(act, score_free, 2 + n + 1, sems.act)
                    nc.scalar.activation(weight[:], strip[:, bass.ds(k * 2, 2), :], ACT.Abs).then_inc(abs_done, 1)
                    act.wait_ge(abs_done, n + 1)
                    act.wait_ge(pair_done, 1 + n)
                    nc.scalar.activation(mark[:], weight[:], ACT.Relu, scale=-MARK, bias=bound[:, 0:1]).then_inc(mark_done, 1)

            def exps(b):
                with act.Fori(0, JP) as k:
                    n = b * JP + k
                    t = strip[:, bass.ds(k * 2, 2), :]
                    wait_alone(act, shifted, n + 1, sems.act)
                    if b is not FIRST:
                        wait_alone(act, prob_used, (b - 1) * JP + k + 1, sems.act)
                    nc.scalar.activation(prob[:, 0, bass.ds(k * 2, 2), :], t, ACT.Exp, scale=-1.0 / SCALE).then_inc(high_done, 1)
                    wait_alone(act, low_done, 1 + n, sems.act)
                    nc.scalar.activation(weight[:], t, ACT.Exp, scale=-1.0 / SCALE).then_inc(weight_done, 1)

            FIRST = 0
            act.sem_inc(mark_done, 1)
            act.wait_ge(bound_in, 1)
            marks(FIRST)
            exps(FIRST)
            with act.Fori(1, BLOCKS) as b:
                marks(b)
                exps(b)

        @block.gpsimd
        def _(pool):
            def top_of(b):
                wait_alone(pool, halves_done, b * 2 + 2, sems.pool)
                nc.gpsimd.partition_all_reduce(least[:, 1, :], least[:, 0, :], P, RMAX).then_inc(top_row, 1)

            def move_rows(b):
                for s in range(2):
                    n = b * 2 + s
                    pool.dma_start(res[:], xv[n]).then_inc(res_in, 16)
                    wait_alone(pool, res_done, 1 + n + 1, sems.pool)
                    pool.dma_start(x1v[n], res[:]).then_inc(stored, 16)
                    wait_alone(pool, stored, n * 16 + 16, sems.pool)

            top_of(0)
            with pool.Fori(1, BLOCKS) as b:
                top_of(b)
                move_rows(b - 1)
            move_rows(BLOCKS - 1)


HEADS, HD = 8, 64
SLOPE = 0.2
GATE = 2.0 ** 60
UP = 64.0


def head_features(nc, sems, d, psum, x1_dram, wh_dram, srow_dram, node):
    T, TILES = 4, NODES // P
    WIDE = 512 + 2 * HEADS
    with ExitStack() as ctx:
        def sb(name, shape, dt=F32):
            return ctx.enter_context(nc.sbuf_tensor(name, shape, dt))

        def sem(name):
            return sems.new((name))

        w_all = sb("w_all", [P, T, WIDE])
        w_half = sb("w_half", [P, 2, T, WIDE], F16)
        a_rows = sb("a_rows", [P, 2, 512])
        w_a = sb("w_a", [P, 512])
        ident = sb("ident2", [P, P])
        x_tile = sb("x_tile2", [P, 2, 512])
        h_t = sb("h_t2", [P, 2, 2, T, 512], F16)
        wh_tile = sb("wh_tile", [P, 2, 512])
        wh_sum = sb("wh_sum", [P, 512])
        mean_w = sb("mean_w", [P, P])
        s_row = sb("s_row2", [HEADS, NODES])
        sd = sb("sd", [P, TILES, 2 * HEADS])
        stats, sums, scale = sb("stats2", [P, 6]), sb("sums2", [P, 4]), sb("scale2", [P, 2])
        d_top, z = sb("d_top", [P, 2, HEADS]), sb("z", [P, 4, TILES, HEADS])
        x_in = [sem(f"x_in2{i}") for i in range(2)]
        wh_stored = [sem(f"wh_stored{i}") for i in range(2)]
        weights_in, ready, exponent_in, zeroed = sem("weights_in2"), sem("ready2"), sem("exponent_in2"), sem("zeroed2")
        wa_step, halves_done = sem("wa_step"), sem("halves2")
        stats_done, sums_done, rstd_done, norm_done, h_done = (sem(n) for n in ("stats_s2", "sums_s2", "rstd2", "norm2", "h2"))
        turned, high_done, low_done = (sem(n) for n in ("turned2", "high2", "low2"))
        feature_done, wh_copied, sd_copied, added = (sem(n) for n in ("feature_done", "wh_copied", "sd_copied", "added"))
        rows_done, rows_copied, rows_stored, mean_done, mean_copied = (sem(n) for n in ("rows_done", "rows_copied", "rows_stored", "mean_done", "mean_copied"))
        factor_step, exp_ready, exp_done = sem("factor_step"), sem("exp_ready"), sem("exp_done")
        block = ctx.enter_context(nc.Block())
        xv = x1_dram.rearrange("(n p) k -> n p k", p=P)
        whv = wh_dram.rearrange("(n p) k -> n p k", p=P)

        @block.sync
        def _(sp):
            sp.dma_start(w_all[:, :, 0:512], d["W_heads"].rearrange("(t p) n -> p t n", p=P)).then_inc(weights_in, 16)
            sp.dma_start(a_rows[:, 0], d["a1_rows"]).then_inc(weights_in, 16)
            sp.dma_start(a_rows[:, 1], d["a2_rows"]).then_inc(weights_in, 16)
            sp.dma_start(ident[:], d["ident"]).then_inc(weights_in, 16)
            for n in range(2):
                sp.dma_start(x_tile[:, n], xv[n]).then_inc(x_in[n], 16)
            with sp.Fori(0, TILES // 2 - 1) as it:
                for par in range(2):
                    n = it * 2 + par
                    sp.wait_ge(turned, n + 1)
                    sp.dma_start(x_tile[:, par], xv[n + 2]).then_inc(x_in[par], 16)
            sp.wait_ge(rows_copied, TILES // T)
            sp.dma_start(srow_dram, s_row[:]).then_inc(rows_stored, 16)
            sp.wait_ge(rows_stored, 16)

        @block.gpsimd
        def _(pool):
            nc.gpsimd.memset(sums[:, 3:4], -0.5).then_inc(exponent_in, 1)
            nc.gpsimd.memset(wh_sum[:], 0.0).then_inc(zeroed, 1)
            pool.sem_inc(added, 1)
            pool.wait_ge(zeroed, 1)
            pool.wait_ge(exponent_in, 1)

            def store(n, par):
                wait_alone(pool, wh_copied, n + 1, sems.pool)
                pool.dma_start(whv[n], wh_tile[:, par]).then_inc(wh_stored[par], 16)
                pool.wait_ge(added, 1 + n)
                nc.gpsimd.tensor_tensor(wh_sum[:], wh_sum[:], wh_tile[:, par], ALU.add).then_inc(added, 1)

            for n in range(2):
                row_rstd(nc, pool, sums, scale, n, sums_done, h_done, rstd_done)
            with pool.Fori(0, TILES // 2 - 1) as it:
                for par in range(2):
                    row_rstd(nc, pool, sums, scale, it * 2 + par + 2, sums_done, h_done, rstd_done)
                    store(it * 2 + par, par)
            for n in range(TILES - 2, TILES):
                store(n, n % 2)
            for par in range(2):
                pool.wait_ge(wh_stored[par], 16 * (TILES // 2))
            pool.wait_ge(factor_step, 1)
            nc.gpsimd.partition_all_reduce(d_top[:, 1], d_top[:, 0], P, RMAX).then_inc(factor_step, 1)

        @block.tensor
        def _(pe):
            pe.wait_ge(weights_in, 64)
            pe.wait_ge(halves_done, 4)

            def turn(q, par):
                pe.wait_ge(h_done, 1 + q + 1)
                pe.wait_ge(low_done, q + 1)
                for t in range(T):
                    last = nc.tensor.transpose(psum[:, 6 + par, t * P:(t + 1) * P], x_tile[:, par, t * P:(t + 1) * P], ident[:])
                last.then_inc(turned, 1)

            def products(out, stationary, moving):
                for t in range(T):
                    for a, b in ((0, 0), (0, 1), (1, 0)):
                        last = nc.tensor.matmul(out, stationary(a, t), moving(b, t), start=(t == 0 and a + b == 0),
                                                stop=(t == T - 1 and a == 1))
                return last

            def four_tiles(m, half, last_block):
                for n in range(T):
                    q = m * T + n
                    if not (last_block and n == T - 1):
                        turn(q + 1, (n + 1) % 2)
                    pe.wait_ge(low_done, 2 + q + 1)
                    pe.wait_ge(sd_copied, q + 1)
                    pe.wait_ge(wh_copied, q - 1 if not isinstance(m, int) or q else 0)
                    mine = lambda a, t: h_t[:, half, a, t, n * P:(n + 1) * P]
                    products(psum[:, n % 2, :], mine, lambda b, t: w_half[:, b, t, 0:512])
                    products(psum[:, 2 + n % 2, 0:2 * HEADS], mine, lambda b, t: w_half[:, b, t, 512:WIDE]).then_inc(feature_done, 1)
                pe.wait_ge(rows_copied, m)
                products(psum[0:HEADS, 4, :], lambda a, t: w_half[:, a, t, 512:512 + HEADS],
                         lambda b, t: h_t[:, half, b, t, :]).then_inc(rows_done, 1)

            pe.sem_inc(rows_done, 1)
            turn(0, 0)
            four_tiles(0, 0, False)
            with pe.Fori(0, TILES // T // 2 - 1) as it:
                four_tiles(it * 2 + 1, 1, False)
                four_tiles(it * 2 + 2, 0, False)
            four_tiles(TILES // T - 1, 1, True)
            pe.wait_ge(added, 1 + TILES)
            pe.wait_ge(rows_copied, TILES // T)
            nc.tensor.matmul(psum[:, 4, :], mean_w[:], wh_sum[:], start=True, stop=True).then_inc(mean_done, 1)

        @block.scalar
        def _(act):
            act.sem_inc(h_done, 1)

            def tile(m, n, half):
                q = m * T + n
                row_relu_norm(nc, act, x_tile[:, n % 2], scale, q, norm_done, h_done)
                act.wait_ge(rows_done, m)
                act.wait_ge(turned, q + 1)
                nc.scalar.copy(h_t[:, half, 0, :, n * P:(n + 1) * P],
                               psum[:, 6 + n % 2, :].rearrange("p (t i) -> p t i", t=T)).then_inc(high_done, 1)

            def feature(q, par, n_stored):
                act.wait_ge(feature_done, q + 1)
                act.wait_ge(added, q if not isinstance(q, int) or q else 0)
                act.wait_ge(wh_stored[par], n_stored * 16)
                nc.scalar.activation(wh_tile[:, par], psum[:, par, :], ACT.Copy, scale=1.0 / UP).then_inc(wh_copied, 1)

            for n in range(2):
                tile(0, n, 0)
            for n in range(2, T):
                feature(n - 2, n % 2, 0)
                tile(0, n, 0)

            def block_of(m, half):
                for n in range(T):
                    feature(m * T + n - 2, n % 2, (m * T + n - 2) // 2 if isinstance(m, int) else m * 2 + n // 2 - 1)
                    tile(m, n, half)

            with act.Fori(0, TILES // T // 2 - 1) as it:
                block_of(it * 2 + 1, 1)
                block_of(it * 2 + 2, 0)
            block_of(TILES // T - 1, 1)
            for n in range(TILES - 2, TILES):
                feature(n, n % 2, n // 2)
            act.wait_ge(exp_ready, 1)
            for k, (src, mult) in enumerate(((0, 1.0), (0, SLOPE), (1, 1.0), (2, 1.0))):
                dst = node["factor_j"] if k < 2 else node["factor_i"]
                nc.scalar.activation(dst[:, :, :, k % 2], z[:, src], ACT.Exp, scale=mult).then_inc(exp_done, 1)
            act.wait_ge(exp_done, 4)

        @block.vector
        def _(dve):
            dve.sem_inc(low_done, 2)
            dve.sem_inc(sd_copied, 2)
            nc.vector.memset(mean_w[:], 1.0 / NODES).then_inc(ready, 1)
            dve.wait_ge(weights_in, 64)
            for n in range(2 * T):
                t, k = n // 2, n % 2
                dve.wait_ge(wa_step, 2 * n)
                nc.vector.tensor_tensor(w_a[:], w_all[:, t, 0:512], a_rows[:, k], ALU.mult).then_inc(wa_step, 1)
                dve.wait_ge(wa_step, 2 * n + 1)
                nc.vector.tensor_reduce(w_all[:, t, 512 + k * HEADS:512 + (k + 1) * HEADS],
                                        w_a[:].rearrange("p (h k) -> p h k", h=HEADS), AX, ALU.add).then_inc(wa_step, 1)
            dve.wait_ge(wa_step, 4 * T)
            for t in range(0, T, 2):
                nc.vector.tensor_scalar(w_half[:, 0, t:t + 2, :], w_all[:, t:t + 2, :], UP, None, ALU.mult).then_inc(halves_done, 1)
            dve.wait_ge(halves_done, 2)
            for t in range(0, T, 2):
                nc.vector.scalar_tensor_tensor(out=w_half[:, 1, t:t + 2, :], in0=w_all[:, t:t + 2, :], scalar=UP,
                                               in1=w_half[:, 0, t:t + 2, :], op0=ALU.mult, op1=ALU.subtract).then_inc(halves_done, 1)

            def norm(q, par, n_in):
                dve.wait_ge(x_in[par], n_in * 16)
                row_norm(nc, dve, x_tile[:, par], stats, sums, scale, q, sems.dve, stats_done, sums_done, rstd_done, norm_done)

            def tile(m, n, half, norm_next):
                q = m * T + n
                if norm_next:
                    norm(q + 1, (n + 1) % 2, m * 2 + (n + 1) // 2 + 1)
                dve.wait_ge(high_done, q + 1)
                nc.vector.tensor_tensor(h_t[:, half, 1, :, n * P:(n + 1) * P],
                                        psum[:, 6 + n % 2, :].rearrange("p (t i) -> p t i", t=T),
                                        h_t[:, half, 0, :, n * P:(n + 1) * P], ALU.subtract).then_inc(low_done, 1)
                dve.wait_ge(feature_done, q + 1)
                nc.vector.tensor_scalar(sd[:, q:q + 1, :] if isinstance(q, int) else sd[:, bass.ds(q, 1), :],
                                        psum[:, 2 + n % 2, 0:2 * HEADS].rearrange("p (o n) -> p o n", o=1),
                                        1.0 / UP, None, ALU.mult).then_inc(sd_copied, 1)

            def rows(m):
                dve.wait_ge(rows_done, 1 + m + 1)
                nc.vector.tensor_scalar(s_row[:, bass.ds(m * 512, 512)], psum[0:HEADS, 4, :], 1.0 / UP, None,
                                        ALU.mult).then_inc(rows_copied, 1)

            norm(0, 0, 1)
            with dve.Fori(0, TILES // T // 2 - 1) as it:
                for half in range(2):
                    for n in range(T):
                        tile(it * 2 + half, n, half, True)
                    rows(it * 2 + half)
            for m in (TILES // T - 2, TILES // T - 1):
                for n in range(T):
                    tile(m, n, m % 2, m * T + n + 1 < TILES)
                rows(m)
            s_all, d_all = sd[:, :, 0:HEADS], sd[:, :, HEADS:2 * HEADS]
            dve.wait_ge(sd_copied, 2 + TILES)
            nc.vector.tensor_reduce(d_top[:, 0], d_all.rearrange("p n h -> p h n"), AX, ALU.max).then_inc(factor_step, 1)
            nc.vector.tensor_scalar(node["gate_d"][:], d_all, GATE, None, ALU.mult).then_inc(ready, 1)
            dve.wait_ge(factor_step, 2)
            top = d_top[:, 1:2, :].broadcast_to([P, TILES, HEADS])
            nc.vector.tensor_tensor(z[:, 0], d_all, top, ALU.subtract).then_inc(factor_step, 1)
            nc.vector.tensor_tensor(z[:, 1], s_all, top, ALU.add).then_inc(factor_step, 1)
            dve.wait_ge(factor_step, 4)
            nc.vector.tensor_scalar(z[:, 2], z[:, 1], SLOPE, None, ALU.mult).then_inc(factor_step, 1)
            dve.wait_ge(factor_step, 5)
            nc.vector.tensor_tensor(z[:, 3], z[:, 1], z[:, 2], ALU.max).then_inc(factor_step, 1)
            dve.wait_ge(factor_step, 6)
            for k in (1, 2):
                nc.vector.tensor_tensor(z[:, k], z[:, k], z[:, 3], ALU.subtract).then_inc(factor_step, 1)
            dve.wait_ge(factor_step, 8)
            dve.sem_inc(exp_ready, 1)
            dve.wait_ge(mean_done, 1)
            nc.vector.tensor_copy(node["mean"][:], psum[:, 4, :]).then_inc(mean_copied, 1)
            dve.wait_ge(mean_copied, 1)


GROUP = 4
PARTS, COLS = 3, HD + 1
HALF = PARTS * COLS


def split_features(nc, sems, psum, wh_dram, node, x_parts, gr):
    TILES = NODES // P
    with ExitStack() as ctx:
        def sb(name, shape, dt=F32):
            return ctx.enter_context(nc.sbuf_tensor(f"{name}_g{gr}", shape, dt))

        def sem(name):
            return sems.new((f"{name}_g{gr}"))

        wh = sb("wh", [P, 2, GROUP, HD])
        f = sb("f", [P, 2, GROUP, 2, COLS])
        rest = sb("rest", [P, 2, GROUP, 2, COLS])
        wh_in = [sem(f"wh_in{i}") for i in range(2)]
        f_done, first_done, rest_done, second_done, third_done = (sem(n) for n in ("f", "first", "rest_s", "second", "third"))
        block = ctx.enter_context(nc.Block())
        whv = wh_dram.rearrange("(n p) k -> n p k", p=P)[:, :, gr * GROUP * HD:(gr + 1) * GROUP * HD]
        hs = slice(gr * GROUP, (gr + 1) * GROUP)

        def part(n, k):
            return x_parts[:, bass.ds(n, 1), :, :, k, :].rearrange("p o h b c -> p (o h b) c")

        def flat(t, par):
            return t[:, par].rearrange("p h b c -> p (h b) c")

        @block.sync
        def _(sp):
            for n in range(2):
                sp.dma_start(wh[:, n].rearrange("p h k -> p (h k)"), whv[n]).then_inc(wh_in[n], 16)
            with sp.Fori(0, TILES // 2 - 1) as it:
                for par in range(2):
                    n = it * 2 + par
                    sp.wait_ge(f_done, n * 3 + 3)
                    sp.dma_start(wh[:, par].rearrange("p h k -> p (h k)"), whv[n + 2]).then_inc(wh_in[par], 16)

        @block.gpsimd
        def _(pool):
            pool.sem_inc(third_done, 2)
            with pool.Fori(0, TILES // 2) as it:
                for par in range(2):
                    n = it * 2 + par
                    pool.wait_ge(wh_in[par], it * 16 + 16)
                    pool.wait_ge(third_done, n + 1)
                    factor = node["factor_j"][:, bass.ds(n, 1), hs, :].rearrange("p o h b -> p (o h) b")
                    for b in range(2):
                        nc.gpsimd.tensor_tensor(f[:, par, :, b, 0:HD], wh[:, par],
                                                factor[:, :, b:b + 1].broadcast_to([P, GROUP, HD]), ALU.mult).then_inc(f_done, 1)
                    nc.gpsimd.tensor_copy(f[:, par, :, :, HD], factor).then_inc(f_done, 1)

        @block.scalar
        def _(act):
            with act.Fori(0, TILES // 2) as it:
                for par in range(2):
                    n = it * 2 + par
                    wait_alone(act, f_done, n * 3 + 3, sems.act)
                    nc.scalar.copy(part(n, 0), flat(f, par)).then_inc(first_done, 1)
                    wait_alone(act, rest_done, n + 1, sems.act)
                    nc.scalar.copy(part(n, 1), flat(rest, par)).then_inc(second_done, 1)

        @block.vector
        def _(dve):
            with dve.Fori(0, TILES // 2) as it:
                for par in range(2):
                    n = it * 2 + par
                    dve.wait_ge(first_done, n + 1)
                    nc.vector.tensor_tensor(flat(rest, par), flat(f, par), part(n, 0), ALU.subtract).then_inc(rest_done, 1)
                    dve.wait_ge(second_done, n + 1)
                    nc.vector.tensor_tensor(part(n, 2), flat(rest, par), part(n, 1), ALU.subtract).then_inc(third_done, 1)


def graph_attention(nc, sems, d, psum, srow_dram, enc_dram, node, x_parts, gr):
    TILES, QW = NODES // P, 512
    BLOCKS, CHUNKS, SUBS = NODES // QW, TILES // 2, QW // P
    with ExitStack() as ctx:
        def sb(name, shape, dt=F32):
            return ctx.enter_context(nc.sbuf_tensor(f"{name}_a{gr}", shape, dt))

        def sem(name):
            return sems.new((f"{name}_a{gr}"))

        adj = sb("adj", [P, 2, TILES, QW], BF16)
        s_row = sb("s_row", [P, 2, QW])
        gate = sb("gate", [P, 2, 2, QW], BF16)
        cells = sb("cells", [P, 2, 2, 2, QW], BF16)
        raw = sb("raw", [P, SUBS, 2, PARTS, COLS])
        num = sb("num", [P, SUBS, 2, COLS])
        y = sb("y", [P, SUBS, COLS])
        none, safe, minus_one = (sb(n, [P, SUBS]) for n in ("none", "safe", "minus_one"))
        spare = sb("spare", [P, SUBS, HD])
        enc = sb("enc", [P, SUBS, GROUP, HD])
        adj_in = [sem(f"adj_in{i}") for i in range(2)]
        s_in = [sem(f"s_in{i}") for i in range(2)]
        gate_done, above_done, cells_done, cells_used = (sem(n) for n in ("gate", "above", "cells", "cells_used"))
        head_done, copied, pool_step, enc_stored, constant_in = (sem(n) for n in ("head", "copied", "pool_step", "enc_stored", "constant_in"))
        block = ctx.enter_context(nc.Block())
        adj_v = d["adjT"].rearrange("(n p) i -> p n i", p=P)
        enc_v = enc_dram.rearrange("(n s p) k -> n p s k", p=P, s=SUBS)[:, :, :, gr * GROUP * HD:(gr + 1) * GROUP * HD]
        STEPS = 11

        @block.sync
        def _(sp):
            def load(b, h):
                src = srow_dram[gr * GROUP + h:gr * GROUP + h + 1, bass.ds(b * QW, QW)]
                sp.dma_start(s_row[:, h % 2], src.broadcast_to([P, QW])).then_inc(s_in[h % 2], 16)

            for h in range(2):
                load(0, h)
            with sp.Fori(0, BLOCKS - 1) as b:
                for h in range(GROUP):
                    sp.wait_ge(gate_done, (b * GROUP + h + 1) * CHUNKS)
                    load(b + (h + 2) // GROUP, (h + 2) % GROUP)
            for h in range(GROUP - 2):
                sp.wait_ge(gate_done, ((BLOCKS - 1) * GROUP + h + 1) * CHUNKS)
                load(BLOCKS - 1, h + 2)

        @block.gpsimd
        def _(pool):
            def load_adj(b, par):
                for c in range(0, TILES, 4):
                    pool.dma_start(adj[:, par, c:c + 4, :], adj_v[:, c:c + 4, bass.ds(b * QW, QW)]).then_inc(adj_in[par], 16)

            def combine(b, h):
                u = b * GROUP + h
                base = u * STEPS

                def op(k, dst, a, c, f):
                    pool.wait_ge(pool_step, 1 + base + k)
                    nc.gpsimd.tensor_tensor(dst, a, c, f).then_inc(pool_step, 1)

                pool.wait_ge(copied, 2 + u + 1)
                raw_v = raw[:].rearrange("p s b k c -> p (s b) k c")
                num_v = num[:].rearrange("p s b c -> p (s b) c")
                op(0, num_v, raw_v[:, :, 0], raw_v[:, :, 1], ALU.add)
                op(1, num_v, num_v, raw_v[:, :, 2], ALU.add)
                f_i = node["factor_i"][:, bass.ds(b * SUBS, SUBS), gr * GROUP + h, :]
                op(2, num[:], num[:], f_i.rearrange("p s (b o) -> p s b o", o=1).broadcast_to([P, SUBS, 2, COLS]), ALU.mult)
                op(3, y[:], num[:, :, 0], num[:, :, 1], ALU.add)
                wait_alone(pool, pool_step, 1 + base + 4, sems.pool)
                nc.gpsimd.tensor_scalar(none[:], y[:, :, HD], 0.0, None, ALU.is_equal).then_inc(pool_step, 1)
                op(5, safe[:], y[:, :, HD], none[:], ALU.add)
                op(6, safe[:], safe[:], minus_one[:], ALU.pow)
                op(7, enc[:, :, h], y[:, :, 0:HD], safe[:].rearrange("p (s o) -> p s o", o=1).broadcast_to([P, SUBS, HD]), ALU.mult)
                mean = node["mean"][:, (gr * GROUP + h) * HD:(gr * GROUP + h + 1) * HD]
                op(8, spare[:], none[:].rearrange("p (s o) -> p s o", o=1).broadcast_to([P, SUBS, HD]),
                   mean.rearrange("p (o k) -> p o k", o=1).broadcast_to([P, SUBS, HD]), ALU.mult)
                op(9, enc[:, :, h], enc[:, :, h], spare[:], ALU.add)
                pool.wait_ge(pool_step, 1 + base + 10)
                pool.sem_inc(pool_step, 1)
                if h == GROUP - 1:
                    wait_alone(pool, pool_step, 1 + base + STEPS, sems.pool)
                    for s in range(SUBS):
                        src = enc[:, s].rearrange("p h k -> p (h k)")
                        dst = enc_v[b, :, s, :] if isinstance(b, int) else enc_v[bass.ds(b, 1), :, s, :].rearrange("o p k -> (o p) k")
                        pool.dma_start(dst, src).then_inc(enc_stored, 16)
                    wait_alone(pool, enc_stored, (b + 1) * SUBS * 16, sems.pool)

            pool.sem_inc(pool_step, 1)
            nc.gpsimd.memset(minus_one[:], -1.0).then_inc(constant_in, 1)
            pool.wait_ge(constant_in, 1)
            load_adj(0, 0)
            load_adj(1, 1)

            def four(b, par, more):
                for h in range(GROUP):
                    combine(b, h)
                if more:
                    wait_alone(pool, cells_done, (b + 1) * GROUP * CHUNKS, sems.pool)
                    load_adj(b + 2, par)

            with pool.Fori(0, BLOCKS // 2 - 1) as it:
                for par in range(2):
                    four(it * 2 + par, par, True)
            for par in range(2):
                four(BLOCKS - 2 + par, par, False)

        @block.scalar
        def _(act):
            act.sem_inc(copied, 2)

            def gates(b, h, c0, c1):
                with act.Fori(c0, c1) as cc:
                    for par in range(2):
                        n = (b * GROUP + h) * CHUNKS + cc * 2 + par
                        wait_alone(act, above_done, n + 1, sems.act)
                        for a in range(2):
                            ins = nc.scalar.activation(gate[:, par, a], s_row[:, h % 2], ACT.Sigmoid, scale=GATE,
                                                       bias=node["gate_d"][:, bass.ds(cc * 4 + par * 2 + a, 1), gr * GROUP + h])
                        ins.then_inc(gate_done, 1)

            def copy_head(u, par):
                act.wait_ge(head_done, u + 1)
                act.wait_ge(pool_step, 1 + u * STEPS)
                nc.scalar.copy(raw[:].rearrange("p s b k c -> p s (b k c)"), psum[:, par * SUBS:(par + 1) * SUBS, 0:2 * HALF]).then_inc(copied, 1)

            def heads(b, first):
                for h in range(GROUP):
                    act.wait_ge(s_in[h % 2], (b * 2 + h // 2) * 16 + 16)
                    gates(b, h, 0, 3)
                    if not (first and h == 0):
                        copy_head(b * GROUP + h - 1, (h - 1) % 2)
                    gates(b, h, 3, CHUNKS // 2)

            heads(0, True)
            with act.Fori(1, BLOCKS) as b:
                heads(b, False)
            copy_head(BLOCKS * GROUP - 1, 1)

        @block.vector
        def _(dve):
            dve.sem_inc(above_done, 2)
            dve.sem_inc(cells_used, 2)
            with dve.Fori(0, BLOCKS // 2) as it:
                for bp in range(2):
                    wait_alone(dve, adj_in[bp], (it + 1) * 16 * (TILES // 4), sems.dve)
                    with dve.Fori(0, GROUP) as h:
                        with dve.Fori(0, CHUNKS // 2) as cc:
                            for par in range(2):
                                n = ((it * 2 + bp) * GROUP + h) * CHUNKS + cc * 2 + par
                                edges = adj[:, bp, bass.ds(cc * 4 + par * 2, 2), :]
                                dve.wait_ge(gate_done, n + 1)
                                dve.wait_ge(cells_used, n + 1)
                                nc.vector.tensor_tensor(cells[:, par, 0], gate[:, par], edges, ALU.mult).then_inc(above_done, 1)
                                dve.wait_ge(above_done, 2 + n + 1)
                                nc.vector.tensor_tensor(cells[:, par, 1], edges, cells[:, par, 0], ALU.subtract).then_inc(cells_done, 1)

        @block.tensor
        def _(pe):
            def chunk(b, h, c, par, first, last_chunk):
                n = (b * GROUP + h) * CHUNKS + c
                pe.wait_ge(cells_done, n + 1)
                for a in range(2):
                    for s in range(SUBS):
                        for k in range(2):
                            moving = x_parts[:, bass.ds(c * 2 + a, 1), h, k].rearrange("p o k c -> p (o k c)")
                            last = nc.tensor.matmul(psum[:, (h % 2) * SUBS + s, k * HALF:(k + 1) * HALF],
                                                    cells[:, par, k, a, s * P:(s + 1) * P], moving,
                                                    start=(first and a == 0 and k == 0),
                                                    stop=(last_chunk and a == 1 and k == 1), skip_group_check=True)
                return last

            with pe.Fori(0, BLOCKS) as b:
                for h in range(GROUP):
                    wait_alone(pe, copied, b * GROUP + h + 1, sems.pe)
                    for par in range(2):
                        chunk(b, h, par, par, par == 0, False).then_inc(cells_used, 1)
                    with pe.Fori(1, CHUNKS // 2 - 1) as cc:
                        for par in range(2):
                            chunk(b, h, cc * 2 + par, par, False, False).then_inc(cells_used, 1)
                    for par in range(2):
                        last = chunk(b, h, CHUNKS - 2 + par, par, False, par == 1)
                        last.then_inc(cells_used, 1)
                    pe.wait_ge(cells_used, 2 + (b * GROUP + h + 1) * CHUNKS)
                    pe.sem_inc(head_done, 1)


def mlp(nc, sems, d, psum, x1_dram, enc_dram):
    QW = 512
    BLOCKS, SUBS = NODES // QW, QW // P
    with ExitStack() as ctx:
        def sb(name, shape, dt=F32):
            return ctx.enter_context(nc.sbuf_tensor(name, shape, dt))

        def sem(name):
            return sems.new((name))

        w1, w2, w3, w4 = sb("w1", [P, 4, 256]), sb("w2", [P, 2, 128]), sb("w3", [P, 1, 256]), sb("w4", [P, 2, 512])
        biases, b4 = sb("biases", [P, 5]), sb("b4", [P, 512])
        ident = sb("ident4", [P, P])
        enc, neg = sb("enc4", [P, 2, SUBS, 512]), sb("neg", [P, 2, SUBS, 512])
        enc_t, a1, a2, a3 = sb("enc_t", [P, 4, QW]), sb("a1t", [P, 2, QW]), sb("a2t", [P, QW]), sb("a3t", [P, 2, QW])
        x1 = sb("x1_4", [P, 2, SUBS, 512])
        weights_in = sem("weights_in4")
        enc_in, x_in, out_stored = ([sem(f"{n}{i}") for i in range(2)] for n in ("enc_in4", "x_in4", "out_stored"))
        neg_done, pos_done, exp_done, elu_done, turned, turn_copied = (sem(n) for n in ("neg_done", "pos_done", "exp_done4", "elu_done", "turned4", "turn_copied"))
        layer_done, layer_copied, biased, out_done = (sem(n) for n in ("layer_done", "layer_copied", "biased", "out_done"))
        block = ctx.enter_context(nc.Block())
        enc_v = enc_dram.rearrange("(n s p) k -> n p s k", p=P, s=SUBS)
        x1_v = x1_dram.rearrange("(n s p) k -> n p s k", p=P, s=SUBS)
        out_v = d["out"].rearrange("(n s p) k -> n p s k", p=P, s=SUBS)
        STAGES = 9

        @block.sync
        def _(sp):
            for dst, name, k in ((w1, "W1T", 4), (w2, "W2T", 2), (w3, "W3T", 1), (w4, "W4T", 2)):
                sp.dma_start(dst[:], d[name].rearrange("(t p) n -> p t n", p=P)).then_inc(weights_in, 16)
            sp.dma_start(biases[:], d["mlp_bias_cols"]).then_inc(weights_in, 16)
            sp.dma_start(b4[:], d["b4_rows"]).then_inc(weights_in, 16)
            sp.dma_start(ident[:], d["ident"]).then_inc(weights_in, 16)

            def load(b, par):
                sp.dma_start(enc[:, par], enc_v[b]).then_inc(enc_in[par], 16)
                sp.dma_start(x1[:, par], x1_v[b]).then_inc(x_in[par], 16)

            for par in range(2):
                load(par, par)

            def store(b, par, it):
                wait_alone(sp, x_in[par], it * 16 + 16, sems.sp)
                wait_alone(sp, out_done, 1 + (b + 1) * SUBS, sems.sp)
                sp.dma_start(out_v[b], x1[:, par]).then_inc(out_stored[par], 16)

            with sp.Fori(0, BLOCKS // 2 - 1) as it:
                for par in range(2):
                    store(it * 2 + par, par, it)
                    sp.wait_ge(out_stored[par], it * 16 + 16)
                    load(it * 2 + par + 2, par)
            for par in range(2):
                store(BLOCKS - 2 + par, par, BLOCKS // 2 - 1)
                sp.wait_ge(out_stored[par], (BLOCKS // 2) * 16)

        @block.vector
        def _(dve):
            dve.sem_inc(out_done, 1)
            dve.wait_ge(weights_in, 112)
            with dve.Fori(0, BLOCKS // 2) as it:
                for par in range(2):
                    b = it * 2 + par
                    dve.wait_ge(enc_in[par], it * 16 + 16)
                    nc.vector.tensor_scalar(neg[:, par], enc[:, par], 0.0, None, ALU.min).then_inc(neg_done, 1)
                    dve.wait_ge(neg_done, b + 1)
                    nc.vector.tensor_scalar(enc[:, par], enc[:, par], 0.0, -1.0, ALU.max, ALU.add).then_inc(pos_done, 1)
                    dve.wait_ge(pos_done, b + 1)
                    dve.wait_ge(exp_done, b + 1)
                    nc.vector.tensor_tensor(enc[:, par], enc[:, par], neg[:, par], ALU.add).then_inc(elu_done, 1)
                    for s in range(SUBS):
                        dve.wait_ge(layer_done, (b * 9) + 5 + s + 1)
                        dve.wait_ge(biased, b + 1)
                        nc.vector.tensor_tensor(x1[:, par, s], psum[:, 4 + s, :], x1[:, par, s], ALU.add).then_inc(out_done, 1)

        @block.gpsimd
        def _(pool):
            pool.wait_ge(weights_in, 112)
            with pool.Fori(0, BLOCKS // 2) as it:
                for par in range(2):
                    pool.wait_ge(x_in[par], it * 16 + 16)
                    nc.gpsimd.tensor_tensor(x1[:, par], x1[:, par],
                                            b4[:].rearrange("p (o k) -> p o k", o=1).broadcast_to([P, SUBS, 512]), ALU.add).then_inc(biased, 1)

        @block.tensor
        def _(pe):
            pe.wait_ge(weights_in, 112)
            with pe.Fori(0, BLOCKS // 2) as it:
                for par in range(2):
                    b = it * 2 + par
                    pe.wait_ge(elu_done, b + 1)
                    for t in range(4):
                        pe.wait_ge(layer_copied, 1 + b * STAGES)
                        for s in range(SUBS):
                            last = nc.tensor.transpose(psum[:, t, s * P:(s + 1) * P], enc[:, par, s, t * P:(t + 1) * P], ident[:])
                        last.then_inc(turned, 1)
                    pe.wait_ge(layer_copied, 1 + b * STAGES + 4)
                    for o in range(2):
                        for t in range(4):
                            last = nc.tensor.matmul(psum[:, o, :], w1[:, t, o * P:(o + 1) * P], enc_t[:, t, :], start=(t == 0), stop=(t == 3))
                        last.then_inc(layer_done, 1)
                    pe.wait_ge(layer_copied, 1 + b * STAGES + 6)
                    for t in range(2):
                        last = nc.tensor.matmul(psum[:, 2, :], w2[:, t, :], a1[:, t, :], start=(t == 0), stop=(t == 1))
                    last.then_inc(layer_done, 1)
                    pe.wait_ge(layer_copied, 1 + b * STAGES + 7)
                    for o in range(2):
                        nc.tensor.matmul(psum[:, o, :], w3[:, 0, o * P:(o + 1) * P], a2[:], start=True, stop=True).then_inc(layer_done, 1)
                    pe.wait_ge(layer_copied, 1 + b * STAGES + 9)
                    pe.wait_ge(out_done, 1 + b * SUBS)
                    for s in range(SUBS):
                        for t in range(2):
                            last = nc.tensor.matmul(psum[:, 4 + s, :], a3[:, t, s * P:(s + 1) * P], w4[:, t, :], start=(t == 0), stop=(t == 1))
                        last.then_inc(layer_done, 1)

        @block.scalar
        def _(act):
            act.sem_inc(layer_copied, 1)
            act.wait_ge(weights_in, 112)
            with act.Fori(0, BLOCKS // 2) as it:
                for par in range(2):
                    b = it * 2 + par
                    act.wait_ge(neg_done, b + 1)
                    nc.scalar.activation(neg[:, par], neg[:, par], ACT.Exp).then_inc(exp_done, 1)
                    for t in range(4):
                        act.wait_ge(turned, b * 4 + t + 1)
                        nc.scalar.copy(enc_t[:, t, :], psum[:, t, :]).then_inc(layer_copied, 1)
                    for k, (dst, bank) in enumerate(((a1[:, 0], 0), (a1[:, 1], 1), (a2[:], 2), (a3[:, 0], 0), (a3[:, 1], 1))):
                        act.wait_ge(layer_done, b * 9 + k + 1)
                        nc.scalar.activation(dst, psum[:, bank, :], ACT.Relu, bias=biases[:, k:k + 1]).then_inc(layer_copied, 1)


def build(nc, d, upto=9):
    ht_dram = nc.dram_tensor("ht_dram", (NODES // QB, P, 2 * 4 * QB), F16, kind="Internal").ap()
    x1_dram = nc.dram_tensor("x1_dram", (NODES, 512), F32, kind="Internal").ap()
    wh_dram = nc.dram_tensor("wh_dram", (NODES, 512), F32, kind="Internal").ap()
    enc_dram = nc.dram_tensor("enc_dram", (NODES, 512), F32, kind="Internal").ap()
    srow_dram = nc.dram_tensor("srow_dram", (HEADS, NODES), F32, kind="Internal").ap()
    with nc.psum_tensor("psum", [P, 8, 512], F32) as psum, ExitStack() as stack:
        sems = Semaphores(nc, stack)
        with nc.sbuf_tensor("g", [P, 2, 4, NODES], F16) as g, nc.sbuf_tensor("v", [P, 2, 32, 512], F16) as v, \
                nc.sbuf_tensor("c_all", [P, 32], F32) as c_all:
            with nc.sbuf_tensor("wqk", [P, 4, 512], F32) as wqk, nc.sbuf_tensor("wvm", [P, 4, 512], F32) as wvm, \
                    nc.sbuf_tensor("bias_cols", [P, 9], F32) as bias_cols, nc.sbuf_tensor("bvm", [P, 512], F32) as bvm:
                keep = {"wqk": wqk, "wvm": wvm, "bias_cols": bias_cols, "bvm": bvm}
                weight_products(nc, sems, d, keep, psum)
                keys_and_values(nc, sems, d, keep, psum, g, v, c_all, ht_dram)
            if upto >= 1:
                attention(nc, sems, d, psum, g, v, c_all, ht_dram, x1_dram)
        if upto >= 2:
            with ExitStack() as ctx:
                node = {n: ctx.enter_context(nc.sbuf_tensor(n, shape, F32)) for n, shape in (
                    ("factor_j", [P, 32, HEADS, 2]), ("factor_i", [P, 32, HEADS, 2]), ("gate_d", [P, 32, HEADS]), ("mean", [P, 512]))}
                head_features(nc, sems, d, psum, x1_dram, wh_dram, srow_dram, node)
                if upto >= 3:
                    x_parts = ctx.enter_context(nc.sbuf_tensor("x_parts", [P, 32, GROUP, 2, PARTS, COLS], BF16))
                    for gr in range(HEADS // GROUP):
                        split_features(nc, sems, psum, wh_dram, node, x_parts, gr)
                        graph_attention(nc, sems, d, psum, srow_dram, enc_dram, node, x_parts, gr)
        if upto >= 4:
            mlp(nc, sems, d, psum, x1_dram, enc_dram)


PLAIN = ("x", "L0_gnn_Wk", "L0_gnn_Wq", "L0_gnn_Wv")


def host_layout(inputs):
    import numpy as np

    def transposed(name):
        return np.ascontiguousarray(np.asarray(inputs[name]).T)

    def rows(a):
        a = np.asarray(a).reshape(-1)
        return np.ascontiguousarray(np.broadcast_to(a, (P, a.size)))

    def cols(name):
        return np.ascontiguousarray(np.asarray(inputs[name]).reshape(-1, P).T)

    arrays = {n: np.ascontiguousarray(inputs[n]) for n in PLAIN}
    arrays["adjT"] = transposed("adj")
    arrays["keyT"] = transposed("L0_gnn_key")
    arrays["valueT"] = transposed("L0_gnn_value")
    arrays["WmT"] = transposed("L0_gnn_Wm")
    arrays["bm_rows"] = rows(inputs["L0_gnn_bm"])
    for b in ("bq", "bk", "bv"):
        arrays[f"{b}_cols"] = cols(f"L0_gnn_{b}")
    w = np.asarray(inputs["L1_gnn_W"])
    arrays["W_heads"] = np.ascontiguousarray(w.transpose(1, 0, 2).reshape(w.shape[1], -1))
    arrays["a1_rows"] = rows(inputs["L1_gnn_a1"])
    arrays["a2_rows"] = rows(inputs["L1_gnn_a2"])
    for n in range(1, 5):
        arrays[f"W{n}T"] = transposed(f"L1_gnn_W{n}")
    arrays["mlp_bias_cols"] = np.ascontiguousarray(np.concatenate([cols(f"L1_gnn_b{n}") for n in (1, 2, 3)], axis=1))
    arrays["b4_rows"] = rows(inputs["L1_gnn_b4"])
    arrays["ident"] = np.eye(P, dtype=np.float32)
    return arrays


def kernel(**inputs):
    import concourse.bacc as bacc
    from concourse import mybir as ir
    from concourse.bass_utils import run_bass_kernel_spmd

    nc = bacc.Bacc("TRN2", target_bir_lowering=False, num_devices=1)
    arrays = host_layout(inputs)
    d = {n: nc.dram_tensor(n, a.shape, ir.dt.from_np(a.dtype), kind="ExternalInput").ap() for n, a in arrays.items()}
    d["out"] = nc.dram_tensor("out", (NODES, 512), F32, kind="ExternalOutput").ap()
    build(nc, d)
    return run_bass_kernel_spmd(nc, [arrays], core_ids=[0]).results[0]["out"]
```

```python
from contextlib import ExitStack

import concourse.bass as bass
from concourse import mybir

F32 = mybir.dt.float32
F16 = mybir.dt.float16
BF16 = mybir.dt.bfloat16
ALU = mybir.AluOpType
ACT = mybir.ActivationFunctionType
AX = mybir.AxisListType.X
RMAX = bass.bass_isa.ReduceOp.max

P = 128
EPS = 1e-5


class Semaphores:

    def __init__(self, nc, ctx):
        self.nc, self.ctx = nc, ctx
        self.act, self.pool, self.pe, self.dve, self.sp = (self.new(f"{n}_carrier") for n in ("act", "pool", "pe", "dve", "sp"))

    def new(self, name):
        return self.ctx.enter_context(self.nc.semaphore(name))


def wait_alone(eng, sem, value, carrier):
    eng.wait_ge(sem, value)
    eng.sem_inc(carrier, 1)


def row_norm(nc, dve, x, stats, sums, scale, tile, carrier, stats_done, sums_done, rstd_done, norm_done):
    nc.vector.bn_stats(stats[:], x).then_inc(stats_done, 1)
    wait_alone(dve, stats_done, tile + 1, carrier)
    nc.vector.bn_aggr(sums[:, 0:2], stats[:]).then_inc(sums_done, 1)
    dve.wait_ge(sums_done, tile * 2 + 1)
    nc.vector.tensor_scalar(sums[:, 2:3], sums[:, 1:2], EPS, None, ALU.add).then_inc(sums_done, 1)
    dve.wait_ge(rstd_done, tile + 1)
    nc.vector.scalar_tensor_tensor(out=scale[:, 1:2], in0=sums[:, 0:1], scalar=-1.0, in1=scale[:, 0:1],
                                   op0=ALU.mult, op1=ALU.mult).then_inc(norm_done, 1)


def row_rstd(nc, pool, sums, scale, tile, sums_done, h_done, rstd_done):
    pool.wait_ge(h_done, 1 + tile)
    pool.wait_ge(sums_done, tile * 2 + 2)
    nc.gpsimd.tensor_tensor(scale[:, 0:1], sums[:, 2:3], sums[:, 3:4], ALU.pow).then_inc(rstd_done, 1)


def row_relu_norm(nc, act, x, scale, tile, norm_done, h_done):
    act.wait_ge(norm_done, tile + 1)
    nc.scalar.activation(x, x, ACT.Relu, scale=scale[:, 0:1], bias=scale[:, 1:2]).then_inc(h_done, 1)


def weight_products(nc, sems, d, keep, psum):
    T = 4
    with ExitStack() as ctx:
        def sb(name, shape, dt=F32):
            return ctx.enter_context(nc.sbuf_tensor(name, shape, dt))

        def sem(name):
            return sems.new((name))

        wk, wq, wv, wm = (sb(f"{n}_raw", [P, T, 512]) for n in ("wk", "wq", "wv", "wm"))
        bq, bk, bv = (sb(f"{n}_col", [P, T]) for n in ("bq", "bk", "bv"))
        bm = sb("bm_row", [P, 512])
        loaded_qk, loaded_vm = sem("loaded_qk"), sem("loaded_vm")
        product_done, product_copied = sem("product_done"), sem("product_copied")
        block = ctx.enter_context(nc.Block())

        @block.sync
        def _(sp):
            for dst, src in ((wk, d["L0_gnn_Wk"]), (wq, d["L0_gnn_Wq"])):
                sp.dma_start(dst[:], src.rearrange("(t p) n -> p t n", p=P)).then_inc(loaded_qk, 16)
            for dst, src in ((wv, d["L0_gnn_Wv"]), (wm, d["WmT"])):
                sp.dma_start(dst[:], src.rearrange("(t p) n -> p t n", p=P)).then_inc(loaded_vm, 16)
            for dst, src in ((bq, d["bq_cols"]), (bk, d["bk_cols"]), (bv, d["bv_cols"])):
                sp.dma_start(dst[:], src).then_inc(loaded_vm, 16)
            sp.dma_start(bm[:], d["bm_rows"]).then_inc(loaded_vm, 16)

        @block.tensor
        def _(pe):
            pe.wait_ge(loaded_qk, 32)
            for a, b, bank in ((wk, wq, 0), (wv, wm, 4)):
                if bank:
                    pe.wait_ge(loaded_vm, 96)
                for e in range(T):
                    for o in range(T):
                        last = nc.tensor.matmul(psum[:, bank + e, :], a[:, o, e * P:(e + 1) * P], b[:, o, :],
                                                start=(o == 0), stop=(o == T - 1))
                    last.then_inc(product_done, 1)
            pe.wait_ge(product_copied, 2)
            for w, bias, col in ((wq, bk, 0), (wk, bq, T)):
                for e in range(T):
                    for o in range(T):
                        last = nc.tensor.matmul(psum[:, 0, col + e:col + e + 1], w[:, o, e * P:(e + 1) * P],
                                                bias[:, o:o + 1], start=(o == 0), stop=(o == T - 1))
            for o in range(T):
                last = nc.tensor.matmul(psum[:, 0, 2 * T:2 * T + 1], bk[:, o:o + 1].broadcast_to([P, P]),
                                        bq[:, o:o + 1], start=(o == 0), stop=(o == T - 1))
            last.then_inc(product_done, 1)
            for o in range(T):
                last = nc.tensor.matmul(psum[:, 1, :], bv[:, o:o + 1].broadcast_to([P, P]), wm[:, o, :],
                                        start=(o == 0), stop=(o == T - 1))
            last.then_inc(product_done, 1)

        @block.vector
        def _(dve):
            for n, dst in enumerate([keep["wqk"][:, e, :] for e in range(T)] + [keep["wvm"][:, e, :] for e in range(T)]):
                dve.wait_ge(product_done, n + 1)
                nc.vector.tensor_copy(dst, psum[:, n, :]).then_inc(product_copied, 1)
            dve.wait_ge(product_done, 2 * T + 1)
            nc.vector.tensor_copy(keep["bias_cols"][:], psum[:, 0, 0:2 * T + 1]).then_inc(product_copied, 1)
            dve.wait_ge(product_done, 2 * T + 2)
            nc.vector.tensor_tensor(keep["bvm"][:], psum[:, 1, :], bm[:], ALU.add).then_inc(product_copied, 1)


def keys_and_values(nc, sems, d, keep, psum, g, v, c_all, ht_dram):
    T, B = 4, 8
    wqk, wvm, gk = keep["wqk"], keep["wvm"], keep["bias_cols"]
    with ExitStack() as ctx:
        def sb(name, shape, dt=F32):
            return ctx.enter_context(nc.sbuf_tensor(name, shape, dt))

        def sem(name):
            return sems.new((name))

        key_t = sb("key_t", [P, 2, T, 512])
        value_t = sb("value_t", [P, 2, T, 512])
        v_sum = sb("v_sum", [P, 2, 512])
        x_tile = sb("x_tile0", [P, 2, 512])
        h_stage = sb("h_stage", [P, 2, 2, T, 256], F16)
        stats, sums, scale = sb("stats0", [P, 6]), sb("sums0", [P, 4]), sb("scale0", [P, 2])
        ident = sb("ident0", [P, P])
        key_in, value_in, x_in, stage_stored = ([sem(f"{n}{i}") for i in range(2)] for n in ("key_in", "value_in", "x_in", "stage_stored"))
        ident_in, exponent_in = sem("ident_in0"), sem("exponent_in0")
        tile_done, bank_free = sem("tile_done"), sem("bank_free")
        c_done, c_free = sem("c_done"), sem("c_free")
        g_high_done, v_high_done, v_sum_free = (sem(n) for n in ("g_high", "v_high", "v_sum_free"))
        stats_done, sums_done, rstd_done, norm_done, h_done = (sem(n) for n in ( "stats_s0", "sums_s0", "rstd0", "norm0", "h0"))
        turned, high_done, low_done = (sem(n) for n in ("turned0", "high0", "low0"))
        block = ctx.enter_context(nc.Block())

        kv = d["keyT"].rearrange("(t p) m -> p t m", p=P)
        vv = d["valueT"].rearrange("(t p) m -> p t m", p=P)
        xv = d["x"].rearrange("(n p) k -> n p k", p=P)

        @block.sync
        def _(sp):
            def load_block(m, half):
                sp.dma_start(key_t[:, half], kv[:, :, bass.ds(m * 512, 512)]).then_inc(key_in[half], 16)
                sp.dma_start(value_t[:, half], vv[:, :, bass.ds(m * 512, 512)]).then_inc(value_in[half], 16)

            def next_x(m, n):
                sp.wait_ge(turned, m * 4 + n + 1)
                sp.dma_start(x_tile[:, n % 2], xv[m * 4 + n + 2]).then_inc(x_in[n % 2], 16)

            def store_h(m, pair):
                wait_alone(sp, low_done, 2 + m * 4 + pair * 2 + 2, sems.sp)
                sp.dma_start(ht_dram[m * 2 + pair], h_stage[:, pair].rearrange("p a t i -> p (a t i)")).then_inc(stage_stored[pair], 16)

            for pair in range(2):
                sp.sem_inc(stage_stored[pair], 16)
            sp.dma_start(ident[:], d["ident"]).then_inc(ident_in, 16)
            for half in range(2):
                sp.dma_start(x_tile[:, half], xv[half]).then_inc(x_in[half], 16)
                load_block(half, half)
            with sp.Fori(0, B // 2 - 1) as it:
                for half in range(2):
                    for n in range(4):
                        next_x(it * 2 + half, n)
                        if n % 2:
                            store_h(it * 2 + half, n // 2)
                    load_block(it * 2 + half + 2, half)
            for n in range(4):
                next_x(B - 2, n)
                if n % 2:
                    store_h(B - 2, n // 2)
            for n in range(2):
                next_x(B - 1, n)
            for pair in range(2):
                store_h(B - 1, pair)
                sp.wait_ge(stage_stored[pair], 16 + 16 * B)

        @block.tensor
        def _(pe):
            pe.wait_ge(ident_in, 16)
            with pe.Fori(0, B // 2) as it:
                for half in range(2):
                    m = it * 2 + half
                    pe.wait_ge(key_in[half], it * 16 + 16)
                    pe.wait_ge(value_in[half], it * 16 + 16)
                    for q in range(2 * T):
                        n = q % T
                        pe.wait_ge(bank_free, m * 8 + q + 1)
                        for e in range(T):
                            if q < T:
                                a, b = wqk[:, e, n * P:(n + 1) * P], key_t[:, half, e, :]
                            else:
                                a, b = value_t[:, half, e, n * P:(n + 1) * P], wvm[:, e, :]
                            last = nc.tensor.matmul(psum[:, n, :], a, b, start=(e == 0), stop=(e == T - 1))
                        last.then_inc(tile_done, 1)
                        if q == T - 1:
                            pe.wait_ge(c_free, m + 1)
                            for s in range(T):
                                for e in range(T):
                                    last = nc.tensor.matmul(psum[:, 4 + half, s:s + 1], key_t[:, half, e, s * P:(s + 1) * P],
                                                            gk[:, T + e:T + e + 1], start=(e == 0), stop=(e == T - 1))
                            last.then_inc(c_done, 1)
                        if q % 2:
                            n = q // 2
                            pe.wait_ge(h_done, 1 + m * 4 + n + 1)
                            pe.wait_ge(low_done, m * 4 + n + 1)
                            for t in range(T):
                                last = nc.tensor.transpose(psum[:, 6 + n % 2, t * P:(t + 1) * P],
                                                           x_tile[:, n % 2, t * P:(t + 1) * P], ident[:])
                            last.then_inc(turned, 1)

        @block.scalar
        def _(act):
            act.sem_inc(h_done, 1)
            with act.Fori(0, B // 2) as it:
                for half in range(2):
                    m = it * 2 + half
                    for n in range(4):
                        row_relu_norm(nc, act, x_tile[:, n % 2], scale, m * 4 + n, norm_done, h_done)
                        for q in (2 * n, 2 * n + 1):
                            if q < T:
                                wait_alone(act, tile_done, m * 8 + q + 1, sems.act)
                                nc.scalar.activation(g[:, 0, q, bass.ds(m * 512, 512)], psum[:, q, :], ACT.Identity,
                                                     bias=gk[:, q:q + 1]).then_inc(g_high_done, 1)
                            else:
                                wait_alone(act, bank_free, T + m * 8 + q + 1, sems.act)
                                nc.scalar.copy(v[:, 0, m * 4 + q - T, :], v_sum[:, q % 2]).then_inc(v_high_done, 1)
                        act.wait_ge(turned, m * 4 + n + 1)
                        if n % 2 == 0:
                            act.wait_ge(stage_stored[n // 2], m * 16 + 16)
                        nc.scalar.copy(h_stage[:, n // 2, 0, :, (n % 2) * P:(n % 2 + 1) * P],
                                       psum[:, 6 + n % 2, :].rearrange("p (t i) -> p t i", t=T)).then_inc(high_done, 1)

        @block.vector
        def _(dve):
            dve.sem_inc(bank_free, T)
            dve.sem_inc(c_free, 2)
            dve.sem_inc(low_done, 2)
            with dve.Fori(0, B // 2) as it:
                for half in range(2):
                    m = it * 2 + half
                    for n in range(4):
                        dve.wait_ge(x_in[n % 2], (m * 2 + n // 2) * 16 + 16)
                        row_norm(nc, dve, x_tile[:, n % 2], stats, sums, scale, m * 4 + n, sems.dve, stats_done, sums_done, rstd_done, norm_done)
                        for q in (2 * n, 2 * n + 1):
                            if q < T:
                                dve.wait_ge(g_high_done, m * 4 + q + 1)
                                cols = bass.ds(m * 512, 512)
                                nc.vector.scalar_tensor_tensor(out=g[:, 1, q, cols], in0=psum[:, q, :], scalar=gk[:, q:q + 1],
                                                               in1=g[:, 0, q, cols], op0=ALU.add, op1=ALU.subtract
                                                               ).then_inc(bank_free, 1)
                            else:
                                dve.wait_ge(tile_done, m * 8 + q + 1)
                                dve.wait_ge(v_sum_free, m * 4 + q - T + 1)
                                nc.vector.tensor_tensor(v_sum[:, q % 2], psum[:, q - T, :], keep["bvm"][:],
                                                        ALU.add).then_inc(bank_free, 1)
                            if q == T:
                                dve.wait_ge(c_done, m + 1)
                                nc.vector.tensor_scalar(c_all[:, bass.ds(m * 4, 4)], psum[:, 4 + half, 0:T],
                                                        gk[:, 2 * T:2 * T + 1], None, ALU.add).then_inc(c_free, 1)
                        dve.wait_ge(high_done, m * 4 + n + 1)
                        nc.vector.tensor_tensor(h_stage[:, n // 2, 1, :, (n % 2) * P:(n % 2 + 1) * P],
                                                psum[:, 6 + n % 2, :].rearrange("p (t i) -> p t i", t=T),
                                                h_stage[:, n // 2, 0, :, (n % 2) * P:(n % 2 + 1) * P],
                                                ALU.subtract).then_inc(low_done, 1)

        @block.gpsimd
        def _(pool):
            nc.gpsimd.memset(sums[:, 3:4], -0.5).then_inc(exponent_in, 1)
            pool.wait_ge(exponent_in, 1)
            pool.sem_inc(v_sum_free, 2)
            with pool.Fori(0, B // 2) as it:
                for half in range(2):
                    m = it * 2 + half
                    for n in range(4):
                        row_rstd(nc, pool, sums, scale, m * 4 + n, sums_done, h_done, rstd_done)
                        if n >= 2:
                            for q in (2 * n - T, 2 * n - T + 1):
                                pool.wait_ge(v_high_done, m * 4 + q + 1)
                                nc.gpsimd.tensor_tensor(v[:, 1, m * 4 + q, :], v_sum[:, q % 2], v[:, 0, m * 4 + q, :],
                                                        ALU.subtract).then_inc(v_sum_free, 1)


NODES = 4096
QB = 256
MASKED = -1e9


def attention(nc, sems, d, psum, g, v, c_all, ht_dram, x1_dram, edge_dram):
    T, JP, BLOCKS = 4, 16, NODES // QB
    SCALE, MARK = 64.0, 2.0 ** 80
    with ExitStack() as ctx:
        def sb(name, shape, dt=F32):
            return ctx.enter_context(nc.sbuf_tensor(name, shape, dt))

        def sem(name):
            return sems.new((name))

        strip = sb("strip", [P, 2 * JP, QB])
        prob = sb("prob", [P, 2, 2 * JP, QB], F16)
        h_t = sb("h_t", [P, 2, T, QB], F16)
        adj = sb("adj", [P, 2, 2, QB])
        least = sb("least", [P, 2, QB])
        weight = sb("weight", [P, 2, QB])
        mark = sb("mark", [P, 2, QB], BF16)
        bound = sb("bound", [P, 1])
        res = sb("res", [P, 512])
        ones = sb("ones", [P, 1], F16)
        total, inv = sb("total", [P, 2]), sb("inv", [P, 2])
        h_in, res_in, ones_in, stored, narrowed = (sem(n) for n in ("h_in", "res_in", "ones_in", "stored1", "narrowed"))
        adj_in = [sem(f"adj_in{i}") for i in range(2)]
        scored, score_free = sem("scored"), sem("score_free")
        abs_done, mark_done, pair_done, least_done, least_clear, bound_in = (sem(n) for n in ("abs_s", "mark_s", "pair_s", "least_s", "least_clear", "bound_in"))
        halves_done, top_row, shifted, high_done, weight_done, low_done = (sem(n) for n in ("halves", "top_row", "shifted", "high1", "weight_s", "low1"))
        prob_used, total_done, inv_done, res_done = (sem(n) for n in ("prob_used", "total_done", "inv_done", "res_done"))
        block = ctx.enter_context(nc.Block())
        adj_v = d["adjT"].rearrange("(k a p) i -> k p a i", p=P, a=2)
        xv = d["x"].rearrange("(n p) k -> n p k", p=P)
        x1v = x1_dram.rearrange("(n p) k -> n p k", p=P)


        @block.sync
        def _(sp):
            def load_adj(b, k, par):
                sp.wait_ge(score_free, (b * JP + k) + 1)
                sp.dma_start(adj[:, par], adj_v[k, :, :, bass.ds(b * QB, QB)]).then_inc(adj_in[par], 16)

            def load_block(b):
                with sp.Fori(0, JP // 2) as kk:
                    for par in range(2):
                        load_adj(b, kk * 2 + par, par)

            sp.dma_start(h_t[:].rearrange("p a t i -> p (a t i)"), ht_dram[0]).then_inc(h_in, 16)
            load_block(0)
            with sp.Fori(1, BLOCKS) as b:
                sp.wait_ge(scored, b * JP)
                sp.dma_start(h_t[:].rearrange("p a t i -> p (a t i)"), ht_dram[b]).then_inc(h_in, 16)
                load_block(b)

        @block.tensor
        def _(pe):
            def scores(b):
                wait_alone(pe, h_in, b * 16 + 16, sems.pe)
                with pe.Fori(0, JP // 2) as kk:
                    for par in range(2):
                        pe.wait_ge(score_free, (b * JP + kk * 2 + par) + 1)
                        for a in range(2):
                            jt = kk * 4 + par * 2 + a
                            first = True
                            for t in range(T):
                                key = [g[:, hl, t, bass.ds(jt * P, P)] for hl in range(2)]
                                for kh, hh in ((0, 0), (0, 1), (1, 0)):
                                    last = nc.tensor.matmul(psum[:, par, a * QB:(a + 1) * QB], key[kh], h_t[:, hh, t, :],
                                                            start=first, stop=(t == T - 1 and kh == 1))
                                    first = False
                        last.then_inc(scored, 1)

            def outputs(b):
                pe.wait_ge(res_done, 1 + b * 2)

                def key_tile(jt, start, stop):
                    for s in range(2):
                        high = prob[:, 0, jt, s * P:(s + 1) * P]
                        low = prob[:, 1, jt, s * P:(s + 1) * P]
                        nc.tensor.matmul(psum[:, 2 + s, :], high, v[:, 0, jt, :], start=start, stop=False)
                        nc.tensor.matmul(psum[:, 2 + s, :], high, v[:, 1, jt, :], start=False, stop=False)
                        nc.tensor.matmul(psum[:, 4 + s, 0:1], high, ones[:], start=start, stop=False)
                        nc.tensor.matmul(psum[:, 2 + s, :], low, v[:, 0, jt, :], start=False, stop=stop)
                        last = nc.tensor.matmul(psum[:, 4 + s, 0:1], low, ones[:], start=False, stop=stop)
                    return last

                pe.wait_ge(low_done, 1 + b * JP + 1)
                key_tile(0, True, False)
                key_tile(1, False, False).then_inc(prob_used, 1)
                with pe.Fori(1, JP - 1) as k:
                    pe.wait_ge(low_done, 1 + b * JP + k + 1)
                    key_tile(k * 2, False, False)
                    key_tile(k * 2 + 1, False, False).then_inc(prob_used, 1)
                pe.wait_ge(low_done, 1 + b * JP + JP)
                key_tile(2 * JP - 2, False, False)
                key_tile(2 * JP - 1, False, True).then_inc(prob_used, 1)

            pe.wait_ge(ones_in, 1)
            scores(0)
            with pe.Fori(1, BLOCKS) as b:
                scores(b)
                outputs(b - 1)
            outputs(BLOCKS - 1)

        @block.vector
        def _(dve):
            dve.sem_inc(score_free, 2)
            for done in (pair_done, low_done, res_done):
                dve.sem_inc(done, 1)
            nc.vector.memset(bound[:], MARK * SCALE * 1e-5).then_inc(bound_in, 1)
            nc.vector.memset(ones[:], 1.0).then_inc(ones_in, 1)

            def product(b, k, par, kk=0):
                n = b * JP + k
                dve.wait_ge(scored, n + 1)
                dve.wait_ge(adj_in[par], (b * (JP // 2) + kk) * 16 + 16)
                for a in range(2):
                    ins = nc.vector.scalar_tensor_tensor(
                        out=strip[:, k * 2 + a, :], in0=psum[:, par, a * QB:(a + 1) * QB],
                        scalar=c_all[:, bass.ds(k * 2 + a, 1)], in1=adj[:, par, a, :], op0=ALU.add, op1=ALU.mult)
                ins.then_inc(score_free, 1)

            def negate(b, k):
                n = b * JP + k
                t = strip[:, bass.ds(k * 2, 2), :]
                dve.wait_ge(mark_done, 1 + n + 1)
                nc.vector.scalar_tensor_tensor(out=t, in0=mark[:], scalar=-MASKED * SCALE, in1=t,
                                               op0=ALU.min, op1=ALU.subtract).then_inc(pair_done, 1)
                dve.wait_ge(pair_done, 1 + n + 1)
                nc.vector.tensor_tensor(least[:], least[:], t, ALU.min).then_inc(least_done, 1)

            def mask_scores(b, ended):
                nc.vector.memset(least[:], 3.0e38).then_inc(least_clear, 1)
                wait_alone(dve, least_clear, b + 1, sems.dve)
                product(b, 0, 0)

                def pairs(k0, k1):
                    with dve.Fori(k0, k1) as kk:
                        product(b, kk * 2 + 1, 1, kk)
                        negate(b, kk * 2)
                        product(b, kk * 2 + 2, 0, kk + 1)
                        negate(b, kk * 2 + 1)

                if ended is None:
                    pairs(0, JP // 2 - 1)
                else:
                    pairs(0, 2)
                    finish(ended, 0)
                    pairs(2, 6)
                    finish(ended, 1)
                    pairs(6, JP // 2 - 1)
                product(b, JP - 1, 1, JP // 2 - 1)
                negate(b, JP - 2)
                negate(b, JP - 1)
                dve.wait_ge(least_done, b * JP + JP)
                nc.vector.scalar_tensor_tensor(out=least[:, 0, :], in0=least[:, 0, :], scalar=1.0, in1=least[:, 1, :],
                                               op0=ALU.mult, op1=ALU.min).then_inc(halves_done, 1)
                dve.wait_ge(halves_done, b * 2 + 1)
                nc.vector.tensor_scalar(least[:, 0, :], least[:, 0, :], -1.0, None, ALU.mult).then_inc(halves_done, 1)

            def probabilities(b):
                wait_alone(dve, top_row, b + 1, sems.dve)

                def shift(k):
                    t = strip[:, bass.ds(k * 2, 2), :]
                    nc.vector.tensor_tensor(t, t, least[:, 1:2, :].broadcast_to([P, 2, QB]), ALU.add).then_inc(shifted, 1)

                def low(k):
                    dve.wait_ge(weight_done, b * JP + k + 1)
                    nc.vector.tensor_tensor(prob[:, 1, bass.ds(k * 2, 2), :], weight[:], prob[:, 0, bass.ds(k * 2, 2), :],
                                            ALU.subtract).then_inc(low_done, 1)

                shift(0)
                with dve.Fori(0, JP - 1) as k:
                    shift(k + 1)
                    low(k)
                low(JP - 1)

            def finish(b, s):
                if s == 0:
                    dve.wait_ge(prob_used, b * JP + JP)
                    for i in range(2):
                        ins = nc.vector.tensor_copy(total[:, i:i + 1], psum[:, 4 + i, 0:1])
                    ins.then_inc(total_done, 1)
                    dve.wait_ge(total_done, b + 1)
                    nc.vector.reciprocal(inv[:], total[:]).then_inc(inv_done, 1)
                    dve.wait_ge(inv_done, b + 1)
                dve.wait_ge(res_in, (b * 2 + s) * 16 + 16)
                nc.vector.scalar_tensor_tensor(out=res[:], in0=psum[:, 2 + s, :], scalar=inv[:, s:s + 1], in1=res[:],
                                               op0=ALU.mult, op1=ALU.add).then_inc(res_done, 1)

            mask_scores(0, None)
            probabilities(0)
            mask_scores(1, None)
            probabilities(1)
            with dve.Fori(2, BLOCKS) as b:
                mask_scores(b, b - 2)
                probabilities(b)
            for b in (BLOCKS - 2, BLOCKS - 1):
                for s in range(2):
                    finish(b, s)

        @block.scalar
        def _(act):
            def marks(b):
                with act.Fori(0, JP) as k:
                    n = b * JP + k
                    act.wait_ge(mark_done, 1 + n)
                    wait_alone(act, score_free, 2 + n + 1, sems.act)
                    nc.scalar.activation(weight[:], strip[:, bass.ds(k * 2, 2), :], ACT.Abs).then_inc(abs_done, 1)
                    act.wait_ge(abs_done, n + 1)
                    act.wait_ge(pair_done, 1 + n)
                    nc.scalar.activation(mark[:], weight[:], ACT.Relu, scale=-MARK, bias=bound[:, 0:1]).then_inc(mark_done, 1)

            def exps(b):
                with act.Fori(0, JP) as k:
                    n = b * JP + k
                    t = strip[:, bass.ds(k * 2, 2), :]
                    wait_alone(act, shifted, n + 1, sems.act)
                    if b is not FIRST:
                        wait_alone(act, prob_used, (b - 1) * JP + k + 1, sems.act)
                    nc.scalar.activation(prob[:, 0, bass.ds(k * 2, 2), :], t, ACT.Exp, scale=-1.0 / SCALE).then_inc(high_done, 1)
                    wait_alone(act, low_done, 1 + n, sems.act)
                    nc.scalar.activation(weight[:], t, ACT.Exp, scale=-1.0 / SCALE).then_inc(weight_done, 1)

            FIRST = 0
            act.sem_inc(mark_done, 1)
            act.wait_ge(bound_in, 1)
            marks(FIRST)
            exps(FIRST)
            with act.Fori(1, BLOCKS) as b:
                marks(b)
                exps(b)

        @block.gpsimd
        def _(pool):
            def top_of(b):
                wait_alone(pool, halves_done, b * 2 + 2, sems.pool)
                nc.gpsimd.partition_all_reduce(least[:, 1, :], least[:, 0, :], P, RMAX).then_inc(top_row, 1)

            def move_rows(b):
                for s in range(2):
                    n = b * 2 + s
                    pool.dma_start(res[:], xv[n]).then_inc(res_in, 16)
                    wait_alone(pool, res_done, 1 + n + 1, sems.pool)
                    pool.dma_start(x1v[n], res[:]).then_inc(stored, 16)
                    wait_alone(pool, stored, n * 16 + 16, sems.pool)

            def narrow_edges(b):
                for n in range(2):
                    rows = bass.ds((b * 2 + n) * P, P)
                    pool.dma_start(edge_dram[rows, :], d["adjT"][rows, :]).then_inc(narrowed, 16)

            narrow_edges(0)
            top_of(0)
            narrow_edges(1)
            top_of(1)
            with pool.Fori(2, BLOCKS) as b:
                move_rows(b - 2)
                narrow_edges(b)
                top_of(b)
            for b in (BLOCKS - 2, BLOCKS - 1):
                move_rows(b)
            pool.wait_ge(narrowed, 2 * BLOCKS * 16)


HEADS, HD = 8, 64
SLOPE = 0.2
GATE = 2.0 ** 60
UP = 64.0


def head_features(nc, sems, d, psum, x1_dram, wh_dram, srow_dram, node):
    T, TILES = 4, NODES // P
    WIDE = 512 + 2 * HEADS
    with ExitStack() as ctx:
        def sb(name, shape, dt=F32):
            return ctx.enter_context(nc.sbuf_tensor(name, shape, dt))

        def sem(name):
            return sems.new((name))

        w_all = sb("w_all", [P, T, WIDE])
        w_half = sb("w_half", [P, 2, T, WIDE], F16)
        a_rows = sb("a_rows", [P, 2, 512])
        w_a = sb("w_a", [P, 512])
        ident = sb("ident2", [P, P])
        x_tile = sb("x_tile2", [P, 2, 512])
        h_t = sb("h_t2", [P, 2, 2, T, 512], F16)
        wh_tile = sb("wh_tile", [P, 2, 512])
        wh_sum = sb("wh_sum", [P, 512])
        mean_w = sb("mean_w", [P, P])
        s_row = sb("s_row2", [HEADS, NODES])
        sd = sb("sd", [P, TILES, 2 * HEADS])
        stats, sums, scale = sb("stats2", [P, 6]), sb("sums2", [P, 4]), sb("scale2", [P, 2])
        d_top, z = sb("d_top", [P, 2, HEADS]), sb("z", [P, 4, TILES, HEADS])
        x_in = [sem(f"x_in2{i}") for i in range(2)]
        wh_stored = [sem(f"wh_stored{i}") for i in range(2)]
        weights_in, ready, exponent_in, zeroed = sem("weights_in2"), sem("ready2"), sem("exponent_in2"), sem("zeroed2")
        wa_step, halves_done = sem("wa_step"), sem("halves2")
        stats_done, sums_done, rstd_done, norm_done, h_done = (sem(n) for n in ("stats_s2", "sums_s2", "rstd2", "norm2", "h2"))
        turned, high_done, low_done = (sem(n) for n in ("turned2", "high2", "low2"))
        feature_done, wh_copied, sd_copied, added = (sem(n) for n in ("feature_done", "wh_copied", "sd_copied", "added"))
        rows_done, rows_copied, rows_stored, mean_done, mean_copied = (sem(n) for n in ("rows_done", "rows_copied", "rows_stored", "mean_done", "mean_copied"))
        factor_step, exp_ready, exp_done = sem("factor_step"), sem("exp_ready"), sem("exp_done")
        block = ctx.enter_context(nc.Block())
        xv = x1_dram.rearrange("(n p) k -> n p k", p=P)
        whv = wh_dram.rearrange("(n p) k -> n p k", p=P)

        @block.sync
        def _(sp):
            sp.dma_start(w_all[:, :, 0:512], d["W_heads"].rearrange("(t p) n -> p t n", p=P)).then_inc(weights_in, 16)
            sp.dma_start(a_rows[:, 0], d["a1_rows"]).then_inc(weights_in, 16)
            sp.dma_start(a_rows[:, 1], d["a2_rows"]).then_inc(weights_in, 16)
            sp.dma_start(ident[:], d["ident"]).then_inc(weights_in, 16)
            for n in range(2):
                sp.dma_start(x_tile[:, n], xv[n]).then_inc(x_in[n], 16)
            with sp.Fori(0, TILES // 2 - 1) as it:
                for par in range(2):
                    n = it * 2 + par
                    sp.wait_ge(turned, n + 1)
                    sp.dma_start(x_tile[:, par], xv[n + 2]).then_inc(x_in[par], 16)
            sp.wait_ge(rows_copied, TILES // T)
            sp.dma_start(srow_dram, s_row[:]).then_inc(rows_stored, 16)
            sp.wait_ge(rows_stored, 16)

        @block.gpsimd
        def _(pool):
            nc.gpsimd.memset(sums[:, 3:4], -0.5).then_inc(exponent_in, 1)
            nc.gpsimd.memset(wh_sum[:], 0.0).then_inc(zeroed, 1)
            pool.sem_inc(added, 1)
            pool.wait_ge(zeroed, 1)
            pool.wait_ge(exponent_in, 1)

            def store(n, par):
                wait_alone(pool, wh_copied, n + 1, sems.pool)
                pool.dma_start(whv[n], wh_tile[:, par]).then_inc(wh_stored[par], 16)
                pool.wait_ge(added, 1 + n)
                nc.gpsimd.tensor_tensor(wh_sum[:], wh_sum[:], wh_tile[:, par], ALU.add).then_inc(added, 1)

            for n in range(2):
                row_rstd(nc, pool, sums, scale, n, sums_done, h_done, rstd_done)
            with pool.Fori(0, TILES // 2 - 1) as it:
                for par in range(2):
                    row_rstd(nc, pool, sums, scale, it * 2 + par + 2, sums_done, h_done, rstd_done)
                    store(it * 2 + par, par)
            for n in range(TILES - 2, TILES):
                store(n, n % 2)
            for par in range(2):
                pool.wait_ge(wh_stored[par], 16 * (TILES // 2))
            pool.wait_ge(factor_step, 1)
            nc.gpsimd.partition_all_reduce(d_top[:, 1], d_top[:, 0], P, RMAX).then_inc(factor_step, 1)

        @block.tensor
        def _(pe):
            pe.wait_ge(weights_in, 64)
            pe.wait_ge(halves_done, 4)

            def turn(q, par):
                pe.wait_ge(h_done, 1 + q + 1)
                pe.wait_ge(low_done, q + 1)
                for t in range(T):
                    last = nc.tensor.transpose(psum[:, 6 + par, t * P:(t + 1) * P], x_tile[:, par, t * P:(t + 1) * P], ident[:])
                last.then_inc(turned, 1)

            def products(out, stationary, moving):
                for t in range(T):
                    for a, b in ((0, 0), (0, 1), (1, 0)):
                        last = nc.tensor.matmul(out, stationary(a, t), moving(b, t), start=(t == 0 and a + b == 0),
                                                stop=(t == T - 1 and a == 1))
                return last

            def four_tiles(m, half, last_block):
                for n in range(T):
                    q = m * T + n
                    if not (last_block and n == T - 1):
                        turn(q + 1, (n + 1) % 2)
                    pe.wait_ge(low_done, 2 + q + 1)
                    pe.wait_ge(sd_copied, q + 1)
                    pe.wait_ge(wh_copied, q - 1 if not isinstance(m, int) or q else 0)
                    mine = lambda a, t: h_t[:, half, a, t, n * P:(n + 1) * P]
                    products(psum[:, n % 2, :], mine, lambda b, t: w_half[:, b, t, 0:512])
                    products(psum[:, 2 + n % 2, 0:2 * HEADS], mine, lambda b, t: w_half[:, b, t, 512:WIDE]).then_inc(feature_done, 1)
                pe.wait_ge(rows_copied, m)
                products(psum[0:HEADS, 4, :], lambda a, t: w_half[:, a, t, 512:512 + HEADS],
                         lambda b, t: h_t[:, half, b, t, :]).then_inc(rows_done, 1)

            pe.sem_inc(rows_done, 1)
            turn(0, 0)
            four_tiles(0, 0, False)
            with pe.Fori(0, TILES // T // 2 - 1) as it:
                four_tiles(it * 2 + 1, 1, False)
                four_tiles(it * 2 + 2, 0, False)
            four_tiles(TILES // T - 1, 1, True)
            pe.wait_ge(added, 1 + TILES)
            pe.wait_ge(rows_copied, TILES // T)
            nc.tensor.matmul(psum[:, 4, :], mean_w[:], wh_sum[:], start=True, stop=True).then_inc(mean_done, 1)

        @block.scalar
        def _(act):
            act.sem_inc(h_done, 1)

            def tile(m, n, half):
                q = m * T + n
                row_relu_norm(nc, act, x_tile[:, n % 2], scale, q, norm_done, h_done)
                act.wait_ge(rows_done, m)
                act.wait_ge(turned, q + 1)
                nc.scalar.copy(h_t[:, half, 0, :, n * P:(n + 1) * P],
                               psum[:, 6 + n % 2, :].rearrange("p (t i) -> p t i", t=T)).then_inc(high_done, 1)

            def feature(q, par, n_stored):
                act.wait_ge(feature_done, q + 1)
                act.wait_ge(added, q if not isinstance(q, int) or q else 0)
                act.wait_ge(wh_stored[par], n_stored * 16)
                nc.scalar.activation(wh_tile[:, par], psum[:, par, :], ACT.Copy, scale=1.0 / UP).then_inc(wh_copied, 1)

            for n in range(2):
                tile(0, n, 0)
            for n in range(2, T):
                feature(n - 2, n % 2, 0)
                tile(0, n, 0)

            def block_of(m, half):
                for n in range(T):
                    feature(m * T + n - 2, n % 2, (m * T + n - 2) // 2 if isinstance(m, int) else m * 2 + n // 2 - 1)
                    tile(m, n, half)

            with act.Fori(0, TILES // T // 2 - 1) as it:
                block_of(it * 2 + 1, 1)
                block_of(it * 2 + 2, 0)
            block_of(TILES // T - 1, 1)
            for n in range(TILES - 2, TILES):
                feature(n, n % 2, n // 2)
            act.wait_ge(exp_ready, 1)
            for k, (src, mult) in enumerate(((0, 1.0), (0, SLOPE), (1, 1.0), (2, 1.0))):
                dst = node["factor_j"] if k < 2 else node["factor_i"]
                nc.scalar.activation(dst[:, :, :, k % 2], z[:, src], ACT.Exp, scale=mult).then_inc(exp_done, 1)
            act.wait_ge(exp_done, 4)

        @block.vector
        def _(dve):
            dve.sem_inc(low_done, 2)
            dve.sem_inc(sd_copied, 2)
            nc.vector.memset(mean_w[:], 1.0 / NODES).then_inc(ready, 1)
            dve.wait_ge(weights_in, 64)
            for n in range(2 * T):
                t, k = n // 2, n % 2
                dve.wait_ge(wa_step, 2 * n)
                nc.vector.tensor_tensor(w_a[:], w_all[:, t, 0:512], a_rows[:, k], ALU.mult).then_inc(wa_step, 1)
                dve.wait_ge(wa_step, 2 * n + 1)
                nc.vector.tensor_reduce(w_all[:, t, 512 + k * HEADS:512 + (k + 1) * HEADS],
                                        w_a[:].rearrange("p (h k) -> p h k", h=HEADS), AX, ALU.add).then_inc(wa_step, 1)
            dve.wait_ge(wa_step, 4 * T)
            for t in range(0, T, 2):
                nc.vector.tensor_scalar(w_half[:, 0, t:t + 2, :], w_all[:, t:t + 2, :], UP, None, ALU.mult).then_inc(halves_done, 1)
            dve.wait_ge(halves_done, 2)
            for t in range(0, T, 2):
                nc.vector.scalar_tensor_tensor(out=w_half[:, 1, t:t + 2, :], in0=w_all[:, t:t + 2, :], scalar=UP,
                                               in1=w_half[:, 0, t:t + 2, :], op0=ALU.mult, op1=ALU.subtract).then_inc(halves_done, 1)

            def norm(q, par, n_in):
                dve.wait_ge(x_in[par], n_in * 16)
                row_norm(nc, dve, x_tile[:, par], stats, sums, scale, q, sems.dve, stats_done, sums_done, rstd_done, norm_done)

            def tile(m, n, half, norm_next):
                q = m * T + n
                if norm_next:
                    norm(q + 1, (n + 1) % 2, m * 2 + (n + 1) // 2 + 1)
                dve.wait_ge(high_done, q + 1)
                nc.vector.tensor_tensor(h_t[:, half, 1, :, n * P:(n + 1) * P],
                                        psum[:, 6 + n % 2, :].rearrange("p (t i) -> p t i", t=T),
                                        h_t[:, half, 0, :, n * P:(n + 1) * P], ALU.subtract).then_inc(low_done, 1)
                dve.wait_ge(feature_done, q + 1)
                nc.vector.tensor_scalar(sd[:, q:q + 1, :] if isinstance(q, int) else sd[:, bass.ds(q, 1), :],
                                        psum[:, 2 + n % 2, 0:2 * HEADS].rearrange("p (o n) -> p o n", o=1),
                                        1.0 / UP, None, ALU.mult).then_inc(sd_copied, 1)

            def rows(m):
                dve.wait_ge(rows_done, 1 + m + 1)
                nc.vector.tensor_scalar(s_row[:, bass.ds(m * 512, 512)], psum[0:HEADS, 4, :], 1.0 / UP, None,
                                        ALU.mult).then_inc(rows_copied, 1)

            norm(0, 0, 1)
            with dve.Fori(0, TILES // T // 2 - 1) as it:
                for half in range(2):
                    for n in range(T):
                        tile(it * 2 + half, n, half, True)
                    rows(it * 2 + half)
            for m in (TILES // T - 2, TILES // T - 1):
                for n in range(T):
                    tile(m, n, m % 2, m * T + n + 1 < TILES)
                rows(m)
            s_all, d_all = sd[:, :, 0:HEADS], sd[:, :, HEADS:2 * HEADS]
            dve.wait_ge(sd_copied, 2 + TILES)
            nc.vector.tensor_reduce(d_top[:, 0], d_all.rearrange("p n h -> p h n"), AX, ALU.max).then_inc(factor_step, 1)
            nc.vector.tensor_scalar(node["gate_d"][:], d_all, GATE, None, ALU.mult).then_inc(ready, 1)
            dve.wait_ge(factor_step, 2)
            top = d_top[:, 1:2, :].broadcast_to([P, TILES, HEADS])
            nc.vector.tensor_tensor(z[:, 0], d_all, top, ALU.subtract).then_inc(factor_step, 1)
            nc.vector.tensor_tensor(z[:, 1], s_all, top, ALU.add).then_inc(factor_step, 1)
            dve.wait_ge(factor_step, 4)
            nc.vector.tensor_scalar(z[:, 2], z[:, 1], SLOPE, None, ALU.mult).then_inc(factor_step, 1)
            dve.wait_ge(factor_step, 5)
            nc.vector.tensor_tensor(z[:, 3], z[:, 1], z[:, 2], ALU.max).then_inc(factor_step, 1)
            dve.wait_ge(factor_step, 6)
            for k in (1, 2):
                nc.vector.tensor_tensor(z[:, k], z[:, k], z[:, 3], ALU.subtract).then_inc(factor_step, 1)
            dve.wait_ge(factor_step, 8)
            dve.sem_inc(exp_ready, 1)
            dve.wait_ge(mean_done, 1)
            nc.vector.tensor_copy(node["mean"][:], psum[:, 4, :]).then_inc(mean_copied, 1)
            dve.wait_ge(mean_copied, 1)


GROUP = 4
PARTS, COLS = 3, HD + 1
HALF = PARTS * COLS


def split_features(nc, sems, psum, wh_dram, node, x_parts, gr):
    STEPS = NODES // P // 2
    with ExitStack() as ctx:
        def sb(name, shape, dt=F32):
            return ctx.enter_context(nc.sbuf_tensor(f"{name}_g{gr}", shape, dt))

        def sem(name):
            return sems.new((f"{name}_g{gr}"))

        wh = sb("wh", [P, 2, 2, GROUP, HD])
        f = sb("f", [P, 2, 2, GROUP, 2, COLS])
        rest = sb("rest", [P, 2, 2, GROUP, 2, COLS])
        wh_in = [sem(f"wh_in{i}") for i in range(2)]
        f_done, first_done, rest_done, second_done, third_done = (sem(n) for n in ("f", "first", "rest_s", "second", "third"))
        block = ctx.enter_context(nc.Block())
        whv = wh_dram.rearrange("(n j p) k -> n p j k", p=P, j=2)[:, :, :, gr * GROUP * HD:(gr + 1) * GROUP * HD]
        hs = slice(gr * GROUP, (gr + 1) * GROUP)

        def part(n, k):
            return x_parts[:, bass.ds(n * 2, 2), :, :, k, :].rearrange("p j h b c -> p (j h b) c")

        def flat(t, par):
            return t[:, par].rearrange("p j h b c -> p (j h b) c")

        @block.sync
        def _(sp):
            for n in range(2):
                sp.dma_start(wh[:, n].rearrange("p j h k -> p j (h k)"), whv[n]).then_inc(wh_in[n], 16)
            with sp.Fori(0, STEPS // 2 - 1) as it:
                for par in range(2):
                    n = it * 2 + par
                    wait_alone(sp, f_done, n * 4 + 4, sems.sp)
                    sp.dma_start(wh[:, par].rearrange("p j h k -> p j (h k)"), whv[n + 2]).then_inc(wh_in[par], 16)

        @block.gpsimd
        def _(pool):
            pool.sem_inc(rest_done, 2)
            with pool.Fori(0, STEPS // 2) as it:
                for par in range(2):
                    n = it * 2 + par
                    pool.wait_ge(wh_in[par], it * 16 + 16)
                    pool.wait_ge(rest_done, n + 1)
                    factor = node["factor_j"][:, bass.ds(n * 2, 2), hs, :]
                    for b in range(2):
                        nc.gpsimd.tensor_tensor(f[:, par, :, :, b, 0:HD], wh[:, par],
                                                factor[:, :, :, b:b + 1].broadcast_to([P, 2, GROUP, HD]), ALU.mult).then_inc(f_done, 1)
                    for j in range(2):
                        nc.gpsimd.tensor_copy(f[:, par, j, :, :, HD], factor[:, j]).then_inc(f_done, 1)

        @block.scalar
        def _(act):
            def first(n, par):
                wait_alone(act, f_done, n * 4 + 4, sems.act)
                nc.scalar.copy(part(n, 0), flat(f, par)).then_inc(first_done, 1)

            def second(n, par):
                wait_alone(act, rest_done, 2 + n + 1, sems.act)
                nc.scalar.copy(part(n, 1), flat(rest, par)).then_inc(second_done, 1)

            first(0, 0)
            with act.Fori(0, STEPS // 2 - 1) as it:
                for par in range(2):
                    first(it * 2 + par + 1, 1 - par)
                    second(it * 2 + par, par)
            first(STEPS - 1, 1)
            second(STEPS - 2, 0)
            second(STEPS - 1, 1)

        @block.vector
        def _(dve):
            dve.sem_inc(third_done, 2)

            def take_first(n, par):
                dve.wait_ge(first_done, n + 1)
                dve.wait_ge(third_done, n + 1)
                nc.vector.tensor_tensor(flat(rest, par), flat(f, par), part(n, 0), ALU.subtract).then_inc(rest_done, 1)

            def take_second(n, par):
                dve.wait_ge(second_done, n + 1)
                nc.vector.tensor_tensor(part(n, 2), flat(rest, par), part(n, 1), ALU.subtract).then_inc(third_done, 1)

            take_first(0, 0)
            with dve.Fori(0, STEPS // 2 - 1) as it:
                for par in range(2):
                    take_first(it * 2 + par + 1, 1 - par)
                    take_second(it * 2 + par, par)
            take_first(STEPS - 1, 1)
            take_second(STEPS - 2, 0)
            take_second(STEPS - 1, 1)


def graph_attention(nc, sems, psum, edge_dram, srow_dram, enc_dram, node, x_parts, gr):
    TILES, QW = NODES // P, 512
    BLOCKS, CHUNKS, SUBS = NODES // QW, TILES // 2, QW // P
    RING, PIECES = 4, 4
    with ExitStack() as ctx:
        def sb(name, shape, dt=F32):
            return ctx.enter_context(nc.sbuf_tensor(f"{name}_a{gr}", shape, dt))

        def sem(name):
            return sems.new((f"{name}_a{gr}"))

        edges = sb("edges", [P, TILES, QW], BF16)
        s_row = sb("s_row", [P, 2, QW])
        gate = sb("gate", [P, RING, 2, QW], BF16)
        cells = sb("cells", [P, RING, 2, 2, QW], BF16)
        raw = sb("raw", [P, SUBS, 2, PARTS, COLS])
        num = sb("num", [P, SUBS, 2, COLS])
        y = sb("y", [P, SUBS, COLS])
        none, safe, minus_one = (sb(n, [P, SUBS]) for n in ("none", "safe", "minus_one"))
        spare = sb("spare", [P, SUBS, HD])
        enc = sb("enc", [P, SUBS, GROUP, HD])
        edges_in = [sem(f"edges_in{i}") for i in range(PIECES)]
        s_in = [sem(f"s_in{i}") for i in range(2)]
        gate_done, above_done, cells_done, cells_used = (sem(n) for n in ("gate", "above", "cells", "cells_used"))
        head_done, copied, pool_step, enc_stored, constant_in = (sem(n) for n in ("head", "copied", "pool_step", "enc_stored", "constant_in"))
        block = ctx.enter_context(nc.Block())
        edge_v = edge_dram.rearrange("(n p) i -> p n i", p=P)
        enc_v = enc_dram.rearrange("(n s p) k -> n p s k", p=P, s=SUBS)[:, :, :, gr * GROUP * HD:(gr + 1) * GROUP * HD]
        STEPS = 11

        @block.sync
        def _(sp):
            def load(b, h):
                src = srow_dram[gr * GROUP + h:gr * GROUP + h + 1, bass.ds(b * QW, QW)]
                sp.dma_start(s_row[:, h % 2], src.broadcast_to([P, QW])).then_inc(s_in[h % 2], 16)

            def load_edges(b, p):
                tiles = slice(p * TILES // PIECES, (p + 1) * TILES // PIECES)
                sp.dma_start(edges[:, tiles, :], edge_v[:, tiles, bass.ds(b * QW, QW)]).then_inc(edges_in[p], 16)

            load(0, 0)
            load_edges(0, 0)
            load(0, 1)
            for p in range(1, PIECES):
                load_edges(0, p)
            with sp.Fori(0, BLOCKS - 1) as b:
                for h in range(GROUP):
                    if h == GROUP - 1:
                        for p in range(PIECES):
                            wait_alone(sp, cells_done, (b * GROUP + h) * CHUNKS + (p + 1) * RING, sems.sp)
                            load_edges(b + 1, p)
                    wait_alone(sp, gate_done, (b * GROUP + h + 1) * CHUNKS, sems.sp)
                    load(b + (h + 2) // GROUP, (h + 2) % GROUP)
            for h in range(GROUP - 2):
                wait_alone(sp, gate_done, ((BLOCKS - 1) * GROUP + h + 1) * CHUNKS, sems.sp)
                load(BLOCKS - 1, h + 2)

        @block.gpsimd
        def _(pool):
            def combine(b, h):
                u = b * GROUP + h
                base = u * STEPS

                def op(k, dst, a, c, f):
                    pool.wait_ge(pool_step, 1 + base + k)
                    nc.gpsimd.tensor_tensor(dst, a, c, f).then_inc(pool_step, 1)

                pool.wait_ge(copied, 2 + u + 1)
                raw_v = raw[:].rearrange("p s b k c -> p (s b) k c")
                num_v = num[:].rearrange("p s b c -> p (s b) c")
                op(0, num_v, raw_v[:, :, 0], raw_v[:, :, 1], ALU.add)
                op(1, num_v, num_v, raw_v[:, :, 2], ALU.add)
                f_i = node["factor_i"][:, bass.ds(b * SUBS, SUBS), gr * GROUP + h, :]
                op(2, num[:], num[:], f_i.rearrange("p s (b o) -> p s b o", o=1).broadcast_to([P, SUBS, 2, COLS]), ALU.mult)
                op(3, y[:], num[:, :, 0], num[:, :, 1], ALU.add)
                wait_alone(pool, pool_step, 1 + base + 4, sems.pool)
                nc.gpsimd.tensor_scalar(none[:], y[:, :, HD], 0.0, None, ALU.is_equal).then_inc(pool_step, 1)
                op(5, safe[:], y[:, :, HD], none[:], ALU.add)
                op(6, safe[:], safe[:], minus_one[:], ALU.pow)
                op(7, enc[:, :, h], y[:, :, 0:HD], safe[:].rearrange("p (s o) -> p s o", o=1).broadcast_to([P, SUBS, HD]), ALU.mult)
                mean = node["mean"][:, (gr * GROUP + h) * HD:(gr * GROUP + h + 1) * HD]
                op(8, spare[:], none[:].rearrange("p (s o) -> p s o", o=1).broadcast_to([P, SUBS, HD]),
                   mean.rearrange("p (o k) -> p o k", o=1).broadcast_to([P, SUBS, HD]), ALU.mult)
                op(9, enc[:, :, h], enc[:, :, h], spare[:], ALU.add)
                pool.wait_ge(pool_step, 1 + base + 10)
                pool.sem_inc(pool_step, 1)
                if h == GROUP - 1:
                    wait_alone(pool, pool_step, 1 + base + STEPS, sems.pool)
                    for s in range(SUBS):
                        src = enc[:, s].rearrange("p h k -> p (h k)")
                        dst = enc_v[b, :, s, :] if isinstance(b, int) else enc_v[bass.ds(b, 1), :, s, :].rearrange("o p k -> (o p) k")
                        pool.dma_start(dst, src).then_inc(enc_stored, 16)
                    wait_alone(pool, enc_stored, (b + 1) * SUBS * 16, sems.pool)

            pool.sem_inc(pool_step, 1)
            nc.gpsimd.memset(minus_one[:], -1.0).then_inc(constant_in, 1)
            pool.wait_ge(constant_in, 1)
            with pool.Fori(0, BLOCKS) as b:
                for h in range(GROUP):
                    combine(b, h)

        @block.scalar
        def _(act):
            act.sem_inc(copied, 2)

            def gates(b, h, p0, p1):
                with act.Fori(p0, p1) as p:
                    for c in range(RING):
                        n = (b * GROUP + h) * CHUNKS + p * RING + c
                        wait_alone(act, above_done, n + 1, sems.act)
                        for a in range(2):
                            ins = nc.scalar.activation(gate[:, c, a], s_row[:, h % 2], ACT.Sigmoid, scale=GATE,
                                                       bias=node["gate_d"][:, bass.ds((p * RING + c) * 2 + a, 1), gr * GROUP + h])
                        ins.then_inc(gate_done, 1)

            def copy_head(u, par):
                act.wait_ge(head_done, u + 1)
                act.wait_ge(pool_step, 1 + u * STEPS)
                nc.scalar.copy(raw[:].rearrange("p s b k c -> p s (b k c)"), psum[:, par * SUBS:(par + 1) * SUBS, 0:2 * HALF]).then_inc(copied, 1)

            def heads(b, first):
                for h in range(GROUP):
                    act.wait_ge(s_in[h % 2], (b * 2 + h // 2) * 16 + 16)
                    gates(b, h, 0, 1)
                    if not (first and h == 0):
                        copy_head(b * GROUP + h - 1, (h - 1) % 2)
                    gates(b, h, 1, PIECES)

            heads(0, True)
            with act.Fori(1, BLOCKS) as b:
                heads(b, False)
            copy_head(BLOCKS * GROUP - 1, 1)

        @block.vector
        def _(dve):
            dve.sem_inc(above_done, RING)
            dve.sem_inc(cells_used, RING)

            def above(n, c, pair):
                dve.wait_ge(gate_done, n + 1)
                dve.wait_ge(cells_used, n + 1)
                nc.vector.tensor_tensor(cells[:, c % RING, 0], gate[:, c % RING], pair, ALU.mult).then_inc(above_done, 1)

            def below(n, c, pair):
                dve.wait_ge(above_done, RING + n + 1)
                nc.vector.tensor_tensor(cells[:, c % RING, 1], pair, cells[:, c % RING, 0], ALU.subtract).then_inc(cells_done, 1)

            with dve.Fori(0, BLOCKS) as b:
                with dve.Fori(0, GROUP) as h:
                    for c in range(CHUNKS + 1):
                        if c < CHUNKS:
                            if c % RING == 0:
                                wait_alone(dve, edges_in[c // RING], (b + 1) * 16, sems.dve)
                            above((b * GROUP + h) * CHUNKS + c, c, edges[:, 2 * c:2 * c + 2, :])
                        if c:
                            below((b * GROUP + h) * CHUNKS + c - 1, c - 1, edges[:, 2 * c - 2:2 * c, :])

        @block.tensor
        def _(pe):
            def piece(b, hh, h, p):
                for c in range(RING):
                    n = (b * GROUP + hh * 2 + h) * CHUNKS + p * RING + c
                    pe.wait_ge(cells_done, n + 1)
                    begins = isinstance(p, int) and p == 0 and c == 0
                    ends = isinstance(p, int) and p == PIECES - 1 and c == RING - 1
                    for a in range(2):
                        for s in range(SUBS):
                            for k in range(2):
                                moving = x_parts[:, bass.ds((p * RING + c) * 2 + a, 1), bass.ds(hh * 2 + h, 1), k]
                                last = nc.tensor.matmul(psum[:, h * SUBS + s, k * HALF:(k + 1) * HALF],
                                                        cells[:, c, k, a, s * P:(s + 1) * P],
                                                        moving.rearrange("p o q k c -> p (o q k c)"),
                                                        start=(begins and a == 0 and k == 0),
                                                        stop=(ends and a == 1 and k == 1), skip_group_check=True)
                    last.then_inc(cells_used, 1)

            with pe.Fori(0, BLOCKS) as b:
                with pe.Fori(0, GROUP // 2) as hh:
                    for h in range(2):
                        wait_alone(pe, copied, b * GROUP + hh * 2 + h + 1, sems.pe)
                        piece(b, hh, h, 0)
                        with pe.Fori(1, PIECES - 1) as p:
                            piece(b, hh, h, p)
                        piece(b, hh, h, PIECES - 1)
                        pe.wait_ge(cells_used, RING + (b * GROUP + hh * 2 + h + 1) * CHUNKS)
                        pe.sem_inc(head_done, 1)


def mlp(nc, sems, d, psum, x1_dram, enc_dram):
    QW = 512
    BLOCKS, SUBS = NODES // QW, QW // P
    with ExitStack() as ctx:
        def sb(name, shape, dt=F32):
            return ctx.enter_context(nc.sbuf_tensor(name, shape, dt))

        def sem(name):
            return sems.new((name))

        w1, w2, w3, w4 = sb("w1", [P, 4, 256]), sb("w2", [P, 2, 128]), sb("w3", [P, 1, 256]), sb("w4", [P, 2, 512])
        biases, b4 = sb("biases", [P, 5]), sb("b4", [P, 512])
        ident = sb("ident4", [P, P])
        enc, neg = sb("enc4", [P, 2, SUBS, 512]), sb("neg", [P, 2, SUBS, 512])
        enc_t, a1, a2, a3 = sb("enc_t", [P, 4, QW]), sb("a1t", [P, 2, QW]), sb("a2t", [P, QW]), sb("a3t", [P, 2, QW])
        x1 = sb("x1_4", [P, 2, SUBS, 512])
        weights_in = sem("weights_in4")
        enc_in, x_in, out_stored = ([sem(f"{n}{i}") for i in range(2)] for n in ("enc_in4", "x_in4", "out_stored"))
        neg_done, pos_done, exp_done, elu_done, turned, turn_copied = (sem(n) for n in ("neg_done", "pos_done", "exp_done4", "elu_done", "turned4", "turn_copied"))
        layer_done, layer_copied, biased, out_done = (sem(n) for n in ("layer_done", "layer_copied", "biased", "out_done"))
        block = ctx.enter_context(nc.Block())
        enc_v = enc_dram.rearrange("(n s p) k -> n p s k", p=P, s=SUBS)
        x1_v = x1_dram.rearrange("(n s p) k -> n p s k", p=P, s=SUBS)
        out_v = d["out"].rearrange("(n s p) k -> n p s k", p=P, s=SUBS)
        STAGES = 9

        @block.sync
        def _(sp):
            for dst, name, k in ((w1, "W1T", 4), (w2, "W2T", 2), (w3, "W3T", 1), (w4, "W4T", 2)):
                sp.dma_start(dst[:], d[name].rearrange("(t p) n -> p t n", p=P)).then_inc(weights_in, 16)
            sp.dma_start(biases[:], d["mlp_bias_cols"]).then_inc(weights_in, 16)
            sp.dma_start(b4[:], d["b4_rows"]).then_inc(weights_in, 16)
            sp.dma_start(ident[:], d["ident"]).then_inc(weights_in, 16)

            def load(b, par):
                sp.dma_start(enc[:, par], enc_v[b]).then_inc(enc_in[par], 16)
                sp.dma_start(x1[:, par], x1_v[b]).then_inc(x_in[par], 16)

            for par in range(2):
                load(par, par)

            def store(b, par, it):
                wait_alone(sp, x_in[par], it * 16 + 16, sems.sp)
                wait_alone(sp, out_done, 1 + (b + 1) * SUBS, sems.sp)
                sp.dma_start(out_v[b], x1[:, par]).then_inc(out_stored[par], 16)

            with sp.Fori(0, BLOCKS // 2 - 1) as it:
                for par in range(2):
                    store(it * 2 + par, par, it)
                    sp.wait_ge(out_stored[par], it * 16 + 16)
                    load(it * 2 + par + 2, par)
            for par in range(2):
                store(BLOCKS - 2 + par, par, BLOCKS // 2 - 1)
                sp.wait_ge(out_stored[par], (BLOCKS // 2) * 16)

        @block.vector
        def _(dve):
            dve.sem_inc(out_done, 1)
            dve.wait_ge(weights_in, 112)
            with dve.Fori(0, BLOCKS // 2) as it:
                for par in range(2):
                    b = it * 2 + par
                    dve.wait_ge(enc_in[par], it * 16 + 16)
                    nc.vector.tensor_scalar(neg[:, par], enc[:, par], 0.0, None, ALU.min).then_inc(neg_done, 1)
                    dve.wait_ge(neg_done, b + 1)
                    nc.vector.tensor_scalar(enc[:, par], enc[:, par], 0.0, -1.0, ALU.max, ALU.add).then_inc(pos_done, 1)
                    dve.wait_ge(pos_done, b + 1)
                    dve.wait_ge(exp_done, b + 1)
                    nc.vector.tensor_tensor(enc[:, par], enc[:, par], neg[:, par], ALU.add).then_inc(elu_done, 1)
                    for s in range(SUBS):
                        dve.wait_ge(layer_done, (b * 9) + 5 + s + 1)
                        dve.wait_ge(biased, b + 1)
                        nc.vector.tensor_tensor(x1[:, par, s], psum[:, 4 + s, :], x1[:, par, s], ALU.add).then_inc(out_done, 1)

        @block.gpsimd
        def _(pool):
            pool.wait_ge(weights_in, 112)
            with pool.Fori(0, BLOCKS // 2) as it:
                for par in range(2):
                    pool.wait_ge(x_in[par], it * 16 + 16)
                    nc.gpsimd.tensor_tensor(x1[:, par], x1[:, par],
                                            b4[:].rearrange("p (o k) -> p o k", o=1).broadcast_to([P, SUBS, 512]), ALU.add).then_inc(biased, 1)

        @block.tensor
        def _(pe):
            pe.wait_ge(weights_in, 112)
            with pe.Fori(0, BLOCKS // 2) as it:
                for par in range(2):
                    b = it * 2 + par
                    pe.wait_ge(elu_done, b + 1)
                    for t in range(4):
                        pe.wait_ge(layer_copied, 1 + b * STAGES)
                        for s in range(SUBS):
                            last = nc.tensor.transpose(psum[:, t, s * P:(s + 1) * P], enc[:, par, s, t * P:(t + 1) * P], ident[:])
                        last.then_inc(turned, 1)
                    pe.wait_ge(layer_copied, 1 + b * STAGES + 4)
                    for o in range(2):
                        for t in range(4):
                            last = nc.tensor.matmul(psum[:, o, :], w1[:, t, o * P:(o + 1) * P], enc_t[:, t, :], start=(t == 0), stop=(t == 3))
                        last.then_inc(layer_done, 1)
                    pe.wait_ge(layer_copied, 1 + b * STAGES + 6)
                    for t in range(2):
                        last = nc.tensor.matmul(psum[:, 2, :], w2[:, t, :], a1[:, t, :], start=(t == 0), stop=(t == 1))
                    last.then_inc(layer_done, 1)
                    pe.wait_ge(layer_copied, 1 + b * STAGES + 7)
                    for o in range(2):
                        nc.tensor.matmul(psum[:, o, :], w3[:, 0, o * P:(o + 1) * P], a2[:], start=True, stop=True).then_inc(layer_done, 1)
                    pe.wait_ge(layer_copied, 1 + b * STAGES + 9)
                    pe.wait_ge(out_done, 1 + b * SUBS)
                    for s in range(SUBS):
                        for t in range(2):
                            last = nc.tensor.matmul(psum[:, 4 + s, :], a3[:, t, s * P:(s + 1) * P], w4[:, t, :], start=(t == 0), stop=(t == 1))
                        last.then_inc(layer_done, 1)

        @block.scalar
        def _(act):
            act.sem_inc(layer_copied, 1)
            act.wait_ge(weights_in, 112)
            with act.Fori(0, BLOCKS // 2) as it:
                for par in range(2):
                    b = it * 2 + par
                    act.wait_ge(neg_done, b + 1)
                    nc.scalar.activation(neg[:, par], neg[:, par], ACT.Exp).then_inc(exp_done, 1)
                    for t in range(4):
                        act.wait_ge(turned, b * 4 + t + 1)
                        nc.scalar.copy(enc_t[:, t, :], psum[:, t, :]).then_inc(layer_copied, 1)
                    for k, (dst, bank) in enumerate(((a1[:, 0], 0), (a1[:, 1], 1), (a2[:], 2), (a3[:, 0], 0), (a3[:, 1], 1))):
                        act.wait_ge(layer_done, b * 9 + k + 1)
                        nc.scalar.activation(dst, psum[:, bank, :], ACT.Relu, bias=biases[:, k:k + 1]).then_inc(layer_copied, 1)


def build(nc, d, upto=9):
    ht_dram = nc.dram_tensor("ht_dram", (NODES // QB, P, 2 * 4 * QB), F16, kind="Internal").ap()
    x1_dram = nc.dram_tensor("x1_dram", (NODES, 512), F32, kind="Internal").ap()
    wh_dram = nc.dram_tensor("wh_dram", (NODES, 512), F32, kind="Internal").ap()
    enc_dram = nc.dram_tensor("enc_dram", (NODES, 512), F32, kind="Internal").ap()
    srow_dram = nc.dram_tensor("srow_dram", (HEADS, NODES), F32, kind="Internal").ap()
    edge_dram = nc.dram_tensor("edge_dram", (NODES, NODES), BF16, kind="Internal").ap()
    with nc.psum_tensor("psum", [P, 8, 512], F32) as psum, ExitStack() as stack:
        sems = Semaphores(nc, stack)
        with nc.sbuf_tensor("g", [P, 2, 4, NODES], F16) as g, nc.sbuf_tensor("v", [P, 2, 32, 512], F16) as v, \
                nc.sbuf_tensor("c_all", [P, 32], F32) as c_all:
            with nc.sbuf_tensor("wqk", [P, 4, 512], F32) as wqk, nc.sbuf_tensor("wvm", [P, 4, 512], F32) as wvm, \
                    nc.sbuf_tensor("bias_cols", [P, 9], F32) as bias_cols, nc.sbuf_tensor("bvm", [P, 512], F32) as bvm:
                keep = {"wqk": wqk, "wvm": wvm, "bias_cols": bias_cols, "bvm": bvm}
                weight_products(nc, sems, d, keep, psum)
                keys_and_values(nc, sems, d, keep, psum, g, v, c_all, ht_dram)
            if upto >= 1:
                attention(nc, sems, d, psum, g, v, c_all, ht_dram, x1_dram, edge_dram)
        if upto >= 2:
            with ExitStack() as ctx:
                node = {n: ctx.enter_context(nc.sbuf_tensor(n, shape, F32)) for n, shape in (
                    ("factor_j", [P, 32, HEADS, 2]), ("factor_i", [P, 32, HEADS, 2]), ("gate_d", [P, 32, HEADS]), ("mean", [P, 512]))}
                head_features(nc, sems, d, psum, x1_dram, wh_dram, srow_dram, node)
                if upto >= 3:
                    x_parts = ctx.enter_context(nc.sbuf_tensor("x_parts", [P, 32, GROUP, 2, PARTS, COLS], BF16))
                    for gr in range(HEADS // GROUP):
                        split_features(nc, sems, psum, wh_dram, node, x_parts, gr)
                        graph_attention(nc, sems, psum, edge_dram, srow_dram, enc_dram, node, x_parts, gr)
        if upto >= 4:
            mlp(nc, sems, d, psum, x1_dram, enc_dram)


PLAIN = ("x", "L0_gnn_Wk", "L0_gnn_Wq", "L0_gnn_Wv")


def host_layout(inputs):
    import numpy as np

    def transposed(name):
        return np.ascontiguousarray(np.asarray(inputs[name]).T)

    def rows(a):
        a = np.asarray(a).reshape(-1)
        return np.ascontiguousarray(np.broadcast_to(a, (P, a.size)))

    def cols(name):
        return np.ascontiguousarray(np.asarray(inputs[name]).reshape(-1, P).T)

    arrays = {n: np.ascontiguousarray(inputs[n]) for n in PLAIN}
    arrays["adjT"] = transposed("adj")
    arrays["keyT"] = transposed("L0_gnn_key")
    arrays["valueT"] = transposed("L0_gnn_value")
    arrays["WmT"] = transposed("L0_gnn_Wm")
    arrays["bm_rows"] = rows(inputs["L0_gnn_bm"])
    for b in ("bq", "bk", "bv"):
        arrays[f"{b}_cols"] = cols(f"L0_gnn_{b}")
    w = np.asarray(inputs["L1_gnn_W"])
    arrays["W_heads"] = np.ascontiguousarray(w.transpose(1, 0, 2).reshape(w.shape[1], -1))
    arrays["a1_rows"] = rows(inputs["L1_gnn_a1"])
    arrays["a2_rows"] = rows(inputs["L1_gnn_a2"])
    for n in range(1, 5):
        arrays[f"W{n}T"] = transposed(f"L1_gnn_W{n}")
    arrays["mlp_bias_cols"] = np.ascontiguousarray(np.concatenate([cols(f"L1_gnn_b{n}") for n in (1, 2, 3)], axis=1))
    arrays["b4_rows"] = rows(inputs["L1_gnn_b4"])
    arrays["ident"] = np.eye(P, dtype=np.float32)
    return arrays


def kernel(**inputs):
    import concourse.bacc as bacc
    from concourse import mybir as ir
    from concourse.bass_utils import run_bass_kernel_spmd

    nc = bacc.Bacc("TRN2", target_bir_lowering=False, num_devices=1)
    arrays = host_layout(inputs)
    d = {n: nc.dram_tensor(n, a.shape, ir.dt.from_np(a.dtype), kind="ExternalInput").ap() for n, a in arrays.items()}
    d["out"] = nc.dram_tensor("out", (NODES, 512), F32, kind="ExternalOutput").ap()
    build(nc, d)
    return run_bass_kernel_spmd(nc, [arrays], core_ids=[0]).results[0]["out"]
```

```python
from contextlib import ExitStack

import concourse.bass as bass
from concourse import mybir

F32 = mybir.dt.float32
F16 = mybir.dt.float16
BF16 = mybir.dt.bfloat16
ALU = mybir.AluOpType
ACT = mybir.ActivationFunctionType
AX = mybir.AxisListType.X
RMAX = bass.bass_isa.ReduceOp.max

P = 128
EPS = 1e-5
HEADS, HD = 8, 64
UP = 64.0


class Semaphores:

    def __init__(self, nc, ctx):
        self.nc, self.ctx = nc, ctx
        self.act, self.pool, self.pe, self.dve, self.sp = (self.new(f"{n}_carrier") for n in ("act", "pool", "pe", "dve", "sp"))

    def new(self, name):
        return self.ctx.enter_context(self.nc.semaphore(name))


def wait_alone(eng, sem, value, carrier):
    eng.wait_ge(sem, value)
    eng.sem_inc(carrier, 1)


def row_norm(nc, dve, x, stats, sums, scale, tile, carrier, stats_done, sums_done, rstd_done, norm_done):
    nc.vector.bn_stats(stats[:], x).then_inc(stats_done, 1)
    wait_alone(dve, stats_done, tile + 1, carrier)
    nc.vector.bn_aggr(sums[:, 0:2], stats[:]).then_inc(sums_done, 1)
    dve.wait_ge(sums_done, tile * 2 + 1)
    nc.vector.tensor_scalar(sums[:, 2:3], sums[:, 1:2], EPS, None, ALU.add).then_inc(sums_done, 1)
    dve.wait_ge(rstd_done, tile + 1)
    nc.vector.scalar_tensor_tensor(out=scale[:, 1:2], in0=sums[:, 0:1], scalar=-1.0, in1=scale[:, 0:1],
                                   op0=ALU.mult, op1=ALU.mult).then_inc(norm_done, 1)


def row_rstd(nc, pool, sums, scale, tile, sums_done, h_done, rstd_done):
    pool.wait_ge(h_done, 1 + tile)
    pool.wait_ge(sums_done, tile * 2 + 2)
    nc.gpsimd.tensor_tensor(scale[:, 0:1], sums[:, 2:3], sums[:, 3:4], ALU.pow).then_inc(rstd_done, 1)


def row_relu_norm(nc, act, x, scale, tile, norm_done, h_done):
    act.wait_ge(norm_done, tile + 1)
    nc.scalar.activation(x, x, ACT.Relu, scale=scale[:, 0:1], bias=scale[:, 1:2]).then_inc(h_done, 1)


def weight_products(nc, sems, d, keep, psum, w_half_dram):
    T, WIDE = 4, 512 + 2 * HEADS
    with ExitStack() as ctx:
        def sb(name, shape, dt=F32):
            return ctx.enter_context(nc.sbuf_tensor(name, shape, dt))

        def sem(name):
            return sems.new((name))

        wk, wq, wv, wm = (sb(f"{n}_raw", [P, T, 512]) for n in ("wk", "wq", "wv", "wm"))
        bq, bk, bv = (sb(f"{n}_col", [P, T]) for n in ("bq", "bk", "bv"))
        bm = sb("bm_row", [P, 512])
        w_all = sb("w_all", [P, T, WIDE])
        w_half = sb("w_half0", [P, 2, T, WIDE], F16)
        a_rows = sb("a_rows", [P, 2, 512])
        w_a = sb("w_a", [P, 512])
        loaded_qk, loaded_vm, loaded_heads = sem("loaded_qk"), sem("loaded_vm"), sem("loaded_heads")
        product_done, product_copied, halves_stored = sem("product_done"), sem("product_copied"), sem("halves_stored")
        wa_step, halves_done, high_done = sem("wa_step"), sem("halves_done"), sem("product_high")
        block = ctx.enter_context(nc.Block())

        @block.sync
        def _(sp):
            for dst, src in ((wk, d["L0_gnn_Wk"]), (wq, d["L0_gnn_Wq"])):
                sp.dma_start(dst[:], src.rearrange("(t p) n -> p t n", p=P)).then_inc(loaded_qk, 16)
            sp.dma_start(w_all[:, :, 0:512], d["W_heads"].rearrange("(t p) n -> p t n", p=P)).then_inc(loaded_heads, 16)
            sp.dma_start(a_rows[:, 0], d["a1_rows"]).then_inc(loaded_heads, 16)
            sp.dma_start(a_rows[:, 1], d["a2_rows"]).then_inc(loaded_heads, 16)
            for dst, src in ((wv, d["L0_gnn_Wv"]), (wm, d["WmT"])):
                sp.dma_start(dst[:], src.rearrange("(t p) n -> p t n", p=P)).then_inc(loaded_vm, 16)
            for dst, src in ((bq, d["bq_cols"]), (bk, d["bk_cols"]), (bv, d["bv_cols"])):
                sp.dma_start(dst[:], src).then_inc(loaded_vm, 16)
            sp.dma_start(bm[:], d["bm_rows"]).then_inc(loaded_vm, 16)
            sp.wait_ge(halves_done, 4)
            sp.dma_start(w_half_dram, w_half[:].rearrange("p a t n -> p (a t n)")).then_inc(halves_stored, 16)
            sp.wait_ge(halves_stored, 16)

        @block.tensor
        def _(pe):
            pe.wait_ge(loaded_qk, 32)
            for a, b, bank in ((wk, wq, 0), (wv, wm, 4)):
                if bank:
                    pe.wait_ge(loaded_vm, 96)
                for e in range(T):
                    for o in range(T):
                        last = nc.tensor.matmul(psum[:, bank + e, :], a[:, o, e * P:(e + 1) * P], b[:, o, :],
                                                start=(o == 0), stop=(o == T - 1))
                    last.then_inc(product_done, 1)
            pe.wait_ge(product_copied, 2)
            for w, bias, col in ((wq, bk, 0), (wk, bq, T)):
                for e in range(T):
                    for o in range(T):
                        last = nc.tensor.matmul(psum[:, 0, col + e:col + e + 1], w[:, o, e * P:(e + 1) * P],
                                                bias[:, o:o + 1], start=(o == 0), stop=(o == T - 1))
            for o in range(T):
                last = nc.tensor.matmul(psum[:, 0, 2 * T:2 * T + 1], bk[:, o:o + 1].broadcast_to([P, P]),
                                        bq[:, o:o + 1], start=(o == 0), stop=(o == T - 1))
            last.then_inc(product_done, 1)
            for o in range(T):
                last = nc.tensor.matmul(psum[:, 1, :], bv[:, o:o + 1].broadcast_to([P, P]), wm[:, o, :],
                                        start=(o == 0), stop=(o == T - 1))
            last.then_inc(product_done, 1)

        @block.scalar
        def _(act):
            for n in range(2 * T):
                act.wait_ge(product_done, n + 1)
                dst = keep["wqk" if n < T else "wvm"][:, 0, n % T, :]
                nc.scalar.activation(dst, psum[:, n, :], ACT.Copy, scale=UP).then_inc(high_done, 1)

        @block.vector
        def _(dve):
            dve.wait_ge(loaded_heads, 48)
            for n in range(2 * T):
                t, k = n // 2, n % 2
                dve.wait_ge(wa_step, 2 * n)
                nc.vector.tensor_tensor(w_a[:], w_all[:, t, 0:512], a_rows[:, k], ALU.mult).then_inc(wa_step, 1)
                dve.wait_ge(wa_step, 2 * n + 1)
                nc.vector.tensor_reduce(w_all[:, t, 512 + k * HEADS:512 + (k + 1) * HEADS],
                                        w_a[:].rearrange("p (h k) -> p h k", h=HEADS), AX, ALU.add).then_inc(wa_step, 1)
            dve.wait_ge(wa_step, 4 * T)
            for t in range(0, T, 2):
                nc.vector.tensor_scalar(w_half[:, 0, t:t + 2, :], w_all[:, t:t + 2, :], UP, None, ALU.mult).then_inc(halves_done, 1)
            dve.wait_ge(halves_done, 2)
            for t in range(0, T, 2):
                nc.vector.scalar_tensor_tensor(out=w_half[:, 1, t:t + 2, :], in0=w_all[:, t:t + 2, :], scalar=UP,
                                               in1=w_half[:, 0, t:t + 2, :], op0=ALU.mult, op1=ALU.subtract).then_inc(halves_done, 1)
            for n in range(2 * T):
                dve.wait_ge(high_done, n + 1)
                dst = keep["wqk" if n < T else "wvm"]
                nc.vector.scalar_tensor_tensor(out=dst[:, 1, n % T, :], in0=psum[:, n, :], scalar=UP, in1=dst[:, 0, n % T, :],
                                               op0=ALU.mult, op1=ALU.subtract).then_inc(product_copied, 1)
            dve.wait_ge(product_done, 2 * T + 1)
            nc.vector.tensor_scalar(keep["bias_cols"][:], psum[:, 0, 0:2 * T + 1], UP, None, ALU.mult).then_inc(product_copied, 1)
            wc, wc_half = keep["bias_cols"][:, T:2 * T], keep["wc_half"]
            dve.wait_ge(product_copied, 2 * T + 1)
            nc.vector.tensor_copy(wc_half[:, 0], wc).then_inc(product_copied, 1)
            dve.wait_ge(product_copied, 2 * T + 2)
            nc.vector.tensor_tensor(wc_half[:, 1], wc, wc_half[:, 0], ALU.subtract).then_inc(product_copied, 1)
            dve.wait_ge(product_done, 2 * T + 2)
            nc.vector.tensor_tensor(keep["bvm"][:], psum[:, 1, :], bm[:], ALU.add).then_inc(product_copied, 1)


def keys_and_values(nc, sems, d, keep, psum, g, v, c_all, ht_dram):
    T, B = 4, 8
    wqk, wvm, gk, wc_half = keep["wqk"], keep["wvm"], keep["bias_cols"], keep["wc_half"]
    with ExitStack() as ctx:
        def sb(name, shape, dt=F32):
            return ctx.enter_context(nc.sbuf_tensor(name, shape, dt))

        def sem(name):
            return sems.new((name))

        key_t, value_t = sb("key_t", [P, T, 512]), sb("value_t", [P, T, 512])
        key_half, value_half = sb("key_half", [P, 2, T, 512], F16), sb("value_half", [P, 2, T, 512], F16)
        v_sum = sb("v_sum", [P, 2, 512])
        x_tile = sb("x_tile0", [P, 2, 512])
        h_stage = sb("h_stage", [P, 2, 2, T, 256], F16)
        stats, sums, scale = sb("stats0", [P, 6]), sb("sums0", [P, 4]), sb("scale0", [P, 2])
        ident = sb("ident0", [P, P])
        x_in, stage_stored = ([sem(f"{n}{i}") for i in range(2)] for n in ("x_in", "stage_stored"))
        key_in, value_in = sem("key_in"), sem("value_in")
        key_high, key_low, value_high, value_low = (sem(n) for n in ("key_high", "key_low", "value_high", "value_low"))
        ident_in, exponent_in = sem("ident_in0"), sem("exponent_in0")
        tile_done, bank_free = sem("tile_done"), sem("bank_free")
        c_done, c_free = sem("c_done"), sem("c_free")
        g_high_done, v_high_done, v_sum_free = (sem(n) for n in ("g_high", "v_high", "v_sum_free"))
        stats_done, sums_done, rstd_done, norm_done, h_done = (sem(n) for n in ("stats_s0", "sums_s0", "rstd0", "norm0", "h0"))
        turned, high_done, low_done = (sem(n) for n in ("turned0", "high0", "low0"))
        block = ctx.enter_context(nc.Block())

        kv = d["keyT"].rearrange("(t p) m -> p t m", p=P)
        vv = d["valueT"].rearrange("(t p) m -> p t m", p=P)
        xv = d["x"].rearrange("(n p) k -> n p k", p=P)

        @block.sync
        def _(sp):
            def load_key(m):
                sp.dma_start(key_t[:], kv[:, :, bass.ds(m * 512, 512)]).then_inc(key_in, 16)

            def load_value(m):
                sp.dma_start(value_t[:], vv[:, :, bass.ds(m * 512, 512)]).then_inc(value_in, 16)

            def next_x(m, n):
                sp.wait_ge(turned, m * 4 + n + 1)
                sp.dma_start(x_tile[:, n % 2], xv[m * 4 + n + 2]).then_inc(x_in[n % 2], 16)

            def store_h(m, pair):
                wait_alone(sp, low_done, 2 + m * 4 + pair * 2 + 2, sems.sp)
                sp.dma_start(ht_dram[m * 2 + pair], h_stage[:, pair].rearrange("p a t i -> p (a t i)")).then_inc(stage_stored[pair], 16)

            for pair in range(2):
                sp.sem_inc(stage_stored[pair], 16)
            load_key(0)
            for n in range(2):
                sp.dma_start(x_tile[:, n], xv[n]).then_inc(x_in[n], 16)
            sp.dma_start(ident[:], d["ident"]).then_inc(ident_in, 16)
            load_value(0)
            with sp.Fori(0, B - 1) as m:
                sp.wait_ge(key_low, m + 1)
                load_key(m + 1)
                next_x(m, 0)
                sp.wait_ge(value_low, m + 1)
                load_value(m + 1)
                next_x(m, 1)
                store_h(m, 0)
                next_x(m, 2)
                next_x(m, 3)
                store_h(m, 1)
            for n in range(2):
                next_x(B - 1, n)
            for pair in range(2):
                store_h(B - 1, pair)
                sp.wait_ge(stage_stored[pair], 16 + 16 * B)

        @block.tensor
        def _(pe):
            pe.wait_ge(ident_in, 16)
            with pe.Fori(0, B) as m:
                pe.wait_ge(key_low, m + 1)
                pe.wait_ge(c_free, m + 1)
                for s in range(T):
                    for e in range(T):
                        for a, b in ((0, 0), (0, 1), (1, 0)):
                            last = nc.tensor.matmul(psum[:, 4, s:s + 1], key_half[:, a, e, s * P:(s + 1) * P], wc_half[:, b, e:e + 1],
                                                    start=(e == 0 and a + b == 0), stop=(e == T - 1 and a == 1))
                last.then_inc(c_done, 1)
                for q in range(2 * T):
                    n = q % T
                    cols = slice(n * P, (n + 1) * P)
                    if q == T:
                        pe.wait_ge(value_low, m + 1)
                    pe.wait_ge(bank_free, m * 8 + q + 1)
                    for e in range(T):
                        for a, b in ((0, 0), (0, 1), (1, 0)):
                            pair = (wqk[:, a, e, cols], key_half[:, b, e, :]) if q < T else (value_half[:, a, e, cols], wvm[:, b, e, :])
                            last = nc.tensor.matmul(psum[:, n, :], *pair, start=(e == 0 and a + b == 0), stop=(e == T - 1 and a == 1))
                    last.then_inc(tile_done, 1)
                    if q % 2:
                        n = q // 2
                        pe.wait_ge(h_done, 1 + m * 4 + n + 1)
                        pe.wait_ge(low_done, m * 4 + n + 1)
                        for t in range(T):
                            last = nc.tensor.transpose(psum[:, 6 + n % 2, t * P:(t + 1) * P],
                                                       x_tile[:, n % 2, t * P:(t + 1) * P], ident[:])
                        last.then_inc(turned, 1)

        @block.scalar
        def _(act):
            def high_of_keys(m):
                act.wait_ge(key_in, m * 16 + 16)
                nc.scalar.copy(key_half[:, 0], key_t[:]).then_inc(key_high, 1)

            def block_of(m, ended):
                for n in range(4):
                    if n == 2 and not ended:
                        wait_alone(act, tile_done, m * 8 + T, sems.act)
                        high_of_keys(m + 1)
                    if not (ended and n == 3):
                        row_relu_norm(nc, act, x_tile[:, (n + 1) % 2], scale, m * 4 + n + 1, norm_done, h_done)
                    for q in (2 * n, 2 * n + 1):
                        if q < T:
                            wait_alone(act, tile_done, m * 8 + q + 1, sems.act)
                            nc.scalar.activation(g[:, 0, q, bass.ds(m * 512, 512)], psum[:, q, :], ACT.Identity,
                                                 bias=gk[:, q:q + 1]).then_inc(g_high_done, 1)
                        else:
                            wait_alone(act, bank_free, T + m * 8 + q + 1, sems.act)
                            nc.scalar.copy(v[:, 0, m * 4 + q - T, :], v_sum[:, q % 2]).then_inc(v_high_done, 1)
                        if q == 0:
                            act.wait_ge(value_in, m * 16 + 16)
                            nc.scalar.copy(value_half[:, 0], value_t[:]).then_inc(value_high, 1)
                    act.wait_ge(turned, m * 4 + n + 1)
                    if n % 2 == 0:
                        act.wait_ge(stage_stored[n // 2], m * 16 + 16)
                    nc.scalar.copy(h_stage[:, n // 2, 0, :, (n % 2) * P:(n % 2 + 1) * P],
                                   psum[:, 6 + n % 2, :].rearrange("p (t i) -> p t i", t=T)).then_inc(high_done, 1)

            act.sem_inc(h_done, 1)
            high_of_keys(0)
            row_relu_norm(nc, act, x_tile[:, 0], scale, 0, norm_done, h_done)
            with act.Fori(0, B - 1) as m:
                block_of(m, False)
            block_of(B - 1, True)

        @block.vector
        def _(dve):
            def low_of_keys(m):
                dve.wait_ge(key_high, m + 1)
                nc.vector.tensor_tensor(key_half[:, 1], key_t[:], key_half[:, 0], ALU.subtract).then_inc(key_low, 1)

            def norm(tile, par, n_in):
                dve.wait_ge(x_in[par], n_in * 16)
                row_norm(nc, dve, x_tile[:, par], stats, sums, scale, tile, sems.dve, stats_done, sums_done, rstd_done, norm_done)

            def block_of(m, ended):
                for n in range(4):
                    if not (ended and n == 3):
                        norm(m * 4 + n + 1, (n + 1) % 2, m * 2 + (n + 1) // 2 + 1)
                    if n == 2 and not ended:
                        low_of_keys(m + 1)
                    for q in (2 * n, 2 * n + 1):
                        if q < T:
                            dve.wait_ge(g_high_done, m * 4 + q + 1)
                            cols = bass.ds(m * 512, 512)
                            nc.vector.scalar_tensor_tensor(out=g[:, 1, q, cols], in0=psum[:, q, :], scalar=gk[:, q:q + 1],
                                                           in1=g[:, 0, q, cols], op0=ALU.add, op1=ALU.subtract
                                                           ).then_inc(bank_free, 1)
                        else:
                            dve.wait_ge(tile_done, m * 8 + q + 1)
                            dve.wait_ge(v_sum_free, m * 4 + q - T + 1)
                            nc.vector.scalar_tensor_tensor(out=v_sum[:, q % 2], in0=psum[:, q - T, :], scalar=1.0 / UP,
                                                           in1=keep["bvm"][:], op0=ALU.mult, op1=ALU.add).then_inc(bank_free, 1)
                        if q == 0:
                            dve.wait_ge(c_done, m + 1)
                            nc.vector.tensor_scalar(c_all[:, bass.ds(m * 4, 4)], psum[:, 4, 0:T], gk[:, 2 * T:2 * T + 1],
                                                    None, ALU.add).then_inc(c_free, 1)
                            dve.wait_ge(value_high, m + 1)
                            nc.vector.tensor_tensor(value_half[:, 1], value_t[:], value_half[:, 0], ALU.subtract).then_inc(value_low, 1)
                    dve.wait_ge(high_done, m * 4 + n + 1)
                    nc.vector.tensor_tensor(h_stage[:, n // 2, 1, :, (n % 2) * P:(n % 2 + 1) * P],
                                            psum[:, 6 + n % 2, :].rearrange("p (t i) -> p t i", t=T),
                                            h_stage[:, n // 2, 0, :, (n % 2) * P:(n % 2 + 1) * P],
                                            ALU.subtract).then_inc(low_done, 1)

            dve.sem_inc(bank_free, T)
            dve.sem_inc(c_free, 1)
            dve.sem_inc(low_done, 2)
            low_of_keys(0)
            norm(0, 0, 1)
            with dve.Fori(0, B - 1) as m:
                block_of(m, False)
            block_of(B - 1, True)

        @block.gpsimd
        def _(pool):
            nc.gpsimd.memset(sums[:, 3:4], -0.5).then_inc(exponent_in, 1)
            pool.wait_ge(exponent_in, 1)
            pool.sem_inc(v_sum_free, 2)

            def block_of(m, ended):
                for n in range(4):
                    if not (ended and n == 3):
                        row_rstd(nc, pool, sums, scale, m * 4 + n + 1, sums_done, h_done, rstd_done)
                    if n >= 2:
                        for q in (2 * n - T, 2 * n - T + 1):
                            pool.wait_ge(v_high_done, m * 4 + q + 1)
                            nc.gpsimd.tensor_tensor(v[:, 1, m * 4 + q, :], v_sum[:, q % 2], v[:, 0, m * 4 + q, :],
                                                    ALU.subtract).then_inc(v_sum_free, 1)

            row_rstd(nc, pool, sums, scale, 0, sums_done, h_done, rstd_done)
            with pool.Fori(0, B - 1) as m:
                block_of(m, False)
            block_of(B - 1, True)


NODES = 4096
QB = 256
MASKED = -1e9


def attention(nc, sems, d, psum, g, v, c_all, ht_dram, x1_dram, edge_dram):
    T, JP, BLOCKS = 4, 16, NODES // QB
    SCALE, MARK = 64.0 * UP, 2.0 ** 80
    with ExitStack() as ctx:
        def sb(name, shape, dt=F32):
            return ctx.enter_context(nc.sbuf_tensor(name, shape, dt))

        def sem(name):
            return sems.new((name))

        strip = sb("strip", [P, 2 * JP, QB])
        prob = sb("prob", [P, 2, 2 * JP, QB], F16)
        h_t = sb("h_t", [P, 2, T, QB], F16)
        adj = sb("adj", [P, 2, 2, QB])
        least = sb("least", [P, 2, QB])
        weight = sb("weight", [P, 2, QB])
        mark = sb("mark", [P, 2, QB], BF16)
        bound = sb("bound", [P, 1])
        res = sb("res", [P, 512])
        ones = sb("ones", [P, 1], F16)
        total, inv = sb("total", [P, 2]), sb("inv", [P, 2])
        h_in, res_in, ones_in, stored, narrowed = (sem(n) for n in ("h_in", "res_in", "ones_in", "stored1", "narrowed"))
        adj_in = [sem(f"adj_in{i}") for i in range(2)]
        scored, score_free = sem("scored"), sem("score_free")
        abs_done, mark_done, pair_done, least_done, least_clear, bound_in = (sem(n) for n in ("abs_s", "mark_s", "pair_s", "least_s", "least_clear", "bound_in"))
        halves_done, top_row, shifted, high_done, weight_done, low_done = (sem(n) for n in ("halves", "top_row", "shifted", "high1", "weight_s", "low1"))
        prob_used, total_done, inv_done, res_done = (sem(n) for n in ("prob_used", "total_done", "inv_done", "res_done"))
        block = ctx.enter_context(nc.Block())
        adj_v = d["adjT"].rearrange("(k a p) i -> k p a i", p=P, a=2)
        xv = d["x"].rearrange("(n p) k -> n p k", p=P)
        x1v = x1_dram.rearrange("(n p) k -> n p k", p=P)

        SCORE_BANKS = (0, 1, 6, 7)
        OUTPUT_BANKS = (2, 3, 4, 5)
        RING = len(SCORE_BANKS)

        @block.sync
        def _(sp):
            def load_adj(b, k, par):
                sp.wait_ge(score_free, (b * JP + k) + RING - 1)
                sp.dma_start(adj[:, par], adj_v[k, :, :, bass.ds(b * QB, QB)]).then_inc(adj_in[par], 16)

            def load_block(b):
                with sp.Fori(0, JP // 2) as kk:
                    for par in range(2):
                        load_adj(b, kk * 2 + par, par)

            sp.dma_start(h_t[:].rearrange("p a t i -> p (a t i)"), ht_dram[0]).then_inc(h_in, 16)
            load_block(0)
            with sp.Fori(1, BLOCKS) as b:
                sp.wait_ge(scored, b * JP)
                sp.dma_start(h_t[:].rearrange("p a t i -> p (a t i)"), ht_dram[b]).then_inc(h_in, 16)
                load_block(b)

        @block.tensor
        def _(pe):
            def scores(b):
                wait_alone(pe, h_in, b * 16 + 16, sems.pe)
                with pe.Fori(0, JP // RING) as kk:
                    for j, bank in enumerate(SCORE_BANKS):
                        pe.wait_ge(score_free, (b * JP + kk * RING + j) + 1)
                        for a in range(2):
                            jt = (kk * RING + j) * 2 + a
                            first = True
                            for t in range(T):
                                key = [g[:, hl, t, bass.ds(jt * P, P)] for hl in range(2)]
                                for kh, hh in ((0, 0), (0, 1), (1, 0)):
                                    last = nc.tensor.matmul(psum[:, bank, a * QB:(a + 1) * QB], key[kh], h_t[:, hh, t, :],
                                                            start=first, stop=(t == T - 1 and kh == 1))
                                    first = False
                        last.then_inc(scored, 1)

            def outputs(b, banks=OUTPUT_BANKS):
                if banks is OUTPUT_BANKS:
                    pe.wait_ge(res_done, 1 + b * 2)

                def key_tile(jt, start, stop):
                    for s in range(2):
                        high = prob[:, 0, jt, s * P:(s + 1) * P]
                        low = prob[:, 1, jt, s * P:(s + 1) * P]
                        out, row_sum = psum[:, banks[s], :], psum[:, banks[2 + s], 0:1]
                        nc.tensor.matmul(out, high, v[:, 0, jt, :], start=start, stop=False)
                        nc.tensor.matmul(out, high, v[:, 1, jt, :], start=False, stop=False)
                        nc.tensor.matmul(row_sum, high, ones[:], start=start, stop=False)
                        nc.tensor.matmul(out, low, v[:, 0, jt, :], start=False, stop=stop)
                        last = nc.tensor.matmul(row_sum, low, ones[:], start=False, stop=stop)
                    return last

                pe.wait_ge(low_done, 1 + b * JP + 1)
                key_tile(0, True, False)
                key_tile(1, False, False).then_inc(prob_used, 1)
                with pe.Fori(1, JP - 1) as k:
                    pe.wait_ge(low_done, 1 + b * JP + k + 1)
                    key_tile(k * 2, False, False)
                    key_tile(k * 2 + 1, False, False).then_inc(prob_used, 1)
                pe.wait_ge(low_done, 1 + b * JP + JP)
                key_tile(2 * JP - 2, False, False)
                key_tile(2 * JP - 1, False, True).then_inc(prob_used, 1)

            pe.wait_ge(ones_in, 1)
            scores(0)
            with pe.Fori(1, BLOCKS) as b:
                scores(b)
                outputs(b - 1)
            pe.wait_ge(score_free, RING + BLOCKS * JP)
            outputs(BLOCKS - 1, SCORE_BANKS)

        @block.vector
        def _(dve):
            dve.sem_inc(score_free, RING)
            for done in (pair_done, low_done, res_done):
                dve.sem_inc(done, 1)
            nc.vector.memset(bound[:], MARK * SCALE * 1e-5).then_inc(bound_in, 1)
            nc.vector.memset(ones[:], 1.0).then_inc(ones_in, 1)

            def product(b, kk, j):
                k, bank, par = kk * RING + j, SCORE_BANKS[j % RING], j % 2
                n = b * JP + k
                dve.wait_ge(scored, n + 1)
                dve.wait_ge(adj_in[par], (b * (JP // 2) + kk * (RING // 2) + j // 2) * 16 + 16)
                for a in range(2):
                    ins = nc.vector.scalar_tensor_tensor(
                        out=strip[:, k * 2 + a, :], in0=psum[:, bank, a * QB:(a + 1) * QB],
                        scalar=c_all[:, bass.ds(k * 2 + a, 1)], in1=adj[:, par, a, :], op0=ALU.add, op1=ALU.mult)
                ins.then_inc(score_free, 1)

            def negate(b, k):
                n = b * JP + k
                t = strip[:, bass.ds(k * 2, 2), :]
                dve.wait_ge(mark_done, 1 + n + 1)
                nc.vector.scalar_tensor_tensor(out=t, in0=mark[:], scalar=-MASKED * SCALE, in1=t,
                                               op0=ALU.min, op1=ALU.subtract).then_inc(pair_done, 1)
                dve.wait_ge(pair_done, 1 + n + 1)
                nc.vector.tensor_tensor(least[:], least[:], t, ALU.min).then_inc(least_done, 1)

            def mask_scores(b, ended):
                nc.vector.memset(least[:], 3.0e38).then_inc(least_clear, 1)
                wait_alone(dve, least_clear, b + 1, sems.dve)
                product(b, 0, 0)

                def pairs(k0, k1):
                    with dve.Fori(k0, k1) as kk:
                        for j in range(RING):
                            product(b, kk, j + 1)
                            negate(b, kk * RING + j)

                ROUNDS = JP // RING
                if ended is None:
                    pairs(0, ROUNDS - 1)
                else:
                    pairs(0, 1)
                    finish(ended, 0)
                    pairs(1, ROUNDS - 1)
                    finish(ended, 1)
                for j in range(RING):
                    if j + 1 < RING:
                        product(b, ROUNDS - 1, j + 1)
                    negate(b, JP - RING + j)
                dve.wait_ge(least_done, b * JP + JP)
                nc.vector.scalar_tensor_tensor(out=least[:, 0, :], in0=least[:, 0, :], scalar=1.0, in1=least[:, 1, :],
                                               op0=ALU.mult, op1=ALU.min).then_inc(halves_done, 1)
                dve.wait_ge(halves_done, b * 2 + 1)
                nc.vector.tensor_scalar(least[:, 0, :], least[:, 0, :], -1.0, None, ALU.mult).then_inc(halves_done, 1)

            def probabilities(b):
                wait_alone(dve, top_row, b + 1, sems.dve)

                def shift(k):
                    t = strip[:, bass.ds(k * 2, 2), :]
                    nc.vector.tensor_tensor(t, t, least[:, 1:2, :].broadcast_to([P, 2, QB]), ALU.add).then_inc(shifted, 1)

                def low(k):
                    dve.wait_ge(weight_done, b * JP + k + 1)
                    nc.vector.tensor_tensor(prob[:, 1, bass.ds(k * 2, 2), :], weight[:], prob[:, 0, bass.ds(k * 2, 2), :],
                                            ALU.subtract).then_inc(low_done, 1)

                shift(0)
                with dve.Fori(0, JP - 1) as k:
                    shift(k + 1)
                    low(k)
                low(JP - 1)

            def finish(b, s, banks=OUTPUT_BANKS):
                if s == 0:
                    dve.wait_ge(prob_used, b * JP + JP)
                    for i in range(2):
                        ins = nc.vector.tensor_copy(total[:, i:i + 1], psum[:, banks[2 + i], 0:1])
                    ins.then_inc(total_done, 1)
                    dve.wait_ge(total_done, b + 1)
                    nc.vector.reciprocal(inv[:], total[:]).then_inc(inv_done, 1)
                    dve.wait_ge(inv_done, b + 1)
                dve.wait_ge(res_in, (b * 2 + s) * 16 + 16)
                nc.vector.scalar_tensor_tensor(out=res[:], in0=psum[:, banks[s], :], scalar=inv[:, s:s + 1], in1=res[:],
                                               op0=ALU.mult, op1=ALU.add).then_inc(res_done, 1)

            mask_scores(0, None)
            probabilities(0)
            mask_scores(1, None)
            probabilities(1)
            with dve.Fori(2, BLOCKS) as b:
                mask_scores(b, b - 2)
                probabilities(b)
            for b, banks in ((BLOCKS - 2, OUTPUT_BANKS), (BLOCKS - 1, SCORE_BANKS)):
                for s in range(2):
                    finish(b, s, banks)

        @block.scalar
        def _(act):
            def marks(b):
                with act.Fori(0, JP) as k:
                    n = b * JP + k
                    act.wait_ge(mark_done, 1 + n)
                    wait_alone(act, score_free, RING + n + 1, sems.act)
                    nc.scalar.activation(weight[:], strip[:, bass.ds(k * 2, 2), :], ACT.Abs).then_inc(abs_done, 1)
                    act.wait_ge(abs_done, n + 1)
                    act.wait_ge(pair_done, 1 + n)
                    nc.scalar.activation(mark[:], weight[:], ACT.Relu, scale=-MARK, bias=bound[:, 0:1]).then_inc(mark_done, 1)

            def exps(b):
                with act.Fori(0, JP) as k:
                    n = b * JP + k
                    t = strip[:, bass.ds(k * 2, 2), :]
                    wait_alone(act, shifted, n + 1, sems.act)
                    if b is not FIRST:
                        wait_alone(act, prob_used, (b - 1) * JP + k + 1, sems.act)
                    nc.scalar.activation(prob[:, 0, bass.ds(k * 2, 2), :], t, ACT.Exp, scale=-1.0 / SCALE).then_inc(high_done, 1)
                    wait_alone(act, low_done, 1 + n, sems.act)
                    nc.scalar.activation(weight[:], t, ACT.Exp, scale=-1.0 / SCALE).then_inc(weight_done, 1)

            FIRST = 0
            act.sem_inc(mark_done, 1)
            act.wait_ge(bound_in, 1)
            marks(FIRST)
            exps(FIRST)
            with act.Fori(1, BLOCKS) as b:
                marks(b)
                exps(b)

        @block.gpsimd
        def _(pool):
            def top_of(b):
                wait_alone(pool, halves_done, b * 2 + 2, sems.pool)
                nc.gpsimd.partition_all_reduce(least[:, 1, :], least[:, 0, :], P, RMAX).then_inc(top_row, 1)

            def move_rows(b):
                for s in range(2):
                    n = b * 2 + s
                    pool.dma_start(res[:], xv[n]).then_inc(res_in, 16)
                    wait_alone(pool, res_done, 1 + n + 1, sems.pool)
                    pool.dma_start(x1v[n], res[:]).then_inc(stored, 16)
                    wait_alone(pool, stored, n * 16 + 16, sems.pool)

            def narrow_edges(b):
                for n in range(2):
                    rows = bass.ds((b * 2 + n) * P, P)
                    pool.dma_start(edge_dram[rows, :], d["adjT"][rows, :]).then_inc(narrowed, 16)

            narrow_edges(0)
            top_of(0)
            narrow_edges(1)
            top_of(1)
            with pool.Fori(2, BLOCKS) as b:
                move_rows(b - 2)
                narrow_edges(b)
                top_of(b)
            for b in (BLOCKS - 2, BLOCKS - 1):
                move_rows(b)
            pool.wait_ge(narrowed, 2 * BLOCKS * 16)


SLOPE = 0.2
GATE = 2.0 ** 60


def head_features(nc, sems, d, psum, x1_dram, w_half_dram, wh_dram, srow_dram, node):
    T, TILES, XBUF = 4, NODES // P, 4
    BLOCKS = TILES // T
    WIDE = 512 + 2 * HEADS
    with ExitStack() as ctx:
        def sb(name, shape, dt=F32):
            return ctx.enter_context(nc.sbuf_tensor(name, shape, dt))

        def sem(name):
            return sems.new((name))

        w_half = sb("w_half", [P, 2, T, WIDE], F16)
        ident = sb("ident2", [P, P])
        x_tile = sb("x_tile2", [P, XBUF, 512])
        h_t = sb("h_t2", [P, 2, 2, T, 512], F16)
        wh_tile = sb("wh_tile", [P, 2, 512])
        wh_sum = sb("wh_sum", [P, 512])
        mean_w = sb("mean_w", [P, P])
        s_row = sb("s_row2", [HEADS, NODES])
        sd = sb("sd", [P, TILES, 2 * HEADS])
        stats, sums, scale = sb("stats2", [P, 6]), sb("sums2", [P, 4]), sb("scale2", [P, 2])
        d_top, z = sb("d_top", [P, 2, HEADS]), sb("z", [P, 4, TILES, HEADS])
        x_in = [sem(f"x_in2{i}") for i in range(XBUF)]
        wh_stored = [sem(f"wh_stored{i}") for i in range(2)]
        weights_in, ready, exponent_in, zeroed = sem("weights_in2"), sem("ready2"), sem("exponent_in2"), sem("zeroed2")
        stats_done, sums_done, rstd_done, norm_done, h_done = (sem(n) for n in ("stats_s2", "sums_s2", "rstd2", "norm2", "h2"))
        turned, high_done, low_done = (sem(n) for n in ("turned2", "high2", "low2"))
        feature_done, wh_copied, sd_copied, added = (sem(n) for n in ("feature_done", "wh_copied", "sd_copied", "added"))
        rows_done, rows_copied, rows_stored, mean_done, mean_copied = (sem(n) for n in ("rows_done", "rows_copied", "rows_stored", "mean_done", "mean_copied"))
        factor_step, exp_ready, exp_done = sem("factor_step"), sem("exp_ready"), sem("exp_done")
        block = ctx.enter_context(nc.Block())
        xv = x1_dram.rearrange("(n p) k -> n p k", p=P)
        whv = wh_dram.rearrange("(n p) k -> n p k", p=P)

        @block.sync
        def _(sp):
            def next_x(m, n):
                sp.wait_ge(turned, m * T + n + 1)
                sp.dma_start(x_tile[:, n], xv[m * T + n + XBUF]).then_inc(x_in[n], 16)

            def store(q, par):
                wait_alone(sp, wh_copied, 2 + q + 1, sems.sp)
                sp.dma_start(whv[q], wh_tile[:, par]).then_inc(wh_stored[par], 16)

            for par in range(2):
                sp.sem_inc(wh_stored[par], 16)
            for n in range(XBUF):
                sp.dma_start(x_tile[:, n], xv[n]).then_inc(x_in[n], 16)
                if n == 0:
                    sp.dma_start(ident[:], d["ident"]).then_inc(weights_in, 16)
                    sp.dma_start(w_half[:].rearrange("p a t n -> p (a t n)"), w_half_dram).then_inc(weights_in, 16)
            for n in range(T):
                next_x(0, n)
                if n >= 2:
                    store(n - 2, n % 2)
            with sp.Fori(1, BLOCKS - 1) as m:
                for n in range(T):
                    next_x(m, n)
                    store(m * T + n - 2, n % 2)
            for q in range(TILES - T - 2, TILES):
                store(q, q % 2)
            sp.wait_ge(rows_copied, 1 + BLOCKS)
            sp.dma_start(srow_dram, s_row[:]).then_inc(rows_stored, 16)
            sp.wait_ge(rows_stored, 16)
            for par in range(2):
                sp.wait_ge(wh_stored[par], 16 + 16 * (TILES // 2))

        @block.gpsimd
        def _(pool):
            nc.gpsimd.memset(sums[:, 3:4], -0.5).then_inc(exponent_in, 1)
            nc.gpsimd.memset(wh_sum[:], 0.0).then_inc(zeroed, 1)
            pool.sem_inc(added, 2)
            pool.wait_ge(zeroed, 1)
            pool.wait_ge(exponent_in, 1)

            def add(q, par):
                pool.wait_ge(wh_copied, 2 + q + 1)
                pool.wait_ge(added, 2 + q)
                nc.gpsimd.tensor_tensor(wh_sum[:], wh_sum[:], wh_tile[:, par], ALU.add).then_inc(added, 1)

            for q in range(3):
                row_rstd(nc, pool, sums, scale, q, sums_done, h_done, rstd_done)
            with pool.Fori(0, BLOCKS - 1) as m:
                for n in range(T):
                    row_rstd(nc, pool, sums, scale, m * T + n + 3, sums_done, h_done, rstd_done)
                    add(m * T + n, n % 2)
            row_rstd(nc, pool, sums, scale, TILES - 1, sums_done, h_done, rstd_done)
            for q in range(TILES - T, TILES):
                add(q, q % 2)
            pool.wait_ge(factor_step, 1)
            nc.gpsimd.partition_all_reduce(d_top[:, 1], d_top[:, 0], P, RMAX).then_inc(factor_step, 1)

        def all_blocks(engine, four_steps):
            with engine.Fori(0, BLOCKS // 2 - 1) as it:
                for half in range(2):
                    four_steps(it * 2 + half, half)
            for half in range(2):
                four_steps(BLOCKS - 2 + half, half)

        def ahead(m, n, steps):
            return not isinstance(m, int) or m * T + n + steps < TILES

        @block.tensor
        def _(pe):
            def turn(q, n):
                pe.wait_ge(h_done, 1 + q + 1)
                pe.wait_ge(low_done, q + 1)
                for t in range(T):
                    last = nc.tensor.transpose(psum[:, 6 + n % 2, t * P:(t + 1) * P], x_tile[:, n % XBUF, t * P:(t + 1) * P], ident[:])
                last.then_inc(turned, 1)

            def products(out, stationary, moving):
                for t in range(T):
                    for a, b in ((0, 0), (0, 1), (1, 0)):
                        last = nc.tensor.matmul(out, stationary(a, t), moving(b, t), start=(t == 0 and a + b == 0),
                                                stop=(t == T - 1 and a == 1))
                return last

            def four_steps(m, half):
                for n in range(T):
                    q = m * T + n
                    if ahead(m, n, 2):
                        turn(q + 2, n + 2)
                    pe.wait_ge(low_done, 2 + q + 1)
                    pe.wait_ge(sd_copied, q + 1)
                    pe.wait_ge(wh_copied, q + 1)
                    mine = lambda a, t: h_t[:, half, a, t, n * P:(n + 1) * P]
                    products(psum[:, n % 2, :], mine, lambda b, t: w_half[:, b, t, 0:512])
                    products(psum[:, 2 + n % 2, 0:2 * HEADS], mine, lambda b, t: w_half[:, b, t, 512:WIDE]).then_inc(feature_done, 1)
                pe.wait_ge(rows_copied, 1 + m)
                products(psum[0:HEADS, 4, :], lambda a, t: w_half[:, a, t, 512:512 + HEADS],
                         lambda b, t: h_t[:, half, b, t, :]).then_inc(rows_done, 1)

            pe.sem_inc(rows_done, 2)
            pe.wait_ge(weights_in, 32)
            for q in range(2):
                turn(q, q)
            all_blocks(pe, four_steps)
            pe.wait_ge(added, 2 + TILES)
            pe.wait_ge(rows_copied, 1 + BLOCKS)
            nc.tensor.matmul(psum[:, 4, :], mean_w[:], wh_sum[:], start=True, stop=True).then_inc(mean_done, 1)

        @block.scalar
        def _(act):
            def relu(q, n):
                row_relu_norm(nc, act, x_tile[:, n % XBUF], scale, q, norm_done, h_done)

            def high(m, n, half):
                act.wait_ge(rows_done, m + 1)
                act.wait_ge(turned, m * T + n + 1)
                nc.scalar.copy(h_t[:, half, 0, :, n * P:(n + 1) * P],
                               psum[:, 6 + n % 2, :].rearrange("p (t i) -> p t i", t=T)).then_inc(high_done, 1)

            def four_steps(m, half):
                for n in range(T):
                    q, par = m * T + n, n % 2
                    if ahead(m, n, 3):
                        relu(q + 3, n + 3)
                    if ahead(m, n, 2):
                        high(m + (n + 2) // T, (n + 2) % T, half if n < 2 else 1 - half)
                    act.wait_ge(feature_done, q + 1)
                    act.wait_ge(added, q + 1)
                    act.wait_ge(wh_stored[par], (m * 2 + n // 2) * 16 + 16)
                    nc.scalar.activation(wh_tile[:, par], psum[:, par, :], ACT.Copy, scale=1.0 / UP).then_inc(wh_copied, 1)

            act.sem_inc(h_done, 1)
            act.sem_inc(wh_copied, 2)
            relu(0, 0)
            for n in range(2):
                relu(n + 1, n + 1)
                high(0, n, 0)
            all_blocks(act, four_steps)
            act.wait_ge(exp_ready, 1)
            for k, (src, mult) in enumerate(((0, 1.0), (0, SLOPE), (1, 1.0), (2, 1.0))):
                dst = node["factor_j"] if k < 2 else node["factor_i"]
                nc.scalar.activation(dst[:, :, :, k % 2], z[:, src], ACT.Exp, scale=mult).then_inc(exp_done, 1)
            act.wait_ge(exp_done, 4)

        @block.vector
        def _(dve):
            def norm(m, n):
                dve.wait_ge(x_in[n], m * 16 + 16)
                row_norm(nc, dve, x_tile[:, n], stats, sums, scale, m * T + n, sems.dve, stats_done, sums_done, rstd_done, norm_done)

            def low(m, n, half):
                dve.wait_ge(high_done, m * T + n + 1)
                nc.vector.tensor_tensor(h_t[:, half, 1, :, n * P:(n + 1) * P],
                                        psum[:, 6 + n % 2, :].rearrange("p (t i) -> p t i", t=T),
                                        h_t[:, half, 0, :, n * P:(n + 1) * P], ALU.subtract).then_inc(low_done, 1)

            def four_steps(m, half):
                for n in range(T):
                    if ahead(m, n, 3):
                        norm(m + (n + 3) // T, (n + 3) % T)
                    if ahead(m, n, 2):
                        low(m + (n + 2) // T, (n + 2) % T, half if n < 2 else 1 - half)
                    dve.wait_ge(feature_done, m * T + n + 1)
                    nc.vector.tensor_scalar(sd[:, bass.ds(m * T + n, 1), :],
                                            psum[:, 2 + n % 2, 0:2 * HEADS].rearrange("p (o n) -> p o n", o=1),
                                            1.0 / UP, None, ALU.mult).then_inc(sd_copied, 1)
                dve.wait_ge(rows_done, 2 + m + 1)
                nc.vector.tensor_scalar(s_row[:, bass.ds(m * 512, 512)], psum[0:HEADS, 4, :], 1.0 / UP, None,
                                        ALU.mult).then_inc(rows_copied, 1)

            dve.sem_inc(low_done, 2)
            dve.sem_inc(sd_copied, 2)
            dve.sem_inc(rows_copied, 1)
            nc.vector.memset(mean_w[:], 1.0 / NODES).then_inc(ready, 1)
            norm(0, 0)
            for n in range(2):
                norm(0, n + 1)
                low(0, n, 0)
            all_blocks(dve, four_steps)
            s_all, d_all = sd[:, :, 0:HEADS], sd[:, :, HEADS:2 * HEADS]
            dve.wait_ge(sd_copied, 2 + TILES)
            nc.vector.tensor_reduce(d_top[:, 0], d_all.rearrange("p n h -> p h n"), AX, ALU.max).then_inc(factor_step, 1)
            nc.vector.tensor_scalar(node["gate_d"][:], d_all, GATE, None, ALU.mult).then_inc(ready, 1)
            dve.wait_ge(factor_step, 2)
            top = d_top[:, 1:2, :].broadcast_to([P, TILES, HEADS])
            nc.vector.tensor_tensor(z[:, 0], d_all, top, ALU.subtract).then_inc(factor_step, 1)
            nc.vector.tensor_tensor(z[:, 1], s_all, top, ALU.add).then_inc(factor_step, 1)
            dve.wait_ge(factor_step, 4)
            nc.vector.tensor_scalar(z[:, 2], z[:, 1], SLOPE, None, ALU.mult).then_inc(factor_step, 1)
            dve.wait_ge(factor_step, 5)
            nc.vector.tensor_tensor(z[:, 3], z[:, 1], z[:, 2], ALU.max).then_inc(factor_step, 1)
            dve.wait_ge(factor_step, 6)
            for k in (1, 2):
                nc.vector.tensor_tensor(z[:, k], z[:, k], z[:, 3], ALU.subtract).then_inc(factor_step, 1)
            dve.wait_ge(factor_step, 8)
            dve.sem_inc(exp_ready, 1)
            dve.wait_ge(mean_done, 1)
            nc.vector.tensor_copy(node["mean"][:], psum[:, 4, :]).then_inc(mean_copied, 1)
            dve.wait_ge(mean_copied, 1)


MLP_SHAPES = ((4, 256), (2, 128), (1, 256), (2, 512))


def views(words, *shapes):
    result, start = [], 0
    for shape in shapes:
        size = 1
        for n in shape:
            size *= n
        names = "abcdefg"[:len(shape)]
        result.append(words[:, start:start + size].rearrange(f"p ({' '.join(names)}) -> p {' '.join(names)}",
                                                             **dict(zip(names, shape))))
        start += size
    return result


def mlp_views(words):
    *weights, ident, enc = views(words, *MLP_SHAPES, (1, P), (4, 512))
    return weights, ident, enc


GROUP = 4
PARTS, COLS = 3, HD + 1
HALF = PARTS * COLS
WORDS = 2 * 2 * GROUP * HD + 2 * (2 * 2 * GROUP * 2 * COLS)


def graph_attention(nc, sems, d, psum, edge_dram, srow_dram, wh_dram, enc_dram, node, words, mlp_in):
    TILES, QW = NODES // P, 512
    BLOCKS, CHUNKS, SUBS, SPLITS = NODES // QW, TILES // 2, QW // P, TILES // 2
    GROUPS = HEADS // GROUP
    RING, PIECES = 4, 4
    with ExitStack() as ctx:
        def sb(name, shape, dt=F32):
            return ctx.enter_context(nc.sbuf_tensor(f"{name}_3", shape, dt))

        def sem(name):
            return sems.new((f"{name}_3"))

        x_parts = sb("x_parts", [P, TILES, GROUP, 2, PARTS, COLS], BF16)
        wh, f, rest = views(words, (2, 2, GROUP, HD), (2, 2, GROUP, 2, COLS), (2, 2, GROUP, 2, COLS))
        edges = sb("edges", [P, TILES, QW], BF16)
        s_row = sb("s_row", [P, 2, QW])
        gate = sb("gate", [P, RING, 2, QW], BF16)
        cells = sb("cells", [P, RING, 2, 2, QW], BF16)
        raw = sb("raw", [P, SUBS, 2, PARTS, COLS])
        num = sb("num", [P, SUBS, 2, COLS])
        y = sb("y", [P, SUBS, COLS])
        none, safe, minus_one = (sb(n, [P, SUBS]) for n in ("none", "safe", "minus_one"))
        spare = sb("spare", [P, SUBS, HD])
        enc = sb("enc", [P, SUBS, GROUP, HD])
        wh_in = [sem(f"wh_in{i}") for i in range(2)]
        f_done, first_done, rest_done, second_done, third_done = (sem(n) for n in ("f", "first", "rest_s", "second", "third"))
        edges_in = [sem(f"edges_in{i}") for i in range(PIECES)]
        s_in = [sem(f"s_in{i}") for i in range(2)]
        gate_done, above_done, cells_done, cells_used = (sem(n) for n in ("gate", "above", "cells", "cells_used"))
        copied, pool_step, enc_stored, constant_in = (sem(n) for n in ("copied", "pool_step", "enc_stored", "constant_in"))
        block = ctx.enter_context(nc.Block())
        edge_v = edge_dram.rearrange("(n p) i -> p n i", p=P)
        whv = wh_dram.rearrange("(n j p) k -> n p j k", p=P, j=2)
        enc_v = enc_dram.rearrange("(n s p) k -> n p s k", p=P, s=SUBS)
        STEPS = 11

        def columns(gr):
            return slice(gr * GROUP * HD, (gr + 1) * GROUP * HD)

        def head_number(gr, b, h):
            return (gr * BLOCKS + b) * GROUP + h

        def part(n, k):
            return x_parts[:, bass.ds(n * 2, 2), :, :, k, :].rearrange("p j h b c -> p (j h b) c")

        def flat(t, par):
            return t[:, par].rearrange("p j h b c -> p (j h b) c")

        def all_splits(engine, gr, leading, trailing):
            n0 = gr * SPLITS
            leading(n0, 0, 0)
            with engine.Fori(0, SPLITS // 2 - 1) as it:
                for par in range(2):
                    leading(n0 + it * 2 + par + 1, it * 2 + par + 1, 1 - par)
                    trailing(n0 + it * 2 + par, it * 2 + par, par)
            leading(n0 + SPLITS - 1, SPLITS - 1, 1)
            for t in (SPLITS - 2, SPLITS - 1):
                trailing(n0 + t, t, t % 2)

        @block.sync
        def _(sp):
            def load_wh(gr, t, par):
                sp.dma_start(wh[:, par].rearrange("p j h k -> p j (h k)"), whv[t][:, :, columns(gr)]).then_inc(wh_in[par], 16)

            def load_s(gr, b, h):
                src = srow_dram[gr * GROUP + h:gr * GROUP + h + 1, bass.ds(b * QW, QW)]
                sp.dma_start(s_row[:, h % 2], src.broadcast_to([P, QW])).then_inc(s_in[h % 2], 16)

            def load_edges(b, p):
                tiles = slice(p * TILES // PIECES, (p + 1) * TILES // PIECES)
                sp.dma_start(edges[:, tiles, :], edge_v[:, tiles, bass.ds(b * QW, QW)]).then_inc(edges_in[p], 16)

            def next_edges(gr, b, next_b):
                for p in range(PIECES):
                    wait_alone(sp, cells_done, head_number(gr, b, GROUP - 1) * CHUNKS + (p + 1) * RING, sems.sp)
                    load_edges(next_b, p)

            def head_gated(gr, b, h):
                wait_alone(sp, gate_done, (head_number(gr, b, h) + 1) * CHUNKS, sems.sp)

            for t in range(2):
                load_wh(0, t, t)
            for gr in range(GROUPS):
                with sp.Fori(0, SPLITS // 2 - 1) as it:
                    for par in range(2):
                        wait_alone(sp, f_done, (gr * SPLITS + it * 2 + par) * 4 + 4, sems.sp)
                        load_wh(gr, it * 2 + par + 2, par)
                if gr == 0:
                    for h in range(2):
                        load_s(0, 0, h)
                    for p in range(PIECES):
                        load_edges(0, p)
                with sp.Fori(0, BLOCKS - 1) as b:
                    for h in range(GROUP):
                        if h == GROUP - 1:
                            next_edges(gr, b, b + 1)
                        head_gated(gr, b, h)
                        load_s(gr, b + (h + 2) // GROUP, (h + 2) % GROUP)
                last = BLOCKS - 1
                for h in range(GROUP - 2):
                    head_gated(gr, last, h)
                    load_s(gr, last, h + 2)
                if gr + 1 < GROUPS:
                    for t in range(2):
                        load_wh(gr + 1, t, t)
                    head_gated(gr, last, GROUP - 2)
                    load_s(gr + 1, 0, 0)
                    next_edges(gr, last, 0)
                    head_gated(gr, last, GROUP - 1)
                    load_s(gr + 1, 0, 1)
                else:
                    sp.wait_ge(third_done, 2 + GROUPS * SPLITS)
                    weights, ident, enc0 = mlp_views(words)
                    for n, dst in enumerate(weights):
                        sp.dma_start(dst, d[f"W{n + 1}T"].rearrange("(t p) n -> p t n", p=P)).then_inc(mlp_in["weights"], 16)
                    sp.dma_start(ident[:, 0], d["ident"]).then_inc(mlp_in["weights"], 16)
                    sp.wait_ge(enc_stored, (gr * BLOCKS + 1) * SUBS * 16)
                    sp.dma_start(enc0, enc_v[0]).then_inc(mlp_in["enc"], 16)

        @block.gpsimd
        def _(pool):
            def product(gr, t, par, it):
                n = gr * SPLITS + t
                pool.wait_ge(wh_in[par], (gr * (SPLITS // 2) + it) * 16 + 16)
                pool.wait_ge(rest_done, n + 1)
                factor = node["factor_j"][:, bass.ds(t * 2, 2), gr * GROUP:(gr + 1) * GROUP, :]
                for b in range(2):
                    nc.gpsimd.tensor_tensor(f[:, par, :, :, b, 0:HD], wh[:, par],
                                            factor[:, :, :, b:b + 1].broadcast_to([P, 2, GROUP, HD]), ALU.mult).then_inc(f_done, 1)
                for j in range(2):
                    nc.gpsimd.tensor_copy(f[:, par, j, :, :, HD], factor[:, j]).then_inc(f_done, 1)

            def combine(gr, b, h):
                u = head_number(gr, b, h)
                base = u * STEPS

                def op(k, dst, a, c, f):
                    pool.wait_ge(pool_step, 1 + base + k)
                    nc.gpsimd.tensor_tensor(dst, a, c, f).then_inc(pool_step, 1)

                pool.wait_ge(copied, 2 + u + 1)
                raw_v = raw[:].rearrange("p s b k c -> p (s b) k c")
                num_v = num[:].rearrange("p s b c -> p (s b) c")
                op(0, num_v, raw_v[:, :, 0], raw_v[:, :, 1], ALU.add)
                op(1, num_v, num_v, raw_v[:, :, 2], ALU.add)
                f_i = node["factor_i"][:, bass.ds(b * SUBS, SUBS), gr * GROUP + h, :]
                op(2, num[:], num[:], f_i.rearrange("p s (b o) -> p s b o", o=1).broadcast_to([P, SUBS, 2, COLS]), ALU.mult)
                op(3, y[:], num[:, :, 0], num[:, :, 1], ALU.add)
                wait_alone(pool, pool_step, 1 + base + 4, sems.pool)
                nc.gpsimd.tensor_scalar(none[:], y[:, :, HD], 0.0, None, ALU.is_equal).then_inc(pool_step, 1)
                op(5, safe[:], y[:, :, HD], none[:], ALU.add)
                op(6, safe[:], safe[:], minus_one[:], ALU.pow)
                op(7, enc[:, :, h], y[:, :, 0:HD], safe[:].rearrange("p (s o) -> p s o", o=1).broadcast_to([P, SUBS, HD]), ALU.mult)
                mean = node["mean"][:, (gr * GROUP + h) * HD:(gr * GROUP + h + 1) * HD]
                op(8, spare[:], none[:].rearrange("p (s o) -> p s o", o=1).broadcast_to([P, SUBS, HD]),
                   mean.rearrange("p (o k) -> p o k", o=1).broadcast_to([P, SUBS, HD]), ALU.mult)
                op(9, enc[:, :, h], enc[:, :, h], spare[:], ALU.add)
                pool.wait_ge(pool_step, 1 + base + 10)
                pool.sem_inc(pool_step, 1)
                if h == GROUP - 1:
                    wait_alone(pool, pool_step, 1 + base + STEPS, sems.pool)
                    for s in range(SUBS):
                        src = enc[:, s].rearrange("p h k -> p (h k)")
                        dst = enc_v[bass.ds(b, 1), :, s, columns(gr)].rearrange("o p k -> (o p) k")
                        pool.dma_start(dst, src).then_inc(enc_stored, 16)
                    wait_alone(pool, enc_stored, (gr * BLOCKS + b + 1) * SUBS * 16, sems.pool)

            pool.sem_inc(rest_done, 2)
            pool.sem_inc(pool_step, 1)
            nc.gpsimd.memset(minus_one[:], -1.0).then_inc(constant_in, 1)
            for t in range(2):
                product(0, t, t, 0)
            pool.wait_ge(constant_in, 1)
            for gr in range(GROUPS):
                with pool.Fori(1, SPLITS // 2) as it:
                    for par in range(2):
                        product(gr, it * 2 + par, par, it)
                if gr:
                    combine(gr - 1, BLOCKS - 1, GROUP - 1)
                with pool.Fori(0, BLOCKS - 1) as b:
                    for h in range(GROUP):
                        combine(gr, b, h)
                for h in range(GROUP - 1):
                    combine(gr, BLOCKS - 1, h)
                if gr + 1 < GROUPS:
                    for t in range(2):
                        product(gr + 1, t, t, 0)
            combine(GROUPS - 1, BLOCKS - 1, GROUP - 1)

        @block.scalar
        def _(act):
            def first(n, t, par):
                wait_alone(act, f_done, n * 4 + 4, sems.act)
                nc.scalar.copy(part(t, 0), flat(f, par)).then_inc(first_done, 1)

            def second(n, t, par):
                wait_alone(act, rest_done, 2 + n + 1, sems.act)
                nc.scalar.copy(part(t, 1), flat(rest, par)).then_inc(second_done, 1)

            def gates(gr, b, h, p0, p1):
                with act.Fori(p0, p1) as p:
                    for c in range(RING):
                        n = head_number(gr, b, h) * CHUNKS + p * RING + c
                        wait_alone(act, above_done, n + 1, sems.act)
                        for a in range(2):
                            ins = nc.scalar.activation(gate[:, c, a], s_row[:, h % 2], ACT.Sigmoid, scale=GATE,
                                                       bias=node["gate_d"][:, bass.ds((p * RING + c) * 2 + a, 1), gr * GROUP + h])
                        ins.then_inc(gate_done, 1)

            def copy_head(u, par):
                act.wait_ge(cells_used, RING + (u + 1) * CHUNKS)
                act.wait_ge(pool_step, 1 + u * STEPS)
                nc.scalar.copy(raw[:].rearrange("p s b k c -> p s (b k c)"), psum[:, par * SUBS:(par + 1) * SUBS, 0:2 * HALF]).then_inc(copied, 1)

            def heads(gr, b, first_block):
                for h in range(GROUP):
                    act.wait_ge(s_in[h % 2], ((gr * BLOCKS + b) * (GROUP // 2) + h // 2) * 16 + 16)
                    gates(gr, b, h, 0, 2)
                    if not (first_block and h == 0):
                        copy_head(head_number(gr, b, h) - 1, (h - 1) % 2)
                    gates(gr, b, h, 2, PIECES)

            act.sem_inc(copied, 2)
            for gr in range(GROUPS):
                all_splits(act, gr, first, second)
                heads(gr, 0, True)
                with act.Fori(1, BLOCKS) as b:
                    heads(gr, b, False)
                copy_head(head_number(gr, BLOCKS - 1, GROUP - 1), 1)

        @block.vector
        def _(dve):
            def take_first(n, t, par):
                dve.wait_ge(first_done, n + 1)
                dve.wait_ge(third_done, n + 1)
                nc.vector.tensor_tensor(flat(rest, par), flat(f, par), part(t, 0), ALU.subtract).then_inc(rest_done, 1)

            def take_second(n, t, par):
                dve.wait_ge(second_done, n + 1)
                nc.vector.tensor_tensor(part(t, 2), flat(rest, par), part(t, 1), ALU.subtract).then_inc(third_done, 1)

            def above(n, c, pair):
                dve.wait_ge(gate_done, n + 1)
                dve.wait_ge(cells_used, n + 1)
                nc.vector.tensor_tensor(cells[:, c % RING, 0], gate[:, c % RING], pair, ALU.mult).then_inc(above_done, 1)

            def below(n, c, pair):
                dve.wait_ge(above_done, RING + n + 1)
                nc.vector.tensor_tensor(cells[:, c % RING, 1], pair, cells[:, c % RING, 0], ALU.subtract).then_inc(cells_done, 1)

            dve.sem_inc(third_done, 2)
            dve.sem_inc(above_done, RING)
            dve.sem_inc(cells_used, RING)
            for gr in range(GROUPS):
                all_splits(dve, gr, take_first, take_second)
                with dve.Fori(0, BLOCKS) as b:
                    with dve.Fori(0, GROUP) as h:
                        for c in range(CHUNKS + 1):
                            n = head_number(gr, b, h) * CHUNKS + c
                            if c < CHUNKS:
                                if c % RING == 0:
                                    wait_alone(dve, edges_in[c // RING], (gr * BLOCKS + b + 1) * 16, sems.dve)
                                above(n, c, edges[:, 2 * c:2 * c + 2, :])
                            if c:
                                below(n - 1, c - 1, edges[:, 2 * c - 2:2 * c, :])

        @block.tensor
        def _(pe):
            def piece(gr, b, hh, h, p):
                for c in range(RING):
                    n = head_number(gr, b, hh * 2 + h) * CHUNKS + p * RING + c
                    pe.wait_ge(cells_done, n + 1)
                    begins = isinstance(p, int) and p == 0 and c == 0
                    ends = isinstance(p, int) and p == PIECES - 1 and c == RING - 1
                    for a in range(2):
                        for s in range(SUBS):
                            for k in range(2):
                                moving = x_parts[:, bass.ds((p * RING + c) * 2 + a, 1), bass.ds(hh * 2 + h, 1), k]
                                last = nc.tensor.matmul(psum[:, h * SUBS + s, k * HALF:(k + 1) * HALF],
                                                        cells[:, c, k, a, s * P:(s + 1) * P],
                                                        moving.rearrange("p o q k c -> p (o q k c)"),
                                                        start=(begins and a == 0 and k == 0),
                                                        stop=(ends and a == 1 and k == 1), skip_group_check=True)
                    last.then_inc(cells_used, 1)

            for gr in range(GROUPS):
                pe.wait_ge(first_done, (gr + 1) * SPLITS)
                pe.wait_ge(second_done, (gr + 1) * SPLITS)
                pe.wait_ge(third_done, 2 + (gr + 1) * SPLITS)
                with pe.Fori(0, BLOCKS) as b:
                    with pe.Fori(0, GROUP // 2) as hh:
                        for h in range(2):
                            wait_alone(pe, copied, head_number(gr, b, hh * 2 + h) + 1, sems.pe)
                            piece(gr, b, hh, h, 0)
                            with pe.Fori(1, PIECES - 1) as p:
                                piece(gr, b, hh, h, p)
                            piece(gr, b, hh, h, PIECES - 1)


def mlp(nc, sems, d, psum, x1_dram, enc_dram, words, mlp_in):
    QW = 512
    BLOCKS, SUBS = NODES // QW, QW // P
    with ExitStack() as ctx:
        def sb(name, shape, dt=F32):
            return ctx.enter_context(nc.sbuf_tensor(name, shape, dt))

        def sem(name):
            return sems.new((name))

        weights, ident, enc0 = mlp_views(words)
        w1, w2, w3, w4 = halves = [sb(f"w{n + 1}_half", [P, 2, *shape], F16) for n, shape in enumerate(MLP_SHAPES)]
        biases, b4 = sb("biases", [P, 5]), sb("b4", [P, 512])
        enc1, neg = sb("enc4", [P, SUBS, 512]), sb("neg", [P, SUBS, 512])
        enc = (enc0, enc1[:])
        enc_t = [sb(f"enc_t{i}", [P, 2, 4, QW], F16) for i in range(2)]
        a1, a2, a3 = (sb(n, [P, 2, t, QW], F16) for n, t in (("a1t", 2), ("a2t", 1), ("a3t", 2)))
        full = sb("full", [P, 5, QW])
        x1 = sb("x1_4", [P, 2, SUBS, 512])
        weights_in, constants_in = mlp_in["weights"], sem("constants_in4")
        enc_in = [mlp_in["enc"], sem("enc_in4")]
        x_in, out_stored = ([sem(f"{n}{i}") for i in range(2)] for n in ("x_in4", "out_stored"))
        neg_done, exp_done, elu_done, turned, turn_high, turn_low = (sem(n) for n in ("neg_done", "exp_done4", "elu_done", "turned4", "turn_high", "turn_low"))
        layer_done, relu_done, relu_low, last_done, biased, out_done = (sem(n) for n in (
            "layer_done", "relu_done", "relu_low", "last_done", "biased", "out_done"))
        weight_high, weight_low = sem("weight_high4"), sem("weight_low4")
        relus = [(a1, 0, 2), (a1, 1, 3), (a2, 0, 4), (a3, 0, 4), (a3, 1, 5)]
        block = ctx.enter_context(nc.Block())
        enc_v = enc_dram.rearrange("(n s p) k -> n p s k", p=P, s=SUBS)
        x1_v = x1_dram.rearrange("(n s p) k -> n p s k", p=P, s=SUBS)
        out_v = d["out"].rearrange("(n s p) k -> n p s k", p=P, s=SUBS)

        def all_steps(engine, step):
            step(0, 0, 0)
            with engine.Fori(0, BLOCKS // 2 - 2) as it:
                for k in range(2):
                    step(it * 2 + 1 + k, 1 - k, it + k)
            for i in range(BLOCKS - 3, BLOCKS + 1):
                step(i, i % 2, i // 2)

        def exists(block):
            return not isinstance(block, int) or 0 <= block < BLOCKS

        @block.sync
        def _(sp):
            def load_enc(b, par):
                sp.dma_start(enc[par], enc_v[b]).then_inc(enc_in[par], 16)

            def load_x1(b, par):
                sp.dma_start(x1[:, par], x1_v[b]).then_inc(x_in[par], 16)

            def store(b, par, n_stored):
                wait_alone(sp, out_done, 2 + (b + 1) * SUBS, sems.sp)
                sp.dma_start(out_v[b], x1[:, par]).then_inc(out_stored[par], 16)
                sp.wait_ge(out_stored[par], n_stored * 16)

            sp.dma_start(biases[:], d["mlp_bias_cols"]).then_inc(constants_in, 16)
            load_enc(1, 1)
            sp.dma_start(b4[:], d["b4_rows"]).then_inc(constants_in, 16)
            for par in range(2):
                load_x1(par, par)
            for b in range(2):
                sp.wait_ge(turned, b * 4 + 4)
                load_enc(b + 2, b)
            with sp.Fori(1, BLOCKS // 2 - 1) as it:
                for par in range(2):
                    b = it * 2 + par
                    sp.wait_ge(turned, b * 4 + 4)
                    load_enc(b + 2, par)
                    store(b - 2, par, it)
                    load_x1(b, par)
            for b in range(BLOCKS - 2, BLOCKS + 2):
                store(b - 2, b % 2, b // 2)
                if b < BLOCKS:
                    load_x1(b, b % 2)

        @block.tensor
        def _(pe):
            def turn(b, par, tiles):
                pe.wait_ge(elu_done, b + 1)
                for t in tiles:
                    pe.wait_ge(turn_low, b * 4 + t + 1)
                    for s in range(SUBS):
                        last = nc.tensor.transpose(psum[:, t % 2, s * P:(s + 1) * P], enc[par][:, s, t * P:(t + 1) * P], ident[:, 0])
                    last.then_inc(turned, 1)

            def products(out, tiles, stationary, moving):
                for t in range(tiles):
                    for a, b in ((0, 0), (0, 1), (1, 0)):
                        last = nc.tensor.matmul(out, stationary(a, t), moving(b, t), start=(t == 0 and a + b == 0),
                                                stop=(t == tiles - 1 and a == 1))
                return last

            def layer(w, x, tiles, o, bank):
                products(psum[:, bank, :], tiles, lambda a, t: w[:, a, t, o * P:(o + 1) * P],
                         lambda b, t: x[:, b, t, :]).then_inc(layer_done, 1)

            def last_layer(b, subs):
                pe.wait_ge(relu_low, b * 5 + 5)
                for s in subs:
                    pe.wait_ge(out_done, b * SUBS + s + 1)
                    products(psum[:, 6 + s % 2, :], 2, lambda a, t: a3[:, a, t, s * P:(s + 1) * P],
                             lambda b, t: w4[:, b, t, :]).then_inc(last_done, 1)

            def step(i, par, half_i):
                for o in range(2):
                    if exists(i):
                        if o == 0:
                            pe.wait_ge(turn_low, 2 + i * 4 + 4)
                        layer(w1, enc_t[par], 4, o, 2 + o)
                    if exists(i + 1):
                        turn(i + 1, 1 - par, (2 * o, 2 * o + 1))
                if exists(i - 1):
                    last_layer(i - 1, (0, 1))
                if exists(i):
                    pe.wait_ge(relu_low, i * 5 + 2)
                    layer(w2, a1, 2, 0, 4)
                if exists(i - 1):
                    last_layer(i - 1, (2, 3))
                if exists(i):
                    pe.wait_ge(relu_low, i * 5 + 3)
                    for o in range(2):
                        layer(w3, a2, 1, o, 4 + o)

            pe.wait_ge(weights_in, 80)
            turn(0, 0, range(4))
            pe.wait_ge(weight_low, 4)
            all_steps(pe, step)

        @block.scalar
        def _(act):
            def exp_neg(b):
                act.wait_ge(neg_done, b * 2 + 1)
                nc.scalar.activation(neg[:], neg[:], ACT.Exp).then_inc(exp_done, 1)

            def high_turned(b, par, tiles):
                for t in tiles:
                    act.wait_ge(turned, b * 4 + t + 1)
                    nc.scalar.copy(enc_t[par][:, 0, t, :], psum[:, t % 2, :]).then_inc(turn_high, 1)

            def relu(i, k):
                dst, tile, bank = relus[k]
                act.wait_ge(layer_done, i * 5 + k + 1)
                nc.scalar.activation(dst[:, 0, tile], psum[:, bank, :], ACT.Relu, scale=1.0 / UP, bias=biases[:, k:k + 1])
                nc.scalar.activation(full[:, k], psum[:, bank, :], ACT.Relu, scale=1.0 / UP, bias=biases[:, k:k + 1]).then_inc(relu_done, 1)

            def step(i, par, half_i):
                for k in range(2):
                    if exists(i):
                        relu(i, k)
                    if exists(i + 1):
                        high_turned(i + 1, 1 - par, (2 * k, 2 * k + 1))
                if exists(i + 2):
                    exp_neg(i + 2)
                if exists(i):
                    for k in range(2, 5):
                        relu(i, k)

            act.wait_ge(weights_in, 80)
            for w, w_half in zip(weights, halves):
                nc.scalar.activation(w_half[:, 0], w, ACT.Copy, scale=UP).then_inc(weight_high, 1)
            exp_neg(0)
            act.wait_ge(constants_in, 32)
            high_turned(0, 0, range(4))
            exp_neg(1)
            all_steps(act, step)

        @block.vector
        def _(dve):
            def signs(b, par, n_in):
                if b is not FIRST:
                    dve.wait_ge(elu_done, b)
                dve.wait_ge(enc_in[par], n_in * 16)
                nc.vector.tensor_scalar(neg[:], enc[par], 0.0, None, ALU.min).then_inc(neg_done, 1)
                dve.wait_ge(neg_done, b * 2 + 1)
                nc.vector.tensor_scalar(enc[par], enc[par], 0.0, -1.0, ALU.max, ALU.add).then_inc(neg_done, 1)

            def elu(b, par):
                dve.wait_ge(neg_done, b * 2 + 2)
                dve.wait_ge(exp_done, b + 1)
                nc.vector.tensor_tensor(enc[par], enc[par], neg[:], ALU.add).then_inc(elu_done, 1)

            def low_turned(b, par, tiles):
                for t in tiles:
                    dve.wait_ge(turn_high, b * 4 + t + 1)
                    nc.vector.tensor_tensor(enc_t[par][:, 1, t, :], psum[:, t % 2, :], enc_t[par][:, 0, t, :],
                                            ALU.subtract).then_inc(turn_low, 1)

            def low(i, k):
                dst, tile, bank = relus[k]
                dve.wait_ge(relu_done, i * 5 + k + 1)
                nc.vector.tensor_tensor(dst[:, 1, tile], full[:, k], dst[:, 0, tile], ALU.subtract).then_inc(relu_low, 1)

            def output(b, par, subs):
                for s in subs:
                    dve.wait_ge(last_done, b * SUBS + s + 1)
                    dve.wait_ge(biased, b + 1)
                    nc.vector.scalar_tensor_tensor(out=x1[:, par, s], in0=psum[:, 6 + s % 2, :], scalar=1.0 / UP,
                                                   in1=x1[:, par, s], op0=ALU.mult, op1=ALU.add).then_inc(out_done, 1)

            def step(i, par, half_i):
                for k in range(2):
                    if exists(i):
                        low(i, k)
                    if exists(i + 1):
                        low_turned(i + 1, 1 - par, (2 * k, 2 * k + 1))
                    if k == 0 and exists(i + 2):
                        signs(i + 2, par, half_i + 2)
                if exists(i - 1):
                    output(i - 1, 1 - par, (0, 1))
                if exists(i + 2):
                    elu(i + 2, par)
                if exists(i):
                    low(i, 2)
                if exists(i - 1):
                    output(i - 1, 1 - par, (2, 3))
                if exists(i):
                    for k in (3, 4):
                        low(i, k)

            FIRST = 0
            dve.sem_inc(out_done, 2)
            dve.sem_inc(turn_low, 2)
            for n, (w, w_half) in enumerate(zip(weights, halves)):
                dve.wait_ge(weight_high, n + 1)
                nc.vector.scalar_tensor_tensor(out=w_half[:, 1], in0=w, scalar=UP, in1=w_half[:, 0],
                                               op0=ALU.mult, op1=ALU.subtract).then_inc(weight_low, 1)
            signs(0, 0, 1)
            elu(0, 0)
            low_turned(0, 0, range(4))
            signs(1, 1, 1)
            elu(1, 1)
            all_steps(dve, step)

        @block.gpsimd
        def _(pool):
            pool.wait_ge(constants_in, 32)
            with pool.Fori(0, BLOCKS // 2) as it:
                for par in range(2):
                    pool.wait_ge(x_in[par], it * 16 + 16)
                    nc.gpsimd.tensor_tensor(x1[:, par], x1[:, par],
                                            b4[:].rearrange("p (o k) -> p o k", o=1).broadcast_to([P, SUBS, 512]), ALU.add).then_inc(biased, 1)


def build(nc, d, upto=9):
    ht_dram = nc.dram_tensor("ht_dram", (NODES // QB, P, 2 * 4 * QB), F16, kind="Internal").ap()
    x1_dram = nc.dram_tensor("x1_dram", (NODES, 512), F32, kind="Internal").ap()
    wh_dram = nc.dram_tensor("wh_dram", (NODES, 512), F32, kind="Internal").ap()
    enc_dram = nc.dram_tensor("enc_dram", (NODES, 512), F32, kind="Internal").ap()
    srow_dram = nc.dram_tensor("srow_dram", (HEADS, NODES), F32, kind="Internal").ap()
    w_half_dram = nc.dram_tensor("w_half_dram", (P, 2 * 4 * (512 + 2 * HEADS)), F16, kind="Internal").ap()
    edge_dram = nc.dram_tensor("edge_dram", (NODES, NODES), BF16, kind="Internal").ap()
    with nc.psum_tensor("psum", [P, 8, 512], F32) as psum, ExitStack() as stack:
        sems = Semaphores(nc, stack)
        with nc.sbuf_tensor("g", [P, 2, 4, NODES], F16) as g, nc.sbuf_tensor("v", [P, 2, 32, 512], F16) as v, \
                nc.sbuf_tensor("c_all", [P, 32], F32) as c_all:
            with nc.sbuf_tensor("wqk", [P, 2, 4, 512], F16) as wqk, nc.sbuf_tensor("wvm", [P, 2, 4, 512], F16) as wvm, \
                    nc.sbuf_tensor("bias_cols", [P, 9], F32) as bias_cols, nc.sbuf_tensor("bvm", [P, 512], F32) as bvm, \
                    nc.sbuf_tensor("wc_half", [P, 2, 4], F16) as wc_half:
                keep = {"wqk": wqk, "wvm": wvm, "bias_cols": bias_cols, "bvm": bvm, "wc_half": wc_half}
                weight_products(nc, sems, d, keep, psum, w_half_dram)
                keys_and_values(nc, sems, d, keep, psum, g, v, c_all, ht_dram)
            if upto >= 1:
                attention(nc, sems, d, psum, g, v, c_all, ht_dram, x1_dram, edge_dram)
        words = stack.enter_context(nc.sbuf_tensor("words", [P, WORDS], F32))
        mlp_in = {n: sems.new(f"mlp_{n}_in") for n in ("weights", "enc")}
        if upto >= 2:
            with ExitStack() as ctx:
                node = {n: ctx.enter_context(nc.sbuf_tensor(n, shape, F32)) for n, shape in (
                    ("factor_j", [P, 32, HEADS, 2]), ("factor_i", [P, 32, HEADS, 2]), ("gate_d", [P, 32, HEADS]), ("mean", [P, 512]))}
                head_features(nc, sems, d, psum, x1_dram, w_half_dram, wh_dram, srow_dram, node)
                if upto >= 3:
                    graph_attention(nc, sems, d, psum, edge_dram, srow_dram, wh_dram, enc_dram, node, words, mlp_in)
        if upto >= 4:
            mlp(nc, sems, d, psum, x1_dram, enc_dram, words, mlp_in)


PLAIN = ("x", "L0_gnn_Wk", "L0_gnn_Wq", "L0_gnn_Wv")


def host_layout(inputs):
    import numpy as np

    def transposed(name):
        return np.ascontiguousarray(np.asarray(inputs[name]).T)

    def rows(a):
        a = np.asarray(a).reshape(-1)
        return np.ascontiguousarray(np.broadcast_to(a, (P, a.size)))

    def cols(name):
        return np.ascontiguousarray(np.asarray(inputs[name]).reshape(-1, P).T)

    arrays = {n: np.ascontiguousarray(inputs[n]) for n in PLAIN}
    arrays["adjT"] = transposed("adj")
    arrays["keyT"] = transposed("L0_gnn_key")
    arrays["valueT"] = transposed("L0_gnn_value")
    arrays["WmT"] = transposed("L0_gnn_Wm")
    arrays["bm_rows"] = rows(inputs["L0_gnn_bm"])
    for b in ("bq", "bk", "bv"):
        arrays[f"{b}_cols"] = cols(f"L0_gnn_{b}")
    w = np.asarray(inputs["L1_gnn_W"])
    arrays["W_heads"] = np.ascontiguousarray(w.transpose(1, 0, 2).reshape(w.shape[1], -1))
    arrays["a1_rows"] = rows(inputs["L1_gnn_a1"])
    arrays["a2_rows"] = rows(inputs["L1_gnn_a2"])
    for n in range(1, 5):
        arrays[f"W{n}T"] = transposed(f"L1_gnn_W{n}")
    arrays["mlp_bias_cols"] = np.ascontiguousarray(np.concatenate([cols(f"L1_gnn_b{n}") for n in (1, 2, 3)], axis=1))
    arrays["b4_rows"] = rows(inputs["L1_gnn_b4"])
    arrays["ident"] = np.eye(P, dtype=np.float32)
    return arrays


def kernel(**inputs):
    import concourse.bacc as bacc
    from concourse import mybir as ir
    from concourse.bass_utils import run_bass_kernel_spmd

    nc = bacc.Bacc("TRN2", target_bir_lowering=False, num_devices=1)
    arrays = host_layout(inputs)
    d = {n: nc.dram_tensor(n, a.shape, ir.dt.from_np(a.dtype), kind="ExternalInput").ap() for n, a in arrays.items()}
    d["out"] = nc.dram_tensor("out", (NODES, 512), F32, kind="ExternalOutput").ap()
    build(nc, d)
    return run_bass_kernel_spmd(nc, [arrays], core_ids=[0]).results[0]["out"]
```
